# Optimizing a Trainium2 kernel written in Bass

```python
import numpy as np
import jax
import jax.numpy as jnp

def _softmax(x, axis=-1):
    return jax.nn.softmax(x, axis=axis)

def _gelu(x):
    return jax.nn.gelu(x, approximate=True)

def _silu(x):
    return jax.nn.silu(x)

def _sigmoid(x):
    return jax.nn.sigmoid(x)

def _layernorm(x, axis=-1, eps=1e-05):
    m = jnp.mean(x, axis=axis, keepdims=True)
    v = jnp.var(x, axis=axis, keepdims=True)
    return (x - m) / jnp.sqrt(v + eps)

def _scatter_add(tgt, idx, src, axis=0):
    return tgt.at[idx].add(src)

def _segment_sum(src, seg, n):
    return jax.ops.segment_sum(src, seg, n)
kernel_name = 'mk_vit_tower_cls_d1_tok_img1024_r4_9b7a0b'

def setup_inputs(seed: int=0):
    np.random.seed(seed)
    _w = jnp.asarray

    def _rec_inputs():
        import jax
        import jax.numpy as jnp
        _rk = jax.random.key(seed)
        x = -0.00016672 + 0.999947 * jax.random.normal(jax.random.fold_in(_rk, 1), (32, 3, 96, 96), jnp.float32)
        cls_tok = 0.02 * jax.random.normal(jax.random.fold_in(_rk, 5), (1, 1, 256), jnp.float32)
        return (x, cls_tok)
    x, cls_tok = _rec_inputs()

    def _L0_tok_setup():
        import jax, jax.numpy as jnp
        import numpy as np
        PATCH = 16
        EPS = 1e-05

        def _patchify(x, p):
            B, C, H, W = x.shape
            hp, wp = (H // p, W // p)
            x = x.reshape(B, C, hp, p, wp, p)
            x = x.transpose(0, 2, 4, 1, 3, 5)
            return x.reshape(B, hp * wp, C * p * p)
        key = jax.random.key(seed)
        ks = jax.random.split(key, 6)
        B, C, H = (64, 3, 96)
        E = 256
        P = PATCH
        N = (H // P) ** 2
        D = C * P * P
        x = jax.random.normal(ks[0], (B, C, H, H), dtype=jnp.float32)
        W = jax.random.normal(ks[1], (D, E), dtype=jnp.float32) * (1.0 / np.sqrt(D))
        b = jnp.zeros((E,), dtype=jnp.float32)
        cls_token = jax.random.normal(ks[2], (1, 1, E), dtype=jnp.float32) * 0.02
        pos_embedding = jax.random.normal(ks[3], (1, N + 1, E), dtype=jnp.float32) * 0.02
        gamma = jnp.ones((E,), dtype=jnp.float32)
        beta = jnp.zeros((E,), dtype=jnp.float32)
        return {'x': x, 'W': W, 'b': b, 'cls_token': cls_token, 'pos_embedding': pos_embedding, 'gamma': gamma, 'beta': beta}
    _L0_tok_all = _L0_tok_setup()
    _L0_tok_in = {k: v for k, v in _L0_tok_all.items() if k in ('W', 'b', 'cls_token', 'pos_embedding', 'gamma', 'beta')}
    del _L0_tok_all

    def _L0_attn_setup():
        import jax, jax.numpy as jnp
        import numpy as np
        B, T, D = (8, 512, 256)
        H, N = (8, 32)

        def _xavier(key, shape, fan_in, fan_out):
            lim = float(np.sqrt(6.0 / (fan_in + fan_out)))
            return jax.random.uniform(key, shape, jnp.float32, -lim, lim)

        def _reference_tuple_inner(x, W_in, W_k, W_v, W_q, W_beta, b_beta, W_out):
            b, t, d = x.shape
            h, n = b_beta.shape
            xp = jax.nn.silu(jnp.einsum('btd,ed->bte', x, W_in))

            def proj(W):
                return jnp.einsum('btd,md->btm', xp, W).reshape(b, t, h, n).transpose(1, 0, 2, 3)
            k_all = proj(W_k)
            v_all = proj(W_v)
            q_all = proj(W_q)
            beta_all = jax.nn.sigmoid(proj(W_beta) + b_beta)
            S0 = jnp.zeros((b, h, n, n), x.dtype)

            def step(S, inp):
                k, v, q, beta = inp
                kn = k / (jnp.linalg.norm(k, axis=-1, keepdims=True) + 1e-06)
                retrieved = jnp.einsum('bhij,bhj->bhi', S, kn)
                delta = v - retrieved
                S = jnp.tanh(beta[..., None] * S + delta[..., None] * kn[..., None, :])
                Sq = jnp.einsum('bhij,bhj->bhi', S, q)
                out = Sq * jax.nn.silu(Sq)
                return (S, out)
            S_final, outs = jax.lax.scan(step, S0, (k_all, v_all, q_all, beta_all))
            cell_out = outs.transpose(1, 0, 2, 3).reshape(b, t, h * n)
            y = jnp.einsum('btm,dm->btd', cell_out, W_out)
            return (y, S_final)
        key = jax.random.key(seed)
        ks = jax.random.split(key, 8)
        x = jax.random.normal(ks[0], (B, T, D), jnp.float32)
        W_in = _xavier(ks[1], (D, D), D, D)
        W_k = _xavier(ks[2], (H * N, D), N, D)
        W_v = _xavier(ks[3], (H * N, D), N, D)
        W_q = _xavier(ks[4], (H * N, D), N, D)
        W_beta = _xavier(ks[5], (H * N, D), N, D)
        b_beta = jnp.full((H, N), 2.0, jnp.float32)
        W_out = _xavier(ks[6], (D, H * N), H * N, D)
        return {'x': x, 'W_in': W_in, 'W_k': W_k, 'W_v': W_v, 'W_q': W_q, 'W_beta': W_beta, 'b_beta': b_beta, 'W_out': W_out}
    _L0_attn_all = _L0_attn_setup()
    _L0_attn_in = {k: v for k, v in _L0_attn_all.items() if k in ('W_in', 'W_k', 'W_v', 'W_q', 'W_beta', 'b_beta', 'W_out')}
    del _L0_attn_all

    def _L0_ffn_setup():
        import jax, jax.numpy as jnp
        import numpy as np
        EMBED = 256
        HEADS = 16
        HEAD_DIM = EMBED // HEADS
        NUM_EXPERTS = 8
        TOP_K = 2
        HIDDEN = (int(2 * (4 * EMBED) / 3) + 63) // 64 * 64
        SEQ = 512
        BATCH = 2
        ROPE_BASE = 10000.0
        EPS = 1e-06

        def _rope_tables(seq_len, dim):
            inv_freq = 1.0 / ROPE_BASE ** (np.arange(0, dim, 2, dtype=np.float32) / dim)
            t = np.arange(seq_len, dtype=np.float32)
            freqs = np.einsum('i,j->ij', t, inv_freq)
            emb = np.concatenate([freqs, freqs], axis=-1)
            return (jnp.asarray(np.cos(emb)), jnp.asarray(np.sin(emb)))

        def _rotate_half(x):
            x1, x2 = jnp.split(x, 2, axis=-1)
            return jnp.concatenate([-x2, x1], axis=-1)

        def _rmsnorm(x, w):
            return x * jax.lax.rsqrt(jnp.mean(x * x, axis=-1, keepdims=True) + EPS) * w

        def _attention(x, wq, wk, wv, wo):
            B, S, _ = x.shape
            q = (x @ wq).reshape(B, S, HEADS, HEAD_DIM).transpose(0, 2, 1, 3)
            k = (x @ wk).reshape(B, S, HEADS, HEAD_DIM).transpose(0, 2, 1, 3)
            v = (x @ wv).reshape(B, S, HEADS, HEAD_DIM).transpose(0, 2, 1, 3)
            cos, sin = _rope_tables(S, HEAD_DIM)
            cos = cos[None, None]
            sin = sin[None, None]
            q = q * cos + _rotate_half(q) * sin
            k = k * cos + _rotate_half(k) * sin
            scale = HEAD_DIM ** (-0.5)
            scores = jnp.einsum('bhqd,bhkd->bhqk', q, k) * scale
            causal = jnp.triu(jnp.ones((S, S), bool), k=1)
            scores = jnp.where(causal, -jnp.inf, scores)
            attn = jax.nn.softmax(scores, axis=-1)
            out = jnp.einsum('bhqk,bhkd->bhqd', attn, v)
            out = out.transpose(0, 2, 1, 3).reshape(B, S, EMBED)
            return out @ wo

        def _moe(x, w_router, wg, wu, wd):
            B, S, E = x.shape
            xf = x.reshape(-1, E)
            logits = xf @ w_router
            probs = jax.nn.softmax(logits, axis=-1)
            topw, topi = jax.lax.top_k(probs, TOP_K)
            topw = topw / jnp.sum(topw, axis=-1, keepdims=True)
            combine = jnp.sum(jax.nn.one_hot(topi, NUM_EXPERTS, dtype=xf.dtype) * topw[..., None], axis=1)
            g = jax.nn.silu(jnp.einsum('td,xdh->txh', xf, wg))
            u = jnp.einsum('td,xdh->txh', xf, wu)
            eo = jnp.einsum('txh,xhd->txd', g * u, wd)
            out = jnp.einsum('txd,tx->td', eo, combine)
            return out.reshape(B, S, E)
        key = jax.random.key(seed)
        ks = jax.random.split(key, 12)
        s = 0.02
        return {'x': jax.random.normal(ks[0], (BATCH, SEQ, EMBED), jnp.float32), 'wq': jax.random.normal(ks[1], (EMBED, EMBED), jnp.float32) * s, 'wk': jax.random.normal(ks[2], (EMBED, EMBED), jnp.float32) * s, 'wv': jax.random.normal(ks[3], (EMBED, EMBED), jnp.float32) * s, 'wo': jax.random.normal(ks[4], (EMBED, EMBED), jnp.float32) * s, 'w_router': jax.random.normal(ks[5], (EMBED, NUM_EXPERTS), jnp.float32) * s, 'wg': jax.random.normal(ks[6], (NUM_EXPERTS, EMBED, HIDDEN), jnp.float32) * s, 'wu': jax.random.normal(ks[7], (NUM_EXPERTS, EMBED, HIDDEN), jnp.float32) * s, 'wd': jax.random.normal(ks[8], (NUM_EXPERTS, HIDDEN, EMBED), jnp.float32) * s, 'g1': jnp.ones((EMBED,), jnp.float32), 'g2': jnp.ones((EMBED,), jnp.float32)}
    _L0_ffn_all = _L0_ffn_setup()
    _L0_ffn_in = {k: v for k, v in _L0_ffn_all.items() if k in ('wq', 'wk', 'wv', 'wo', 'w_router', 'wg', 'wu', 'wd', 'g1', 'g2')}
    del _L0_ffn_all
    return {'x': x, 'cls_tok': cls_tok, 'L0_tok_W': _L0_tok_in['W'], 'L0_tok_b': _L0_tok_in['b'], 'L0_tok_cls_token': _L0_tok_in['cls_token'], 'L0_tok_pos_embedding': _L0_tok_in['pos_embedding'], 'L0_tok_gamma': _L0_tok_in['gamma'], 'L0_tok_beta': _L0_tok_in['beta'], 'L0_attn_W_in': _L0_attn_in['W_in'], 'L0_attn_W_k': _L0_attn_in['W_k'], 'L0_attn_W_v': _L0_attn_in['W_v'], 'L0_attn_W_q': _L0_attn_in['W_q'], 'L0_attn_W_beta': _L0_attn_in['W_beta'], 'L0_attn_b_beta': _L0_attn_in['b_beta'], 'L0_attn_W_out': _L0_attn_in['W_out'], 'L0_ffn_wq': _L0_ffn_in['wq'], 'L0_ffn_wk': _L0_ffn_in['wk'], 'L0_ffn_wv': _L0_ffn_in['wv'], 'L0_ffn_wo': _L0_ffn_in['wo'], 'L0_ffn_w_router': _L0_ffn_in['w_router'], 'L0_ffn_wg': _L0_ffn_in['wg'], 'L0_ffn_wu': _L0_ffn_in['wu'], 'L0_ffn_wd': _L0_ffn_in['wd'], 'L0_ffn_g1': _L0_ffn_in['g1'], 'L0_ffn_g2': _L0_ffn_in['g2']}

def reference(x, cls_tok, L0_tok_W, L0_tok_b, L0_tok_cls_token, L0_tok_pos_embedding, L0_tok_gamma, L0_tok_beta, L0_attn_W_in, L0_attn_W_k, L0_attn_W_v, L0_attn_W_q, L0_attn_W_beta, L0_attn_b_beta, L0_attn_W_out, L0_ffn_wq, L0_ffn_wk, L0_ffn_wv, L0_ffn_wo, L0_ffn_w_router, L0_ffn_wg, L0_ffn_wu, L0_ffn_wd, L0_ffn_g1, L0_ffn_g2):
    import jax
    import jax.numpy as jnp

    def _L0_tok_ref(x, W, b, cls_token, pos_embedding, gamma, beta):
        import jax, jax.numpy as jnp
        import numpy as np
        PATCH = 16
        EPS = 1e-05

        def _patchify(x, p):
            B, C, H, W = x.shape
            hp, wp = (H // p, W // p)
            x = x.reshape(B, C, hp, p, wp, p)
            x = x.transpose(0, 2, 4, 1, 3, 5)
            return x.reshape(B, hp * wp, C * p * p)
        B = x.shape[0]
        patches = _patchify(x, PATCH)
        tok = jnp.einsum('bnd,de->bne', patches, W) + b
        cls = jnp.broadcast_to(cls_token, (B, 1, tok.shape[-1]))
        h = jnp.concatenate([cls, tok], axis=1) + pos_embedding
        mu = jnp.mean(h, axis=-1, keepdims=True)
        var = jnp.mean(jnp.square(h - mu), axis=-1, keepdims=True)
        out = (h - mu) * jax.lax.rsqrt(var + EPS) * gamma + beta
        return out

    def _L0_attn_ref(x, W_in, W_k, W_v, W_q, W_beta, b_beta, W_out):
        import jax, jax.numpy as jnp
        import numpy as np
        B, T, D = (8, 512, 256)
        H, N = (8, 32)

        def _xavier(key, shape, fan_in, fan_out):
            lim = float(np.sqrt(6.0 / (fan_in + fan_out)))
            return jax.random.uniform(key, shape, jnp.float32, -lim, lim)

        def _reference_tuple_inner(x, W_in, W_k, W_v, W_q, W_beta, b_beta, W_out):
            b, t, d = x.shape
            h, n = b_beta.shape
            xp = jax.nn.silu(jnp.einsum('btd,ed->bte', x, W_in))

            def proj(W):
                return jnp.einsum('btd,md->btm', xp, W).reshape(b, t, h, n).transpose(1, 0, 2, 3)
            k_all = proj(W_k)
            v_all = proj(W_v)
            q_all = proj(W_q)
            beta_all = jax.nn.sigmoid(proj(W_beta) + b_beta)
            S0 = jnp.zeros((b, h, n, n), x.dtype)

            def step(S, inp):
                k, v, q, beta = inp
                kn = k / (jnp.linalg.norm(k, axis=-1, keepdims=True) + 1e-06)
                retrieved = jnp.einsum('bhij,bhj->bhi', S, kn)
                delta = v - retrieved
                S = jnp.tanh(beta[..., None] * S + delta[..., None] * kn[..., None, :])
                Sq = jnp.einsum('bhij,bhj->bhi', S, q)
                out = Sq * jax.nn.silu(Sq)
                return (S, out)
            S_final, outs = jax.lax.scan(step, S0, (k_all, v_all, q_all, beta_all))
            cell_out = outs.transpose(1, 0, 2, 3).reshape(b, t, h * n)
            y = jnp.einsum('btm,dm->btd', cell_out, W_out)
            return (y, S_final)
        return _reference_tuple_inner(x, W_in, W_k, W_v, W_q, W_beta, b_beta, W_out)[0]

    def _L0_ffn_ref(x, wq, wk, wv, wo, w_router, wg, wu, wd, g1, g2):
        import jax, jax.numpy as jnp
        import numpy as np
        EMBED = 256
        HEADS = 16
        HEAD_DIM = EMBED // HEADS
        NUM_EXPERTS = 8
        TOP_K = 2
        HIDDEN = (int(2 * (4 * EMBED) / 3) + 63) // 64 * 64
        SEQ = 512
        BATCH = 2
        ROPE_BASE = 10000.0
        EPS = 1e-06

        def _rope_tables(seq_len, dim):
            inv_freq = 1.0 / ROPE_BASE ** (np.arange(0, dim, 2, dtype=np.float32) / dim)
            t = np.arange(seq_len, dtype=np.float32)
            freqs = np.einsum('i,j->ij', t, inv_freq)
            emb = np.concatenate([freqs, freqs], axis=-1)
            return (jnp.asarray(np.cos(emb)), jnp.asarray(np.sin(emb)))

        def _rotate_half(x):
            x1, x2 = jnp.split(x, 2, axis=-1)
            return jnp.concatenate([-x2, x1], axis=-1)

        def _rmsnorm(x, w):
            return x * jax.lax.rsqrt(jnp.mean(x * x, axis=-1, keepdims=True) + EPS) * w

        def _attention(x, wq, wk, wv, wo):
            B, S, _ = x.shape
            q = (x @ wq).reshape(B, S, HEADS, HEAD_DIM).transpose(0, 2, 1, 3)
            k = (x @ wk).reshape(B, S, HEADS, HEAD_DIM).transpose(0, 2, 1, 3)
            v = (x @ wv).reshape(B, S, HEADS, HEAD_DIM).transpose(0, 2, 1, 3)
            cos, sin = _rope_tables(S, HEAD_DIM)
            cos = cos[None, None]
            sin = sin[None, None]
            q = q * cos + _rotate_half(q) * sin
            k = k * cos + _rotate_half(k) * sin
            scale = HEAD_DIM ** (-0.5)
            scores = jnp.einsum('bhqd,bhkd->bhqk', q, k) * scale
            causal = jnp.triu(jnp.ones((S, S), bool), k=1)
            scores = jnp.where(causal, -jnp.inf, scores)
            attn = jax.nn.softmax(scores, axis=-1)
            out = jnp.einsum('bhqk,bhkd->bhqd', attn, v)
            out = out.transpose(0, 2, 1, 3).reshape(B, S, EMBED)
            return out @ wo

        def _moe(x, w_router, wg, wu, wd):
            B, S, E = x.shape
            xf = x.reshape(-1, E)
            logits = xf @ w_router
            probs = jax.nn.softmax(logits, axis=-1)
            topw, topi = jax.lax.top_k(probs, TOP_K)
            topw = topw / jnp.sum(topw, axis=-1, keepdims=True)
            combine = jnp.sum(jax.nn.one_hot(topi, NUM_EXPERTS, dtype=xf.dtype) * topw[..., None], axis=1)
            g = jax.nn.silu(jnp.einsum('td,xdh->txh', xf, wg))
            u = jnp.einsum('td,xdh->txh', xf, wu)
            eo = jnp.einsum('txh,xhd->txd', g * u, wd)
            out = jnp.einsum('txd,tx->td', eo, combine)
            return out.reshape(B, S, E)
        h = x + _attention(_rmsnorm(x, g1), wq, wk, wv, wo)
        y = h + _moe(_rmsnorm(h, g2), w_router, wg, wu, wd)
        return y
    h = _L0_tok_ref(x, L0_tok_W, L0_tok_b, L0_tok_cls_token, L0_tok_pos_embedding, L0_tok_gamma, L0_tok_beta)
    h = jnp.concatenate([jnp.broadcast_to(cls_tok, (h.shape[0], 1, h.shape[2])), h], axis=1)
    h = h + _L0_attn_ref(_layernorm(h, axis=-1), L0_attn_W_in, L0_attn_W_k, L0_attn_W_v, L0_attn_W_q, L0_attn_W_beta, L0_attn_b_beta, L0_attn_W_out)
    h = h + _L0_ffn_ref(_layernorm(h, axis=-1), L0_ffn_wq, L0_ffn_wk, L0_ffn_wv, L0_ffn_wo, L0_ffn_w_router, L0_ffn_wg, L0_ffn_wu, L0_ffn_wd, L0_ffn_g1, L0_ffn_g2)
    return h

_drawn_inputs = setup_inputs


def setup_inputs(seed=0):
    import zlib

    import numpy as np

    out = dict(_drawn_inputs(seed))
    spreads = {'L0_tok_b': (0.0, 0.1),
     'L0_tok_gamma': (1.0, 0.2),
     'L0_tok_beta': (0.0, 0.1),
     'L0_attn_b_beta': (2.0, 0.2),
     'L0_ffn_g1': (1.0, 0.6),
     'L0_ffn_g2': (1.0, 0.6)}
    factors = {'L0_ffn_wq': 8.0,
     'L0_ffn_wk': 8.0,
     'L0_ffn_wv': 3.678,
     'L0_ffn_wo': 3.856,
     'L0_ffn_w_router': 8.0,
     'L0_ffn_wg': 8.0,
     'L0_ffn_wu': 8.0,
     'L0_ffn_wd': 8.0}
    for name, (base, spread) in spreads.items():
        noise = np.random.default_rng([zlib.crc32(name.encode()), seed]).standard_normal(out[name].shape)
        drawn = base * np.exp(spread * noise) if base else spread * noise
        out[name] = jnp.asarray(drawn.astype(out[name].dtype))
    for name, factor in factors.items():
        out[name] = (out[name] * factor).astype(out[name].dtype)
    return out
```

```python
from contextlib import ExitStack

import concourse.bass as bass
from concourse import mybir
from concourse.alu_op_type import AluOpType as ALU

ACT = mybir.ActivationFunctionType
AX = mybir.AxisListType
F32 = mybir.dt.float32
BF16 = mybir.dt.bfloat16
ds = bass.ds

P = 128
IMAGES = 32
PATCHES = 36
T = PATCHES + 2
E = 256
EC = E // P
DPATCH = 768
DC = DPATCH // P
PAIRS = IMAGES // 2
SLOT = 64
TOKENS = IMAGES * T
NH_CELL, NCELL = 8, 32
B4 = P // NCELL
B8 = IMAGES // B4
CHUNK = B8 * T
HEADS, DH = 16, 16
HG = HEADS // EC
EXPERTS = 8
HID = 704
PARTS = 3
EPS_LN = 1e-5
EPS_RMS = 1e-6


class Mem:

    def __init__(self, nc):
        self.nc, self.stack = nc, ExitStack()

    def __enter__(self):
        self.stack.__enter__()
        return self

    def __exit__(self, *a):
        return self.stack.__exit__(*a)

    def sb(self, name, shape, dt=F32):
        return self.stack.enter_context(self.nc.sbuf_tensor(name, shape, dt))

    def sem(self, name):
        return self.stack.enter_context(self.nc.semaphore(name))


def pair_columns(ap, p, n=1):
    return ap[:, :, ds(p * 2 * T, 2 * T * n)].rearrange("q c (i t) -> q c i t", t=T)


def tokens_stage(nc, d, ps, h_all, zT, ident):
    with Mem(nc) as m:
        w = m.sb("tok_w", [P, DC, E])
        xt = m.sb("tok_x", [P, 2, DC, P])
        pos, bias = m.sb("tok_pos", [P, E]), m.sb("tok_bias", [P, E])
        gamma, beta = m.sb("tok_gamma", [P, E]), m.sb("tok_beta", [P, E])
        add = m.sb("tok_add", [P, E])
        stats = m.sb("tok_stats", [P, PAIRS, 6])
        mv = m.sb("tok_mv", [P, 2, PAIRS, 2])
        ve, sd, rs = m.sb("tok_ve", [P, 2, PAIRS]), m.sb("tok_sd", [P, 2, PAIRS]), m.sb("tok_rs", [P, 2, PAIRS])
        z = m.sb("tok_z", [P, 2, E])
        w_in, tab_in = m.sem("w_in"), m.sem("tab_in")
        x_in = [m.sem("x_in0"), m.sem("x_in1")]
        add_ready, proj_done, h_ready, stats_ready, mv_ready = (m.sem(n) for n in (
            "add_ready", "proj_done", "h_ready", "stats_ready", "mv_ready"))
        ve_ready, sd_ready, rs_ready = m.sem("ve_ready"), m.sem("sd_ready"), m.sem("rs_ready")
        n_ready, g_ready, h0_ready = m.sem("n_ready"), m.sem("g_ready"), m.sem("h0_ready")
        stats2_ready, mv2_ready = m.sem("stats2_ready"), m.sem("mv2_ready")
        z_ready, zt_done, zt_out = m.sem("z_ready"), m.sem("zt_done"), m.sem("zt_out")
        block = m.stack.enter_context(nc.Block())

        @block.sync
        def _(sp):
            sp.dma_start(w[:], d["tok_W"]).then_inc(w_in, 16)
            for s in range(2):
                sp.dma_start(xt[:, s], d["xT"][s]).then_inc(x_in[s], 16)
            for t, src in ((pos, "t_pos"), (bias, "t_bias"), (gamma, "t_gamma"), (beta, "t_beta")):
                sp.dma_start(t[:], d[src]).then_inc(tab_in, 16)
            sp.dma_start(ident[:], d["ident"]).then_inc(tab_in, 16)
            with sp.Fori(0, PAIRS // 2 - 1) as i:
                for s in range(2):
                    sp.wait_ge(proj_done, 2 * i + s + 1)
                    sp.dma_start(xt[:, s], d["xT"][ds(2 * i + s + 2, 1)].rearrange("a p c n -> (a p) c n")
                                 ).then_inc(x_in[s], 16)

        @block.tensor
        def _(pe):
            def project(i, s, first):
                pe.wait_ge(x_in[s], 16 * i + 16)
                if not first:
                    pe.wait_ge(h_ready, 2 * i + s - 1)
                for c in range(DC):
                    mm = pe.matmul(ps[:, s, 0:E], xt[:, s, c, :], w[:, c, :], start=(c == 0), stop=(c == DC - 1))
                mm.then_inc(proj_done, 1)

            pe.wait_ge(w_in, 16)
            for s in range(2):
                project(0, s, True)
            with pe.Fori(1, PAIRS // 2) as i:
                for s in range(2):
                    project(i, s, False)
            pe.wait_ge(tab_in, 80)

            def turn(i, s, first):
                pe.wait_ge(z_ready, 2 * i + s + 1)
                if not first:
                    pe.wait_ge(zt_out, 2 * i + s - 1)
                for c in range(EC):
                    mm = pe.transpose(ps[:, 2 + s, c * P:(c + 1) * P], z[:, s, c * P:(c + 1) * P], ident[:])
                mm.then_inc(zt_done, 1)

            for s in range(2):
                turn(0, s, True)
            with pe.Fori(1, PAIRS // 2) as i:
                for s in range(2):
                    turn(i, s, False)

        @block.vector
        def _(dve):
            dve.wait_ge(tab_in, 80)
            dve.tensor_tensor(add[:], pos[:], bias[:], ALU.add).then_inc(add_ready, 1)
            dve.wait_ge(add_ready, 1)
            with dve.Fori(0, PAIRS // 2) as i:
                for s in range(2):
                    p = 2 * i + s
                    dve.wait_ge(proj_done, p + 1)
                    h = h_all[:, ds(p, 1), :].rearrange("q a e -> q (a e)")
                    dve.tensor_tensor(h, ps[:, s, 0:E], add[:], ALU.add).then_inc(h_ready, 1)
                    dve.wait_ge(h_ready, p + 1)
                    st = stats[:, ds(p, 1), :].rearrange("q a e -> q (a e)")
                    dve.bn_stats(st, h).then_inc(stats_ready, 1)

            def inverse_deviation(k, st_ready, ready):
                dve.wait_ge(st_ready, PAIRS)
                for p in range(PAIRS):
                    dve.bn_aggr(mv[:, k, p], stats[:, p]).then_inc(ready, 1)
                dve.wait_ge(ready, PAIRS)
                dve.tensor_scalar(ve[:, k], mv[:, k, :, 1], EPS_LN, None, ALU.add).then_inc(ve_ready, 1)
                dve.wait_ge(sd_ready, k + 1)
                dve.reciprocal(rs[:, k], sd[:, k]).then_inc(rs_ready, 1)
                dve.wait_ge(rs_ready, k + 1)

            inverse_deviation(0, stats_ready, mv_ready)
            with dve.Fori(0, PAIRS) as p:
                h = h_all[:, ds(p, 1), :].rearrange("q a e -> q (a e)")
                dve.tensor_scalar(h, h, mv[:, 0, ds(p, 1), 0], rs[:, 0, ds(p, 1)],
                                  ALU.subtract, ALU.mult).then_inc(n_ready, 1)
                dve.wait_ge(n_ready, p + 1)
                dve.tensor_tensor(h, h, gamma[:], ALU.mult).then_inc(g_ready, 1)
                dve.wait_ge(g_ready, p + 1)
                dve.tensor_tensor(h, h, beta[:], ALU.add).then_inc(h0_ready, 1)
                dve.wait_ge(h0_ready, p + 1)
                st = stats[:, ds(p, 1), :].rearrange("q a e -> q (a e)")
                dve.bn_stats(st, h).then_inc(stats2_ready, 1)
            inverse_deviation(1, stats2_ready, mv2_ready)

            def normalised(i, s, first):
                p = 2 * i + s
                if not first:
                    dve.wait_ge(zt_done, 2 * i + s - 1)
                h = h_all[:, ds(p, 1), :].rearrange("q a e -> q (a e)")
                dve.tensor_scalar(z[:, s], h, mv[:, 1, ds(p, 1), 0], rs[:, 1, ds(p, 1)],
                                  ALU.subtract, ALU.mult).then_inc(z_ready, 1)

            for s in range(2):
                normalised(0, s, True)
            with dve.Fori(1, PAIRS // 2) as i:
                for s in range(2):
                    normalised(i, s, False)

        @block.scalar
        def _(act):
            for k in range(2):
                act.wait_ge(ve_ready, k + 1)
                act.activation(sd[:, k], ve[:, k], ACT.Sqrt).then_inc(sd_ready, 1)
            with act.Fori(0, PAIRS // 2) as i:
                for s in range(2):
                    p = 2 * i + s
                    act.wait_ge(zt_done, p + 1)
                    src = ps[:, 2 + s, 0:E].rearrange("q (c i t) -> q c i t", c=EC, i=2)
                    for c in range(EC):
                        cp = act.activation(pair_columns(zT, p)[:, c], src[:, c, :, 0:T], ACT.Copy)
                    cp.then_inc(zt_out, 1)


def projections_stage(nc, d, ps, zT, kn, qn, v_rows):
    TILES = -(-TOKENS // P)
    NV = 2 * E
    with Mem(nc) as m:
        wi, wk, wq = (m.sb(n, [P, EC, E]) for n in ("w_in_t", "w_k_t", "w_q_t"))
        wvb = m.sb("w_vb_t", [P, EC, NV])
        bb = m.sb("b_beta_rows", [P, E])
        ones = m.sb("block_ones", [P, P])
        half = m.sb("tanh_half", [P, 2, CHUNK])
        xpT = m.sb("xpT", [P, EC, TOKENS])
        kT, qT = m.sb("kT", [P, EC, TOKENS]), m.sb("qT", [P, EC, TOKENS])
        sq = m.sb("k_squares", [P, 2, CHUNK])
        nrm = m.sb("k_norm", [P, EC, TOKENS])
        vb = m.sb("vb", [P, 2, NV])
        rest = m.sb("vb_rest", [P, 2, NV])
        parts = m.sb("vb_parts", [P, 2, PARTS, NV], BF16)
        (wts_in, mm_done, th_ready, xp2_ready, xp_ready, k_done, q_done, sq_ready, n2_done, n_ready, e_ready, r_ready,
         k_ready, kc_ready, qc_ready, turned, vb_done, bx_ready, bt_ready, b_ready, v_ready, p0_ready, r1_ready,
         p1_ready, p2_ready) = (m.sem(n) for n in (
            "wts_in", "mm_done", "th_ready", "xp2_ready", "xp_ready", "k_done", "q_done", "sq_ready", "n2_done",
            "n_ready", "e_ready", "r_ready", "k_ready", "kc_ready", "qc_ready", "turned", "vb_done", "bx_ready",
            "bt_ready", "b_ready", "v_ready", "p0_ready", "r1_ready", "p1_ready", "p2_ready"))
        rows_out = [m.sem("rows_out0"), m.sem("rows_out1")]
        block = m.stack.enter_context(nc.Block())
        cells = [(n, c) for n in range(B4) for c in range(EC)]

        def cols(n):
            return slice(n * CHUNK, (n + 1) * CHUNK)

        @block.sync
        def _(sp):
            for t, src in ((wi, "W_in"), (wk, "W_k"), (wq, "W_q"), (wvb, "W_vb"), (bb, "b_beta"), (ones, "block_ones")):
                sp.dma_start(t[:], d[src]).then_inc(wts_in, 16)
            for h4 in range(B4):
                for b4 in range(B4):
                    if h4 == 0 and b4 == 0:
                        sp.wait_ge(qc_ready, len(cells))
                    sp.dma_start(qn[32 * b4:32 * b4 + 32, h4::B4, :], qT[32 * h4:32 * h4 + 32, :, cols(b4)]
                                 ).then_inc(turned, 16)
            sp.wait_ge(k_ready, 1)
            for h4 in range(B4):
                for b4 in range(B4):
                    sp.dma_start(kn[32 * b4:32 * b4 + 32, h4::B4, :], kT[32 * h4:32 * h4 + 32, :, cols(b4)]
                                 ).then_inc(turned, 16)
            for i in range(TILES):
                rows = min(P, TOKENS - i * P)
                sp.wait_ge(p2_ready, i + 1)
                sp.dma_start(v_rows[i * P:i * P + rows, :], parts[0:rows, i % 2].rearrange("p a n -> p (a n)")
                             ).then_inc(rows_out[i % 2], 16)
            sp.wait_ge(turned, 16 * 2 * B4 * B4)
            sp.wait_ge(rows_out[0], 16 * ((TILES + 1) // 2))
            sp.wait_ge(rows_out[1], 16 * (TILES // 2))

        @block.tensor
        def _(pe):
            pe.wait_ge(wts_in, 96)

            def product(w, src, bank, n, c):
                for k in range(EC):
                    mm = pe.matmul(ps[:, bank, 0:CHUNK], w[:, k, c * P:(c + 1) * P], src[:, k, cols(n)],
                                   start=(k == 0), stop=(k == EC - 1))
                return mm

            for j, (n, c) in enumerate(cells):
                if j >= 2:
                    pe.wait_ge(xp2_ready, j - 1)
                product(wi, zT, j % 2, n, c).then_inc(mm_done, 1)
            for j, (n, c) in enumerate(cells):
                pe.wait_ge(xp_ready, 1)
                if j >= 2:
                    pe.wait_ge(qc_ready, j - 1)
                product(wq, xpT, 2 + j % 2, n, c).then_inc(q_done, 1)
            for j, (n, c) in enumerate(cells):
                if j >= 2:
                    pe.wait_ge(kc_ready, j - 1)
                product(wk, xpT, 4 + j % 2, n, c).then_inc(k_done, 1)
                pe.wait_ge(sq_ready, j + 1)
                if j >= 2:
                    pe.wait_ge(n_ready, j - 1)
                pe.matmul(ps[:, 6 + j % 2, 0:CHUNK], ones[:], sq[:, j % 2, :], start=True, stop=True
                          ).then_inc(n2_done, 1)
            for i in range(TILES):
                rows = min(P, TOKENS - i * P)
                if i < 2:
                    pe.wait_ge(xp2_ready, len(cells))
                else:
                    pe.wait_ge(bx_ready, i - 1)
                    pe.wait_ge(v_ready, i - 1)
                for k in range(EC):
                    mm = pe.matmul(ps[0:rows, i % 2, :], xpT[:, k, i * P:i * P + rows], wvb[:, k, :],
                                   start=(k == 0), stop=(k == EC - 1))
                mm.then_inc(vb_done, 1)

        @block.scalar
        def _(act):
            def root(j):
                n, c = cells[j]
                act.wait_ge(n2_done, j + 1)
                act.activation(nrm[:, c, cols(n)], ps[:, 6 + j % 2, 0:CHUNK], ACT.Sqrt).then_inc(n_ready, 1)

            for j, (n, c) in enumerate(cells):
                act.wait_ge(mm_done, j + 1)
                if j >= 2:
                    act.wait_ge(xp2_ready, j - 1)
                act.activation(half[:, j % 2], ps[:, j % 2, 0:CHUNK], ACT.Tanh, scale=0.5).then_inc(th_ready, 1)
            for j, (n, c) in enumerate(cells):
                act.wait_ge(q_done, j + 1)
                act.activation(qT[:, c, cols(n)], ps[:, 2 + j % 2, 0:CHUNK], ACT.Copy).then_inc(qc_ready, 1)
            for j, (n, c) in enumerate(cells):
                act.wait_ge(k_done, j + 1)
                if j >= 2:
                    act.wait_ge(n2_done, j - 1)
                act.activation(sq[:, j % 2], ps[:, 4 + j % 2, 0:CHUNK], ACT.Square).then_inc(sq_ready, 1)
                act.activation(kT[:, c, cols(n)], ps[:, 4 + j % 2, 0:CHUNK], ACT.Copy).then_inc(kc_ready, 1)
                if j >= 1:
                    root(j - 1)
            root(len(cells) - 1)
            for i in range(TILES):
                rows = min(P, TOKENS - i * P)
                s = i % 2
                act.wait_ge(bx_ready, i + 1)
                act.activation(vb[0:rows, s, E:], vb[0:rows, s, E:], ACT.Tanh, scale=0.5).then_inc(bt_ready, 1)
                act.wait_ge(b_ready, i + 1)
                act.wait_ge(v_ready, i + 1)
                if i >= 2:
                    act.wait_ge(rows_out[s], 16 * (i // 2))
                act.activation(parts[0:rows, s, 0], vb[0:rows, s], ACT.Copy).then_inc(p0_ready, 1)
                act.wait_ge(r1_ready, i + 1)
                act.activation(parts[0:rows, s, 1], rest[0:rows, s], ACT.Copy).then_inc(p1_ready, 1)

        @block.vector
        def _(dve):
            for j, (n, c) in enumerate(cells):
                dve.wait_ge(th_ready, j + 1)
                dve.scalar_tensor_tensor(out=xpT[:, c, cols(n)], in0=half[:, j % 2], scalar=1.0,
                                         in1=ps[:, j % 2, 0:CHUNK], op0=ALU.add, op1=ALU.mult).then_inc(xp2_ready, 1)
            dve.wait_ge(xp2_ready, len(cells))
            dve.tensor_scalar(xpT[:], xpT[:], 0.5, None, ALU.mult).then_inc(xp_ready, 1)
            dve.wait_ge(n_ready, len(cells))
            dve.tensor_scalar(nrm[:], nrm[:], 1e-6, None, ALU.add).then_inc(e_ready, 1)
            dve.wait_ge(e_ready, 1)
            dve.reciprocal(nrm[:], nrm[:]).then_inc(r_ready, 1)
            dve.wait_ge(r_ready, 1)
            dve.wait_ge(kc_ready, len(cells))
            dve.tensor_tensor(kT[:], kT[:], nrm[:], ALU.mult).then_inc(k_ready, 1)
            for i in range(TILES):
                rows = min(P, TOKENS - i * P)
                s = i % 2
                dve.wait_ge(vb_done, i + 1)
                if i >= 2:
                    dve.wait_ge(p0_ready, i - 1)
                dve.tensor_tensor(vb[0:rows, s, E:], ps[0:rows, s, E:], bb[0:rows], ALU.add).then_inc(bx_ready, 1)
                dve.tensor_copy(vb[0:rows, s, 0:E], ps[0:rows, s, 0:E]).then_inc(v_ready, 1)
                dve.wait_ge(bt_ready, i + 1)
                dve.tensor_scalar(vb[0:rows, s, E:], vb[0:rows, s, E:], 0.5, 0.5, ALU.mult, ALU.add).then_inc(b_ready, 1)
                dve.wait_ge(p0_ready, i + 1)
                dve.tensor_tensor(rest[0:rows, s], vb[0:rows, s], parts[0:rows, s, 0], ALU.subtract).then_inc(r1_ready, 1)
                dve.wait_ge(p1_ready, i + 1)
                dve.tensor_tensor(parts[0:rows, s, 2], rest[0:rows, s], parts[0:rows, s, 1], ALU.subtract
                                  ).then_inc(p2_ready, 1)


def scan_stage(nc, d, ps, kn, qn, v_rows, o_rows):
    HALF = B8 // 2
    N = HALF * E
    LAST = T - 1
    with Mem(nc) as m:
        S = [m.sb(f"state{a}", [P, N]) for a in range(2)]
        Pb = [m.sb(f"s_times_kn{a}", [P, N]) for a in range(2)]
        Qb = [m.sb(f"s_times_q{a}", [P, N]) for a in range(2)]
        Tb = [m.sb(f"beta_s{a}", [P, N]) for a in range(2)]
        bsb = [m.sb(f"beta_sb{a}", [P, N]) for a in range(2)]
        vrow = m.sb("v_row", [P, 2, B8, 2, E], BF16)
        obuf = m.sb("o_buf", [16, 2, 2, E])
        sel = m.sb("part_rows_to_block", [P, P], BF16)
        neg = m.sb("minus_block_ones", [P, P])
        osel = m.sb("block_sum_to_row", [P, 4, P])
        p_ready, r_done, u_ready, a_ready, s_ready, q_ready, o_done, t_ready = (
            [m.sem(f"{n}{a}") for a in range(2)] for n in (
                "p_ready", "r_done", "u_ready", "a_ready", "s_ready", "q_ready", "o_done", "t_ready"))
        beta_done, beta_ready, v1_done, o_out = (m.sem(n) for n in ("beta_done", "beta_ready", "v1_done", "o_out"))
        row_in, stored = ([m.sem(f"{n}{s}") for s in range(2)] for n in ("row_in", "stored"))
        zeroed, row_zeroed, const_in = m.sem("zeroed"), m.sem("row_zeroed"), m.sem("const_in")
        block = m.stack.enter_context(nc.Block())

        def st(ap):
            return ap.rearrange("q (b h i) -> q b h i", b=HALF, h=NH_CELL)

        def vec(ap, t, a):
            v = ap[:].rearrange("q h (b t) -> q b h t", t=T)[:, HALF * a:HALF * a + HALF, :, ds(t, 1)]
            return v.broadcast_to([P, HALF, NH_CELL, NCELL])

        def D(a):
            return ps[:, 2 * a:2 * a + 2, :].rearrange("q n (b h i) -> q (n b) h i", h=NH_CELL, i=NCELL)

        def cycles(eng, cycle, first=4, last=LAST + 1):
            for c in range(first):
                cycle(c, c % 2)
            with eng.Fori(first // 2, LAST // 2) as i:
                for s in range(2):
                    cycle(2 * i + s, s, i)
            for c in range(2 * (LAST // 2), last + 1):
                cycle(c, c % 2)

        @block.sync
        def _(sp):
            for t, src in ((sel, "part_rows_to_block"), (neg, "minus_block_ones"), (osel, "block_sum_to_row")):
                sp.dma_start(t[:], d[src]).then_inc(const_in, 16)
            rows = v_rows.rearrange("(g b t) (a n) -> a g b t n", g=B4, t=T, a=PARTS)

            def load(t, s):
                for a in range(PARTS):
                    sp.dma_start(vrow[B4 * a:B4 * a + B4, s].rearrange("q b k m -> q b (k m)"),
                                 rows[a][:, :, ds(t, 1), :].rearrange("g b t n -> g b (t n)")).then_inc(row_in[s], 16)

            def store(t, s):
                for k in range(4):
                    sp.dma_start(o_rows.rearrange("(g k b) t n -> k g b t n", g=B4, k=4)[k][:, :, ds(t, 1), :]
                                 .rearrange("g b t n -> g b (t n)"), obuf[4 * k:4 * k + 4, s]).then_inc(stored[s], 16)

            sp.wait_ge(row_zeroed, 1)
            load(0, 0)
            load(1, 1)

            def cycle(c, s, i=None):
                if i is not None or c >= 2:
                    sp.wait_ge(o_out, c - 1)
                    store(c - 2, s)
                if i is not None or c + 2 <= LAST:
                    sp.wait_ge(v1_done, c + 1)
                    load(c + 2, s)

            cycles(sp, cycle, last=LAST + 2)
            for s in range(2):
                sp.wait_ge(stored[s], 16 * 4 * (T // 2))

        @block.gpsimd
        def _(pool):
            def cycle(c, s, i=None):
                for a in range(2):
                    pool.wait_ge(beta_ready, 2 * c + 1 + a)
                    if i is None and c == 0:
                        pool.wait_ge(zeroed, 2)
                    else:
                        pool.wait_ge(s_ready[a], c)
                    pool.tensor_tensor(Tb[a][:], bsb[a][:], S[a][:], ALU.mult).then_inc(t_ready[a], 1)

            cycles(pool, cycle, last=LAST)

        @block.scalar
        def _(act):
            def beta_copy(a, c, first):
                act.wait_ge(beta_done, 2 * c + 1 + a)
                if not first:
                    act.wait_ge(t_ready[a], c)
                act.activation(bsb[a][:], ps[:, 4:6, :].rearrange("q n x -> q (n x)"), ACT.Copy).then_inc(beta_ready, 1)

            def tanh(a, n):
                act.wait_ge(a_ready[a], n)
                act.activation(S[a][:], Tb[a][:], ACT.Tanh).then_inc(s_ready[a], 1)

            def cycle(c, s, i=None):
                if i is not None or c >= 2:
                    act.wait_ge(o_done[1], c - 1)
                    if i is not None or c >= 4:
                        stores = (c // 2 if i is None else i) - 1
                        act.wait_ge(stored[s], 64 * stores)
                    act.activation(obuf[:, s].rearrange("q b m -> q (b m)"), ps[0:16, 6 + s, :], ACT.Copy
                                   ).then_inc(o_out, 1)
                if i is not None or 1 <= c <= LAST + 1:
                    tanh(1, c)
                if i is not None or c <= LAST:
                    beta_copy(1, c, i is None and c == 0)
                    tanh(0, c + 1)
                if i is not None or c < LAST:
                    beta_copy(0, c + 1, False)

            beta_copy(0, 0, True)
            cycles(act, cycle, last=LAST + 2)

        @block.vector
        def _(dve):
            for s in range(2):
                ms = dve.memset(vrow[:, s].rearrange("q b k m -> q (b k m)"), 0.0)
            ms.then_inc(row_zeroed, 1)
            for a in range(2):
                dve.memset(S[a][:], 0.0).then_inc(zeroed, 1)
            dve.wait_ge(zeroed, 2)

            def s_kn(a, c, first):
                if not first:
                    dve.wait_ge(s_ready[a], c)
                dve.tensor_tensor(st(Pb[a][:]), st(S[a][:]), vec(kn, c, a), ALU.mult).then_inc(p_ready[a], 1)

            def s_q(a, t, first):
                dve.wait_ge(s_ready[a], t + 1)
                if not first:
                    dve.wait_ge(o_done[a], t)
                dve.tensor_tensor(st(Qb[a][:]), st(S[a][:]), vec(qn, t, a), ALU.mult).then_inc(q_ready[a], 1)

            def update(a, t):
                dve.wait_ge(r_done[a], t + 1)
                dve.tensor_tensor(D(a), D(a), vec(kn, t, a), ALU.mult).then_inc(u_ready[a], 1)
                dve.wait_ge(u_ready[a], t + 1)
                dve.wait_ge(t_ready[a], t + 1)
                dve.tensor_tensor(Tb[a][:], ps[:, 2 * a:2 * a + 2, :].rearrange("q n x -> q (n x)"), Tb[a][:],
                                  ALU.add).then_inc(a_ready[a], 1)

            def cycle(c, s, i=None):
                front, back = i is not None or c <= LAST, i is not None or c >= 1
                if front:
                    s_kn(0, c, i is None and c == 0)
                if back:
                    s_q(0, c - 1, i is None and c == 1)
                    update(1, c - 1)
                if front:
                    update(0, c)
                    s_kn(1, c, i is None and c == 0)
                if back:
                    s_q(1, c - 1, i is None and c == 1)

            cycles(dve, cycle)

        @block.tensor
        def _(pe):
            pe.wait_ge(const_in, 48)

            def rows(kind, a, s, bank, more):
                for n in range(2):
                    b = HALF * a + 2 * n
                    mm = pe.matmul(ps[:, bank + n, :].rearrange("q (b m) -> q b m", b=2), sel[:],
                                   vrow[:, s, b:b + 2, kind, :], start=True, stop=not more)
                return mm

            def sums(a):
                for n in range(2):
                    mm = pe.matmul(ps[:, 2 * a + n, :], neg[:], Pb[a][:, 512 * n:512 * n + 512], start=False, stop=True)
                mm.then_inc(r_done[a], 1)

            def outs(a, s):
                for n in range(2):
                    k = 2 * a + n
                    mm = pe.matmul(ps[:, 6 + s, :], osel[:, k, :], Qb[a][:, 512 * n:512 * n + 512],
                                   start=(k == 0), stop=(k == 3))
                mm.then_inc(o_done[a], 1)

            def cycle(c, s, i=None):
                front, back = i is not None or c <= LAST, i is not None or c >= 1
                if front:
                    pe.wait_ge(p_ready[0], c + 1)
                    sums(0)
                    pe.wait_ge(beta_ready, 2 * c + 1)
                    rows(1, 1, s, 4, False).then_inc(beta_done, 1)
                if back:
                    pe.wait_ge(q_ready[0], c)
                    if i is not None or c >= 3:
                        pe.wait_ge(o_out, c - 2)
                    outs(0, 1 - s)
                if front:
                    if back:
                        pe.wait_ge(a_ready[1], c)
                    rows(0, 1, s, 2, True).then_inc(v1_done, 1)
                if i is not None or c < LAST:
                    passes = (c + 1) // 2 if i is None else i + s
                    pe.wait_ge(row_in[1 - s], 48 * passes + 48)
                    pe.wait_ge(a_ready[0], c + 1)
                    rows(0, 0, 1 - s, 0, True)
                    pe.wait_ge(beta_ready, 2 * c + 2)
                    rows(1, 0, 1 - s, 4, False).then_inc(beta_done, 1)
                if front:
                    pe.wait_ge(p_ready[1], c + 1)
                    sums(1)
                if back:
                    pe.wait_ge(q_ready[1], c)
                    outs(1, 1 - s)

            pe.wait_ge(row_in[0], 48)
            rows(1, 0, 0, 4, False).then_inc(beta_done, 1)
            rows(0, 0, 0, 0, True)
            cycles(pe, cycle)


def row(ap, p):
    return ap[:, ds(p, 1), :].rearrange("q a e -> q (a e)")


def ring(eng, step, count=PAIRS):
    for s in range(2):
        step(s, s, True)
    with eng.Fori(1, count // 2) as i:
        for s in range(2):
            step(2 * i + s, s, False)


def cell_output_stage(nc, d, ps, o_pad, h_all, xh_all, xnT, ident):
    with Mem(nc) as m:
        wo = m.sb("w_out_t", [P, EC, E])
        g1 = m.sb("g1_cols", [P, EC])
        o = m.sb("o_tile", [P, 2, E])
        th, a = m.sb("o_tanh", [P, 2, E]), m.sb("o_gate", [P, 2, E])
        cell = m.sb("cell", [P, 2, E])
        cellT = m.sb("cellT", [P, 2, E])
        stats = m.sb("h1_stats", [P, PAIRS, 6])
        mv = m.sb("h1_mv", [P, PAIRS, 2])
        ve, sd, rs = m.sb("h1_ve", [P, PAIRS]), m.sb("h1_sd", [P, PAIRS]), m.sb("h1_rs", [P, PAIRS])
        ss, ms, rm, rr = (m.sb(n, [P, PAIRS]) for n in ("xh_ss", "xh_ms", "xh_rms", "xh_rrms"))
        junk = m.sb("xh_squares", [P, E])
        xn = m.sb("xn", [P, 2, E])
        (w_in, zeroed, th_ready, a_ready, c_ready, ct_done, ct_out, y_done, h_ready, st_ready, mv_ready, ve_ready,
         sd_ready, rs_ready, xh_ready, ss_ready, ms_ready, rm_ready, rr_ready, xn_ready, xt_done, xt_out) = (
            m.sem(n) for n in ("w_in", "zeroed", "th_ready", "a_ready", "c_ready", "ct_done", "ct_out", "y_done",
                               "h_ready", "st_ready", "mv_ready", "ve_ready", "sd_ready", "rs_ready", "xh_ready",
                               "ss_ready", "ms_ready", "rm_ready", "rr_ready", "xn_ready", "xt_done", "xt_out"))
        o_in = [m.sem("o_in0"), m.sem("o_in1")]
        block = m.stack.enter_context(nc.Block())

        @block.sync
        def _(sp):
            sp.dma_start(wo[:], d["W_out"]).then_inc(w_in, 16)
            sp.dma_start(g1[:], d["g1"]).then_inc(w_in, 16)
            sp.wait_ge(zeroed, 1)

            def load(p, s, first):
                if not first:
                    sp.wait_ge(c_ready, p - 1)
                for k in range(2):
                    sp.dma_start(o[SLOT * k:SLOT * k + T, s], o_pad[ds(2 * p + k, 1)].rearrange("a t m -> (a t) m")
                                 ).then_inc(o_in[s], 16)

            ring(sp, load)

        @block.scalar
        def _(act):
            def gate(p, s, first):
                act.wait_ge(o_in[s], 32 * (p // 2) + 32 if first else 16 * (p - s) + 32)
                if not first:
                    act.wait_ge(a_ready, p - 1)
                act.activation(th[:, s], o[:, s], ACT.Tanh, scale=0.5).then_inc(th_ready, 1)
                act.wait_ge(ct_done, p + 1)
                if not first:
                    act.wait_ge(y_done, p - 1)
                act.activation(cellT[:, s], ps[:, s, 0:E], ACT.Copy).then_inc(ct_out, 1)

            ring(act, gate)
            act.wait_ge(ve_ready, 1)
            act.activation(sd[:], ve[:], ACT.Sqrt).then_inc(sd_ready, 1)

            def squares(p):
                act.wait_ge(xh_ready, p + 1)
                act.activation(junk[:], row(xh_all, p), ACT.Square, accum_out=ss[:, ds(p, 1)]).then_inc(ss_ready, 1)

            squares(0)
            with act.Fori(1, PAIRS) as p:
                act.wait_ge(ss_ready, p)
                squares(p)
            act.wait_ge(ms_ready, 1)
            act.activation(rm[:], ms[:], ACT.Sqrt).then_inc(rm_ready, 1)
            with act.Fori(0, PAIRS // 2) as i:
                for s in range(2):
                    act.wait_ge(xt_done, 2 * i + s + 1)
                    for c in range(EC):
                        cp = act.activation(xnT[:, c, ds((2 * i + s) * P, P)], ps[:, 4 + s, c * P:(c + 1) * P],
                                            ACT.Copy, scale=g1[:, c:c + 1])
                    cp.then_inc(xt_out, 1)

        @block.tensor
        def _(pe):
            pe.wait_ge(w_in, 32)

            def turn(p, s, first):
                pe.wait_ge(c_ready, p + 1)
                if not first:
                    pe.wait_ge(ct_out, p - 1)
                for c in range(EC):
                    mm = pe.transpose(ps[:, s, c * P:(c + 1) * P], cell[:, s, c * P:(c + 1) * P], ident[:])
                mm.then_inc(ct_done, 1)
                pe.wait_ge(ct_out, p + 1)
                if not first:
                    pe.wait_ge(h_ready, p - 1)
                for c in range(EC):
                    mm = pe.matmul(ps[:, 2 + s, 0:E], cellT[:, s, c * P:(c + 1) * P], wo[:, c, :],
                                   start=(c == 0), stop=(c == EC - 1))
                mm.then_inc(y_done, 1)

            ring(pe, turn)

            def turn_xn(p, s, first):
                pe.wait_ge(xn_ready, p + 1)
                if not first:
                    pe.wait_ge(xt_out, p - 1)
                for c in range(EC):
                    mm = pe.transpose(ps[:, 4 + s, c * P:(c + 1) * P], xn[:, s, c * P:(c + 1) * P], ident[:])
                mm.then_inc(xt_done, 1)

            ring(pe, turn_xn)

        @block.vector
        def _(dve):
            dve.memset(o[:].rearrange("q a e -> q (a e)"), 0.0).then_inc(zeroed, 1)

            def front(p, s, first):
                dve.wait_ge(th_ready, p + 1)
                dve.scalar_tensor_tensor(out=a[:, s], in0=th[:, s], scalar=1.0, in1=o[:, s], op0=ALU.add, op1=ALU.mult
                                         ).then_inc(a_ready, 1)
                dve.wait_ge(a_ready, p + 1)
                if not first:
                    dve.wait_ge(ct_done, p - 1)
                dve.scalar_tensor_tensor(out=cell[:, s], in0=a[:, s], scalar=0.5, in1=o[:, s], op0=ALU.mult,
                                         op1=ALU.mult).then_inc(c_ready, 1)

            def back(p, s):
                dve.wait_ge(y_done, p + 1)
                dve.tensor_tensor(row(h_all, p), ps[:, 2 + s, 0:E], row(h_all, p), ALU.add).then_inc(h_ready, 1)
                dve.wait_ge(h_ready, p + 1)
                dve.bn_stats(row(stats, p), row(h_all, p)).then_inc(st_ready, 1)

            front(0, 0, True)
            front(1, 1, True)
            back(0, 0)
            with dve.Fori(1, PAIRS // 2) as i:
                front(2 * i, 0, False)
                back(2 * i - 1, 1)
                front(2 * i + 1, 1, False)
                back(2 * i, 0)
            back(PAIRS - 1, 1)
            dve.wait_ge(st_ready, PAIRS)
            for p in range(PAIRS):
                dve.bn_aggr(mv[:, p], stats[:, p]).then_inc(mv_ready, 1)
            dve.wait_ge(mv_ready, PAIRS)
            dve.tensor_scalar(ve[:], mv[:, :, 1], EPS_LN, None, ALU.add).then_inc(ve_ready, 1)
            dve.wait_ge(sd_ready, 1)
            dve.reciprocal(rs[:], sd[:]).then_inc(rs_ready, 1)
            dve.wait_ge(rs_ready, 1)
            with dve.Fori(0, PAIRS) as p:
                dve.tensor_scalar(row(xh_all, p), row(h_all, p), mv[:, ds(p, 1), 0], rs[:, ds(p, 1)],
                                  ALU.subtract, ALU.mult).then_inc(xh_ready, 1)
            dve.wait_ge(ss_ready, PAIRS)
            dve.tensor_scalar(ms[:], ss[:], 1.0 / E, EPS_RMS, ALU.mult, ALU.add).then_inc(ms_ready, 1)
            dve.wait_ge(rm_ready, 1)
            dve.reciprocal(rr[:], rm[:]).then_inc(rr_ready, 1)
            dve.wait_ge(rr_ready, 1)
            dve.wait_ge(xh_ready, PAIRS)

            def scaled(p, s, first):
                if not first:
                    dve.wait_ge(xt_done, p - 1)
                dve.tensor_scalar(xn[:, s], row(xh_all, p), rr[:, ds(p, 1)], None, ALU.mult).then_inc(xn_ready, 1)

            ring(dve, scaled)


def rotary_stage(nc, d, ps, xnT, qr, kr):
    NW = 512
    SLOTS = PAIRS * P // NW
    cells = [(n, c) for n in range(SLOTS) for c in range(EC)]
    with Mem(nc) as m:
        w = m.sb("w_rope", [P, 4, EC, E])
        cos, sin = m.sb("cos", [P, SLOT]), m.sb("sin", [P, SLOT])
        t1, t2 = m.sb("rope_cos", [P, 2, 2, NW]), m.sb("rope_sin", [P, 2, 2, NW])
        w_in, mm_done, t1_ready, t2_ready, r_ready = (m.sem(n) for n in (
            "w_in", "mm_done", "t1_ready", "t2_ready", "r_ready"))
        block = m.stack.enter_context(nc.Block())

        @block.sync
        def _(sp):
            for k, src in enumerate(("wq", "wk", "wq_perm", "wk_perm")):
                sp.dma_start(w[:, k], d[src]).then_inc(w_in, 16)
            sp.dma_start(cos[:], d["cos"]).then_inc(w_in, 16)
            sp.dma_start(sin[:], d["sin"]).then_inc(w_in, 16)

        @block.tensor
        def _(pe):
            pe.wait_ge(w_in, 96)
            for j, (n, c) in enumerate(cells):
                if j >= 2:
                    pe.wait_ge(t2_ready, 2 * j - 2)
                for k in range(4):
                    for e in range(EC):
                        mm = pe.matmul(ps[:, 4 * (j % 2) + k, :], w[:, k, e, c * P:(c + 1) * P],
                                       xnT[:, e, n * NW:(n + 1) * NW], start=(e == 0), stop=(e == EC - 1))
                mm.then_inc(mm_done, 1)

        @block.vector
        def _(dve):
            dve.wait_ge(w_in, 96)

            def tab(t):
                return t[:].rearrange("q (a t) -> q a t", a=1).broadcast_to([P, NW // SLOT, SLOT])

            for j, (n, c) in enumerate(cells):
                dve.wait_ge(mm_done, j + 1)
                if j >= 2:
                    dve.wait_ge(r_ready, 2 * j - 2)
                for k in range(2):
                    for t, table, bank, ready in ((t1, cos, k, t1_ready), (t2, sin, 2 + k, t2_ready)):
                        dve.tensor_tensor(t[:, j % 2, k].rearrange("q (a t) -> q a t", t=SLOT),
                                          ps[:, 4 * (j % 2) + bank, :].rearrange("q (a t) -> q a t", t=SLOT),
                                          tab(table), ALU.mult).then_inc(ready, 1)

        @block.gpsimd
        def _(pool):
            for j, (n, c) in enumerate(cells):
                for k, dst in enumerate((qr, kr)):
                    pool.wait_ge(t1_ready, 2 * j + k + 1)
                    pool.wait_ge(t2_ready, 2 * j + k + 1)
                    pool.tensor_tensor(dst[:, c, n * NW:(n + 1) * NW], t1[:, j % 2, k], t2[:, j % 2, k], ALU.add
                                       ).then_inc(r_ready, 1)
            pool.wait_ge(r_ready, 2 * len(cells))


def attention_stage(nc, d, ps, xnT, qr, kr, h_all, xh_all, ss, ident):
    W = HG * T
    with Mem(nc) as m:
        wv, wo = m.sb("wv", [P, EC, E]), m.sb("wo", [P, EC, E])
        causal = m.sb("causal", [P, T])
        hmask = m.sb("head_mask", [P, HG])
        q = m.sb("q_pair", [P, 2, EC, P])
        x = m.sb("xn_pair", [P, 2, EC, 2, 2, SLOT])
        km = m.sb("k_masked", [P, 2, EC, 2, HG, T])
        v2 = m.sb("v_blocks", [P, 2, 2, HEADS // 2, 2, DH])
        sc = m.sb("scores", [P, 2, HEADS, T])
        pr = m.sb("probs", [P, 2, HEADS, SLOT])
        pt = m.sb("probs_t", [P, 2, HEADS // 2, P])
        mx, sm, ri = m.sb("max", [P, 2, HEADS]), m.sb("sum", [P, 2, HEADS]), m.sb("inv_sum", [P, 2, HEADS])
        at = m.sb("attn", [P, 2, E])
        atT = m.sb("attnT", [P, 2, E])
        junk = m.sb("hh_squares", [P, E])
        (c_in, zeroed, x_ready, q_ready, k_ready, v_done, v_out, s_done, sc_ready, mx_ready, sub_ready, p_ready,
         sum_ready, ri_ready, pt_done, pt_out, pv_done, at_ready, at_done, at_out, wo_done, hh_ready, r_ready,
         ss_ready) = (m.sem(n) for n in (
            "c_in", "zeroed", "x_ready", "q_ready", "k_ready", "v_done", "v_out", "s_done", "sc_ready", "mx_ready",
            "sub_ready", "p_ready", "sum_ready", "ri_ready", "pt_done", "pt_out", "pv_done", "at_ready", "at_done",
            "at_out", "wo_done", "hh_ready", "r_ready", "ss_ready"))
        block = m.stack.enter_context(nc.Block())
        PT, SC, VB, PV, AT, WO = 0, 2, 4, 5, 6, 7

        def cycles(eng, cycle):
            for c in range(4):
                cycle(c, c % 2, False)
            with eng.Fori(2, PAIRS // 2) as i:
                for s in range(2):
                    cycle(2 * i + s, s, True)
            cycle(PAIRS, 0, False)
            cycle(PAIRS + 1, 1, False)

        def has(c, loop, lag):
            return loop or 0 <= c - lag < PAIRS

        @block.sync
        def _(sp):
            for t, src in ((wv, "wv"), (wo, "wo"), (causal, "causal"), (hmask, "head_mask")):
                sp.dma_start(t[:], d[src]).then_inc(c_in, 16)

        @block.gpsimd
        def _(pool):
            pool.wait_ge(c_in, 64)

            def prepare(p, s, first):
                cols = ds(p * P, P)
                if not first:
                    pool.wait_ge(v_done, p - 1)
                for k in range(2):
                    cp = pool.tensor_copy(x[:, s, :, :, k, :], xnT[:, :, cols].rearrange("q c (i t) -> q c i t", i=2))
                cp.then_inc(x_ready, 1)
                if not first:
                    pool.wait_ge(s_done, p - 1)
                pool.tensor_copy(q[:, s], qr[:, :, cols]).then_inc(q_ready, 1)
                for c in range(EC):
                    for k in range(2):
                        keys = kr[:, c, ds(p * P + SLOT * k, T)].rearrange("q (a t) -> q a t", a=1)
                        mask = hmask[:].rearrange("q (h a) -> q h a", a=1)
                        mul = pool.tensor_tensor(km[:, s, c, k], keys.broadcast_to([P, HG, T]),
                                                 mask.broadcast_to([P, HG, T]), ALU.mult)
                mul.then_inc(k_ready, 1)

            ring(pool, prepare)

        @block.tensor
        def _(pe):
            pe.wait_ge(c_in, 64)

            def cycle(c, s, loop):
                if has(c, loop, 2):
                    pe.wait_ge(at_ready, c - 1)
                    if loop or c > 2:
                        pe.wait_ge(at_out, c - 2)
                    for e in range(EC):
                        mm = pe.transpose(ps[:, AT, e * P:(e + 1) * P], at[:, s, e * P:(e + 1) * P], ident[:])
                    mm.then_inc(at_done, 1)
                if has(c, loop, 1):
                    pe.wait_ge(p_ready, c)
                    if loop or c > 1:
                        pe.wait_ge(pt_out, c - 1)
                    for h in range(HEADS // 2):
                        mm = pe.transpose(ps[:, PT + h // 4, (h % 4) * P:(h % 4 + 1) * P],
                                          pr[:, 1 - s, 2 * h:2 * h + 2, :].rearrange("q h k -> q (h k)"), ident[:])
                    mm.then_inc(pt_done, 1)
                if has(c, loop, 0):
                    pe.wait_ge(x_ready, c + 1)
                    if loop or c > 0:
                        pe.wait_ge(v_out, c)
                    for k in range(2):
                        for e in range(EC):
                            mm = pe.matmul(ps[:, VB, k * E:(k + 1) * E], x[:, s, e, k].rearrange("q a t -> q (a t)"),
                                           wv[:, e, :], start=(e == 0), stop=(e == EC - 1))
                    mm.then_inc(v_done, 1)
                    pe.wait_ge(q_ready, c + 1)
                    pe.wait_ge(k_ready, c + 1)
                    if loop or c > 0:
                        pe.wait_ge(sc_ready, c)
                    for e in range(EC):
                        for k in range(2):
                            mm = pe.matmul(ps[SLOT * k:SLOT * k + SLOT, SC + e, 0:W], q[:, s, e, SLOT * k:SLOT * k + SLOT],
                                           km[:, s, e, k].rearrange("q h t -> q (h t)"), start=True, stop=True)
                    mm.then_inc(s_done, 1)
                if has(c, loop, 1):
                    pe.wait_ge(pt_out, c)
                    if loop or c > 1:
                        pe.wait_ge(at_ready, c - 1)
                    for k in range(2):
                        for h in range(HEADS // 2):
                            mm = pe.matmul(ps[SLOT * k:SLOT * k + SLOT, PV, 32 * h:32 * h + 32],
                                           pt[:, 1 - s, h, SLOT * k:SLOT * k + SLOT],
                                           v2[:, 1 - s, k, h].rearrange("q a e -> q (a e)"), start=True, stop=True)
                    mm.then_inc(pv_done, 1)
                if has(c, loop, 2):
                    pe.wait_ge(at_out, c - 1)
                    if loop or c > 2:
                        pe.wait_ge(hh_ready, c - 2)
                    for e in range(EC):
                        mm = pe.matmul(ps[:, WO, 0:E], atT[:, s, e * P:(e + 1) * P], wo[:, e, :],
                                       start=(e == 0), stop=(e == EC - 1))
                    mm.then_inc(wo_done, 1)

            cycles(pe, cycle)

        @block.scalar
        def _(act):
            def cycle(c, s, loop):
                if has(c, loop, 2):
                    act.wait_ge(at_done, c - 1)
                    if loop or c > 3:
                        act.wait_ge(wo_done, c - 2)
                    act.activation(atT[:, s], ps[:, AT, 0:E], ACT.Copy).then_inc(at_out, 1)
                if has(c, loop, 1):
                    act.wait_ge(pt_done, c)
                    act.activation(pt[:, 1 - s].rearrange("q h k -> q (h k)"),
                                   ps[:, PT:PT + 2, :].rearrange("q n x -> q (n x)"), ACT.Copy).then_inc(pt_out, 1)
                if has(c, loop, 0):
                    act.wait_ge(v_done, c + 1)
                    if loop or c > 1:
                        act.wait_ge(pv_done, c - 1)
                    else:
                        act.wait_ge(zeroed, 2)
                    for k in range(2):
                        rows = slice(SLOT * k, SLOT * k + SLOT)
                        src = ps[rows, VB, :].rearrange("q (i h a e) -> q i h a e", i=2, a=2, e=DH)
                        cp = act.activation(v2[rows, s, :, :, k, :], src[:, :, :, k, :], ACT.Copy)
                    cp.then_inc(v_out, 1)
                    act.wait_ge(sub_ready, c + 1)
                    if loop or c > 1:
                        act.wait_ge(pt_done, c - 1)
                        act.wait_ge(sum_ready, c - 1)
                    act.activation(pr[:, s, :, 0:T], sc[:, s], ACT.Exp, scale=float(DH) ** -0.5).then_inc(p_ready, 1)
                if has(c, loop, 2):
                    act.wait_ge(hh_ready, c - 1)
                    if loop or c > 2:
                        act.wait_ge(ss_ready, c - 2)
                    act.activation(junk[:], row(xh_all, c - 2), ACT.Square, accum_out=ss[:, ds(c - 2, 1)]
                                   ).then_inc(ss_ready, 1)

            cycles(act, cycle)
            act.wait_ge(ss_ready, PAIRS)

        @block.vector
        def _(dve):
            dve.memset(v2[:].rearrange("q s i h a e -> q (s i h a e)"), 0.0).then_inc(zeroed, 1)
            dve.memset(pr[:].rearrange("q s h k -> q (s h k)"), 0.0).then_inc(zeroed, 1)
            dve.wait_ge(c_in, 64)

            def per_head(t, s, n):
                return t[:, s].rearrange("q (h a) -> q h a", a=1).broadcast_to([P, HEADS, n])

            def cycle(c, s, loop):
                if has(c, loop, 1):
                    dve.wait_ge(p_ready, c)
                    if loop or c > 2:
                        dve.wait_ge(ri_ready, c - 2)
                    dve.tensor_reduce(sm[:, 1 - s], pr[:, 1 - s, :, 0:T], AX.X, ALU.add).then_inc(sum_ready, 1)
                    dve.wait_ge(sum_ready, c)
                    dve.reciprocal(ri[:, 1 - s], sm[:, 1 - s]).then_inc(ri_ready, 1)
                if has(c, loop, 0):
                    dve.wait_ge(s_done, c + 1)
                    if loop or c > 1:
                        dve.wait_ge(p_ready, c - 1)
                    mask = causal[:].rearrange("q (a t) -> q a t", a=1).broadcast_to([P, HG, T])
                    for e in range(EC):
                        add = dve.tensor_tensor(sc[:, s, HG * e:HG * e + HG],
                                                ps[:, SC + e, 0:W].rearrange("q (h t) -> q h t", t=T), mask, ALU.add)
                    add.then_inc(sc_ready, 1)
                    dve.wait_ge(sc_ready, c + 1)
                    dve.tensor_reduce(mx[:, s], sc[:, s], AX.X, ALU.max).then_inc(mx_ready, 1)
                    dve.wait_ge(mx_ready, c + 1)
                    dve.tensor_tensor(sc[:, s], sc[:, s], per_head(mx, s, T), ALU.subtract).then_inc(sub_ready, 1)
                if has(c, loop, 1):
                    dve.wait_ge(pv_done, c)
                    dve.wait_ge(ri_ready, c)
                    if loop or c > 2:
                        dve.wait_ge(at_done, c - 2)
                    dve.tensor_tensor(at[:, 1 - s].rearrange("q (h e) -> q h e", e=DH),
                                      ps[:, PV, 0:E].rearrange("q (h e) -> q h e", e=DH),
                                      per_head(ri, 1 - s, DH), ALU.mult).then_inc(at_ready, 1)
                if has(c, loop, 2):
                    p = c - 2
                    dve.wait_ge(wo_done, c - 1)
                    dve.tensor_tensor(row(xh_all, p), ps[:, WO, 0:E], row(xh_all, p), ALU.add).then_inc(hh_ready, 1)
                    dve.wait_ge(hh_ready, c - 1)
                    dve.tensor_tensor(row(h_all, p), row(xh_all, p), row(h_all, p), ALU.add).then_inc(r_ready, 1)

            cycles(dve, cycle)
            dve.wait_ge(r_ready, PAIRS)


def router_stage(nc, d, ps, h_all, xh_all, ss, xfT, r_rows, c_rows, ident):
    with Mem(nc) as m:
        wr = m.sb("w_router", [P, EC, EXPERTS])
        g2 = m.sb("g2_cols", [P, EC])
        ms, rm, rr = (m.sb(n, [P, PAIRS]) for n in ("hh_ms", "hh_rms", "hh_rrms"))
        xf = m.sb("xf", [P, 2, E])
        xp = m.sb("xfT_pair", [P, 2, EC, P])
        lg = m.sb("logits", [P, PAIRS, EXPERTS])
        pb = m.sb("router_probs", [P, PAIRS, EXPERTS])
        top = m.sb("top8", [P, PAIRS, 8])
        best = m.sb("top2", [P, PAIRS, 8])
        left = m.sb("others", [P, PAIRS, EXPERTS])
        mask = m.sb("chosen", [P, PAIRS, EXPERTS])
        comb = m.sb("combine", [P, PAIRS, EXPERTS])
        red = m.sb("router_red", [P, 4, PAIRS])
        (w_in, ms_ready, rm_ready, rr_ready, xf_ready, xt_done, xt_out, l_done, l_ready, chain, e_ready, best_ready,
         top_ready, left_ready, comb_ready, stored) = (m.sem(n) for n in (
            "w_in", "ms_ready", "rm_ready", "rr_ready", "xf_ready", "xt_done", "xt_out", "l_done", "l_ready", "chain",
            "e_ready", "best_ready", "top_ready", "left_ready", "comb_ready", "stored"))
        block = m.stack.enter_context(nc.Block())

        @block.sync
        def _(sp):
            sp.dma_start(wr[:], d["w_router"]).then_inc(w_in, 16)
            sp.dma_start(g2[:], d["g2"]).then_inc(w_in, 16)
            for k in range(2):
                sp.dma_start(r_rows.rearrange("(p i t) e -> i t p e", i=2, t=T)[k], h_all[SLOT * k:SLOT * k + T]
                             ).then_inc(stored, 16)
            sp.wait_ge(comb_ready, 1)
            for k in range(2):
                sp.dma_start(c_rows.rearrange("(p i t) e -> i t p e", i=2, t=T)[k], comb[SLOT * k:SLOT * k + T]
                             ).then_inc(stored, 16)
            sp.wait_ge(stored, 64)

        @block.tensor
        def _(pe):
            pe.wait_ge(w_in, 32)

            def turn(p, s, first):
                pe.wait_ge(xf_ready, p + 1)
                if not first:
                    pe.wait_ge(xt_out, p - 1)
                for c in range(EC):
                    mm = pe.transpose(ps[:, s, c * P:(c + 1) * P], xf[:, s, c * P:(c + 1) * P], ident[:])
                mm.then_inc(xt_done, 1)
                pe.wait_ge(xt_out, p + 1)
                if not first:
                    pe.wait_ge(l_ready, p - 1)
                for c in range(EC):
                    mm = pe.matmul(ps[:, 2 + s, 0:EXPERTS], xp[:, s, c, :], wr[:, c, :], start=(c == 0), stop=(c == EC - 1))
                mm.then_inc(l_done, 1)

            ring(pe, turn)

        @block.scalar
        def _(act):
            act.wait_ge(ms_ready, 1)
            act.activation(rm[:], ms[:], ACT.Sqrt).then_inc(rm_ready, 1)
            act.wait_ge(w_in, 32)

            def out(p, s, first):
                act.wait_ge(xt_done, p + 1)
                if not first:
                    act.wait_ge(l_done, p - 1)
                for c in range(EC):
                    src = ps[:, s, c * P:(c + 1) * P]
                    act.activation(pair_columns(xfT, p)[:, c], src.rearrange("q (i t) -> q i t", i=2)[:, :, 0:T],
                                   ACT.Copy, scale=g2[:, c:c + 1])
                    cp = act.activation(xp[:, s, c], src, ACT.Copy, scale=g2[:, c:c + 1])
                cp.then_inc(xt_out, 1)

            ring(act, out)
            act.wait_ge(chain, 2)
            act.activation(pb[:], lg[:], ACT.Exp).then_inc(e_ready, 1)

        @block.vector
        def _(dve):
            dve.tensor_scalar(ms[:], ss[:], 1.0 / E, EPS_RMS, ALU.mult, ALU.add).then_inc(ms_ready, 1)
            dve.wait_ge(rm_ready, 1)
            dve.reciprocal(rr[:], rm[:]).then_inc(rr_ready, 1)
            dve.wait_ge(rr_ready, 1)

            def scaled(p, s, first):
                if not first:
                    dve.wait_ge(xt_done, p - 1)
                dve.tensor_scalar(xf[:, s], row(xh_all, p), rr[:, ds(p, 1)], None, ALU.mult).then_inc(xf_ready, 1)

            def logits(p, s):
                dve.wait_ge(l_done, p + 1)
                dve.tensor_copy(row(lg, p), ps[:, 2 + s, 0:EXPERTS]).then_inc(l_ready, 1)

            scaled(0, 0, True)
            scaled(1, 1, True)
            logits(0, 0)
            with dve.Fori(1, PAIRS // 2) as i:
                scaled(2 * i, 0, False)
                logits(2 * i - 1, 1)
                scaled(2 * i + 1, 1, False)
                logits(2 * i, 0)
            logits(PAIRS - 1, 1)

            def each(t):
                return t.rearrange("q (p a) -> q p a", a=1).broadcast_to([P, PAIRS, EXPERTS])

            dve.wait_ge(l_ready, PAIRS)
            dve.tensor_reduce(red[:, 0], lg[:], AX.X, ALU.max).then_inc(chain, 1)
            dve.wait_ge(chain, 1)
            dve.tensor_tensor(lg[:], lg[:], each(red[:, 0]), ALU.subtract).then_inc(chain, 1)
            dve.wait_ge(e_ready, 1)
            dve.tensor_reduce(red[:, 1], pb[:], AX.X, ALU.add).then_inc(chain, 1)
            dve.wait_ge(chain, 3)
            dve.reciprocal(red[:, 2], red[:, 1]).then_inc(chain, 1)
            dve.wait_ge(chain, 4)
            dve.tensor_tensor(pb[:], pb[:], each(red[:, 2]), ALU.mult).then_inc(chain, 1)
            dve.memset(best[:].rearrange("q p k -> q (p k)"), -1.0).then_inc(best_ready, 1)
            dve.wait_ge(chain, 5)
            for p in range(PAIRS):
                dve.max(top[:, p], pb[:, p]).then_inc(top_ready, 1)
            dve.wait_ge(top_ready, PAIRS)
            dve.wait_ge(best_ready, 1)
            dve.tensor_copy(best[:, :, 0:2], top[:, :, 0:2]).then_inc(best_ready, 1)
            dve.wait_ge(best_ready, 2)
            for p in range(PAIRS):
                dve.match_replace(left[:, p], best[:, p], pb[:, p], -1.0).then_inc(left_ready, 1)
            dve.wait_ge(left_ready, PAIRS)
            dve.tensor_tensor(mask[:], left[:], pb[:], ALU.not_equal).then_inc(chain, 1)
            dve.tensor_tensor(red[:, 3], top[:, :, 0], top[:, :, 1], ALU.add).then_inc(chain, 1)
            dve.wait_ge(chain, 7)
            dve.reciprocal(red[:, 0], red[:, 3]).then_inc(chain, 1)
            dve.tensor_tensor(comb[:], pb[:], mask[:], ALU.mult).then_inc(chain, 1)
            dve.wait_ge(chain, 9)
            dve.tensor_tensor(comb[:], comb[:], each(red[:, 0]), ALU.mult).then_inc(comb_ready, 1)


def experts_stage(nc, d, ps, xfT, r_rows, c_rows, out):
    TILES = -(-TOKENS // P)
    FULL = HID // P
    TAIL = HID - FULL * P
    chunks = [(c, min(512, TOKENS - c)) for c in range(0, TOKENS, 512)]
    NC = len(chunks)
    tiles = [[(c + t, min(P, c + n - c - t)) for t in range(0, n, P)] for c, n in chunks]
    with Mem(nc) as m:
        wg, wu = m.sb("wg", [P, 2, EC, FULL * P]), m.sb("wu", [P, 2, EC, FULL * P])
        wt = m.sb("w_gate_up_tail", [P, 2, EC, 2 * TAIL])
        wd = m.sb("wd", [P, 2, FULL + 1, E])
        acc = m.sb("acc", [P, TILES, E])
        comb = m.sb("comb", [P, TILES, EXPERTS])
        g = m.sb("gate", [P, 2, 512])
        h = m.sb("hidden", [P, 2, FULL + 1, 512])
        w_in = [m.sem("w_in0"), m.sem("w_in1")]
        r_in, gu_done, g_ready, h_ready, y_done, y_added, out_done = (m.sem(n) for n in (
            "r_in", "gu_done", "g_ready", "h_ready", "y_done", "y_added", "out_done"))
        block = m.stack.enter_context(nc.Block())
        M = FULL + 1
        TILES2 = 2 * TILES

        @block.sync
        def _(sp):
            def load(e, s):
                for t, name in ((wg, "wg"), (wu, "wu"), (wt, "w_tail"), (wd, "wd")):
                    sp.dma_start(t[:, s], d[name][ds(e, 1)].rearrange("a p k n -> (a p) k n")).then_inc(w_in[s], 16)

            load(0, 0)
            load(1, 1)
            for t in range(TILES):
                rows = min(P, TOKENS - t * P)
                sp.dma_start(acc[0:rows, t], r_rows[t * P:t * P + rows, :]).then_inc(r_in, 16)
                sp.dma_start(comb[0:rows, t], c_rows[t * P:t * P + rows, :]).then_inc(r_in, 16)
            with sp.Fori(0, EXPERTS // 2 - 1) as i:
                for s in range(2):
                    sp.wait_ge(y_done, TILES2 * i + TILES * (s + 1))
                    load(2 * i + s + 2, s)
            for t in range(TILES):
                rows = min(P, TOKENS - t * P)
                sp.wait_ge(y_added, TILES * (EXPERTS - 1) + t + 1)
                sp.dma_start(out[t * P:t * P + rows, :], acc[0:rows, t]).then_inc(out_done, 16)
            sp.wait_ge(out_done, 16 * TILES)

        def order(eng, up, down):
            def passage(i, first):
                for s in range(2):
                    for x in range(NC):
                        up(i, s, x, first)
                        if x:
                            down(i, s, x - 1)
                        elif s:
                            down(i, 0, NC - 1)
                        elif not first:
                            down(i - 1, 1, NC - 1)

            passage(0, True)
            with eng.Fori(1, EXPERTS // 2) as i:
                passage(i, False)
            down(EXPERTS // 2 - 1, 1, NC - 1)

        @block.tensor
        def _(pe):
            def up(i, s, x, first):
                c, n = chunks[x]
                if x == 0:
                    pe.wait_ge(w_in[s], 64 * i + 64)
                for j in range(M):
                    k = s * NC * M + x * M + j
                    if not first or k >= 2:
                        pe.wait_ge(h_ready, 2 * NC * M * i + k - 1)
                    for b, w in ((0, wg), (1, wu)) if j < FULL else ((0, None),):
                        for e in range(EC):
                            lhs = wt[:, s, e, :] if w is None else w[:, s, e, j * P:(j + 1) * P]
                            mm = pe.matmul(ps[:, 2 * (k % 2) + b, 0:n], lhs, xfT[:, e, c:c + n],
                                           start=(e == 0), stop=(e == EC - 1))
                    mm.then_inc(gu_done, 1)

            def down(i, s, x):
                k = s * NC + x
                pe.wait_ge(h_ready, 2 * NC * M * i + (k + 1) * M)
                for t, (row0, rows) in enumerate(tiles[x]):
                    n = s * TILES + row0 // P
                    if n >= 4 or not (isinstance(i, int) and i == 0):
                        pe.wait_ge(y_added, TILES2 * i + n - 3)
                    col = row0 - chunks[x][0]
                    for j in range(M):
                        lo = 0 if j < FULL else P - TAIL
                        mm = pe.matmul(ps[0:rows, 4 + n % 4, 0:E], h[lo:, k % 2, j, col:col + rows], wd[lo:, s, j, :],
                                       start=(j == 0), stop=(j == M - 1))
                    mm.then_inc(y_done, 1)

            order(pe, up, down)

        @block.scalar
        def _(act):
            def up(i, s, x, first):
                c, n = chunks[x]
                for j in range(M):
                    k = s * NC * M + x * M + j
                    act.wait_ge(gu_done, 2 * NC * M * i + k + 1)
                    if not first or k >= 2:
                        act.wait_ge(h_ready, 2 * NC * M * i + k - 1)
                    src, dst = (ps[0:P], g[0:P]) if j < FULL else (ps[0:TAIL], g[P - TAIL:P])
                    act.activation(dst[:, k % 2, 0:n], src[:, 2 * (k % 2), 0:n], ACT.Silu).then_inc(g_ready, 1)

            order(act, up, lambda i, s, x: None)

        @block.vector
        def _(dve):
            dve.wait_ge(r_in, 32 * TILES)

            def up(i, s, x, first):
                c, n = chunks[x]
                q = s * NC + x
                for j in range(M):
                    k = s * NC * M + x * M + j
                    dve.wait_ge(g_ready, 2 * NC * M * i + k + 1)
                    if j == 0 and (not first or q >= 2):
                        before = q - 2
                        done = (before // NC) * TILES + tiles[before % NC][-1][0] // P + 1
                        dve.wait_ge(y_done, TILES2 * i + done)
                    lo, bank = (0, 1) if j < FULL else (P - TAIL, 0)
                    dve.tensor_tensor(h[lo:, q % 2, j, 0:n], ps[lo:, 2 * (k % 2) + bank, 0:n], g[lo:, k % 2, 0:n],
                                      ALU.mult).then_inc(h_ready, 1)

            def down(i, s, x):
                for row0, rows in tiles[x]:
                    n = s * TILES + row0 // P
                    t = row0 // P
                    dve.wait_ge(y_done, TILES2 * i + n + 1)
                    dve.scalar_tensor_tensor(out=acc[0:rows, t], in0=ps[0:rows, 4 + n % 4, 0:E],
                                             scalar=comb[0:rows, t, ds(2 * i + s, 1)], in1=acc[0:rows, t],
                                             op0=ALU.mult, op1=ALU.add).then_inc(y_added, 1)

            order(dve, up, down)


def build(nc, d, out):
    v_rows = nc.dram_tensor("v_rows", (TOKENS, PARTS * 2 * E), BF16).ap()
    o_rows = nc.dram_tensor("o_rows", (IMAGES, T, E), F32).ap()
    r_rows = nc.dram_tensor("r_rows", (TOKENS, E), F32).ap()
    c_rows = nc.dram_tensor("c_rows", (TOKENS, EXPERTS), F32).ap()
    with nc.psum_tensor("ps", [P, 8, 512], F32) as ps, Mem(nc) as m:
        ident = m.sb("ident", [P, P])
        h_all = m.sb("h_all", [P, PAIRS, E])
        with Mem(nc) as cell:
            kn = cell.sb("kn", [P, NH_CELL, CHUNK])
            qn = cell.sb("qn", [P, NH_CELL, CHUNK])
            with Mem(nc) as early:
                zT = early.sb("zT", [P, EC, TOKENS])
                tokens_stage(nc, d, ps, h_all, zT, ident)
                projections_stage(nc, d, ps, zT, kn, qn, v_rows)
            scan_stage(nc, d, ps, kn, qn, v_rows, o_rows)
        xh_all = m.sb("xh_all", [P, PAIRS, E])
        ss = m.sb("hh_ss", [P, PAIRS])
        with Mem(nc) as att:
            xnT, qr, kr = (att.sb(n, [P, EC, PAIRS * P]) for n in ("xnT", "q_rot", "k_rot"))
            cell_output_stage(nc, d, ps, o_rows, h_all, xh_all, xnT, ident)
            rotary_stage(nc, d, ps, xnT, qr, kr)
            attention_stage(nc, d, ps, xnT, qr, kr, h_all, xh_all, ss, ident)
        xfT = m.sb("xfT", [P, EC, TOKENS])
        router_stage(nc, d, ps, h_all, xh_all, ss, xfT, r_rows, c_rows, ident)
        experts_stage(nc, d, ps, xfT, r_rows, c_rows, out)


def host_layout(np, bf16, inp):
    f = {k: np.ascontiguousarray(v) for k, v in inp.items()}
    a = {}

    def chunked(w):
        k = w.shape[0] // P
        return np.ascontiguousarray(w.reshape(k, P, w.shape[1]).transpose(1, 0, 2))

    x = f["x"].reshape(IMAGES, 3, 6, 16, 6, 16).transpose(0, 1, 3, 5, 2, 4).reshape(IMAGES, DC, P, PATCHES)
    xT = np.zeros((PAIRS, P, DC, 2, SLOT), np.float32)
    xT[..., 2:T] = x.reshape(PAIRS, 2, DC, P, PATCHES).transpose(0, 3, 2, 1, 4)
    a["xT"] = xT.reshape(PAIRS, P, DC, P)
    a["tok_W"] = chunked(f["L0_tok_W"])

    def padded(rows):
        t = np.zeros((2, SLOT, E), np.float32)
        t[:, :T] = rows
        return t.reshape(P, E)

    z = np.zeros((T, E), np.float32)
    pos, bias, gamma, beta = z.copy(), z.copy(), z.copy(), z.copy()
    pos[1:] = f["L0_tok_pos_embedding"][0]
    bias[1], bias[2:] = f["L0_tok_cls_token"][0, 0], f["L0_tok_b"]
    gamma[1:] = f["L0_tok_gamma"]
    beta[0], beta[1:] = f["cls_tok"][0, 0], f["L0_tok_beta"]
    a["t_pos"], a["t_bias"], a["t_gamma"], a["t_beta"] = (padded(t) for t in (pos, bias, gamma, beta))
    a["W_in"], a["W_k"], a["W_q"] = (chunked(f[f"L0_attn_{n}"].T) for n in ("W_in", "W_k", "W_q"))
    a["W_vb"] = chunked(np.concatenate([f["L0_attn_W_v"].T, f["L0_attn_W_beta"].T], 1))
    a["W_out"] = chunked(f["L0_attn_W_out"].T)
    a["b_beta"] = np.ascontiguousarray(np.broadcast_to(f["L0_attn_b_beta"].reshape(1, E), (P, E)))
    perm = np.arange(E).reshape(HEADS, 2, DH // 2)[:, ::-1].reshape(E)
    for n in ("wq", "wk"):
        a[n], a[n + "_perm"] = chunked(f[f"L0_ffn_{n}"]), chunked(f[f"L0_ffn_{n}"][:, perm])
    a["wv"], a["wo"] = chunked(f["L0_ffn_wv"]), chunked(f["L0_ffn_wo"])
    a["g1"], a["g2"] = (np.ascontiguousarray(f[f"L0_ffn_{n}"].reshape(EC, P).T) for n in ("g1", "g2"))
    a["w_router"] = chunked(f["L0_ffn_w_router"])
    full = HID // P * P
    by_expert = [[chunked(w) for w in f[f"L0_ffn_{n}"]] for n in ("wg", "wu")]
    a["wg"], a["wu"] = (np.ascontiguousarray(np.stack(w)[..., :full]) for w in by_expert)
    a["w_tail"] = np.concatenate([np.stack(w)[..., full:] for w in by_expert], -1)
    wd = np.zeros((EXPERTS, full + P, E), np.float32)
    wd[:, :full] = f["L0_ffn_wd"][:, :full]
    wd[:, full + P - (HID - full):] = f["L0_ffn_wd"][:, full:]
    a["wd"] = np.stack([chunked(w) for w in wd])

    p = np.arange(P)
    a["ident"] = np.eye(P, dtype=np.float32)
    block = p // NCELL
    a["block_ones"] = (block[:, None] == block[None]).astype(np.float32)
    a["minus_block_ones"] = -a["block_ones"]
    osel = np.zeros((P, 4, P), np.float32)
    for k in range(4):
        osel[p, k, B4 * k + block] = 1.0
    a["block_sum_to_row"] = osel
    rows = (p[:, None] < PARTS * B4) & (p[:, None] % B4 == block[None])
    a["part_rows_to_block"] = rows.astype(bf16)
    freq = 1.0 / 10000.0 ** (np.arange(0, DH, 2, dtype=np.float32) / DH)
    ang = np.einsum("i,j->ij", np.arange(T, dtype=np.float32), freq)
    ang = np.concatenate([ang, ang], -1)[:, p % DH].T
    cos, sin = np.zeros((P, SLOT), np.float32), np.zeros((P, SLOT), np.float32)
    cos[:, :T] = np.cos(ang)
    sin[:, :T] = np.sin(ang) * np.where(p % DH < DH // 2, -1.0, 1.0)[:, None]
    a["cos"], a["sin"] = cos.astype(np.float32), sin.astype(np.float32)
    t = p % SLOT
    a["causal"] = np.where(np.arange(T)[None] > t[:, None], -1e30, 0.0).astype(np.float32)
    a["head_mask"] = (p[:, None] // DH == np.arange(HG)[None]).astype(np.float32)
    return a


def kernel(**inputs):
    import ml_dtypes
    import numpy as np
    import concourse.bacc as bacc
    from concourse.bass_utils import run_bass_kernel_spmd

    nc = bacc.Bacc("TRN2", target_bir_lowering=False, num_devices=1)
    arrays = host_layout(np, ml_dtypes.bfloat16, inputs)
    d = {k: nc.dram_tensor(f"in_{k}", v.shape, mybir.dt.from_np(v.dtype), kind="ExternalInput").ap()
         for k, v in arrays.items()}
    out = nc.dram_tensor("out_0", (TOKENS, E), F32, kind="ExternalOutput").ap()
    build(nc, d, out)
    r = run_bass_kernel_spmd(nc, [{f"in_{k}": v for k, v in arrays.items()}], core_ids=[0])
    return r.results[0]["out_0"].reshape(IMAGES, T, E)
```

```python
from contextlib import ExitStack

import concourse.bass as bass
from concourse import mybir
from concourse.alu_op_type import AluOpType as ALU

ACT = mybir.ActivationFunctionType
AX = mybir.AxisListType
F32 = mybir.dt.float32
BF16 = mybir.dt.bfloat16
ds = bass.ds

P = 128
IMAGES = 32
PATCHES = 36
T = PATCHES + 2
E = 256
EC = E // P
DPATCH = 768
DC = DPATCH // P
PAIRS = IMAGES // 2
SLOT = 64
TOKENS = IMAGES * T
NH_CELL, NCELL = 8, 32
B4 = P // NCELL
B8 = IMAGES // B4
CHUNK = B8 * T
HEADS, DH = 16, 16
HG = HEADS // EC
EXPERTS = 8
HID = 704
TOPK = 2
TILES = (TOKENS * TOPK + EXPERTS * (P - 1)) // P
PARTS = 3
EPS_LN = 1e-5
EPS_RMS = 1e-6


class Mem:

    def __init__(self, nc, stage="core"):
        self.stage = stage
        self.nc, self.stack = nc, ExitStack()

    def __enter__(self):
        self.stack.__enter__()
        return self

    def __exit__(self, *a):
        return self.stack.__exit__(*a)

    def sb(self, name, shape, dt=F32):
        return self.stack.enter_context(self.nc.sbuf_tensor(name, shape, dt))

    def sem(self, name):
        return self.nc.alloc_semaphore(f"{self.stage}_{name}")


def pair_columns(ap, p, n=1):
    return ap[:, :, ds(p * 2 * T, 2 * T * n)].rearrange("q c (i t) -> q c i t", t=T)


def tokens_stage(nc, d, ps, h_all, zT, ident):
    with Mem(nc, "tokens") as m:
        w = m.sb("tok_w", [P, DC, E])
        xt = m.sb("tok_x", [P, 2, DC, P])
        pos, bias = m.sb("tok_pos", [P, E]), m.sb("tok_bias", [P, E])
        gamma, beta = m.sb("tok_gamma", [P, E]), m.sb("tok_beta", [P, E])
        add = m.sb("tok_add", [P, E])
        stats = m.sb("tok_stats", [P, PAIRS, 6])
        mv = m.sb("tok_mv", [P, 2, PAIRS, 2])
        ve, sd, rs = m.sb("tok_ve", [P, 2, PAIRS]), m.sb("tok_sd", [P, 2, PAIRS]), m.sb("tok_rs", [P, 2, PAIRS])
        z = m.sb("tok_z", [P, 2, E])
        w_in, tab_in = m.sem("w_in"), m.sem("tab_in")
        x_in = [m.sem("x_in0"), m.sem("x_in1")]
        add_ready, proj_done, h_ready, stats_ready, mv_ready = (m.sem(n) for n in (
            "add_ready", "proj_done", "h_ready", "stats_ready", "mv_ready"))
        ve_ready, sd_ready, rs_ready = m.sem("ve_ready"), m.sem("sd_ready"), m.sem("rs_ready")
        n_ready, g_ready, h0_ready = m.sem("n_ready"), m.sem("g_ready"), m.sem("h0_ready")
        stats2_ready, mv2_ready = m.sem("stats2_ready"), m.sem("mv2_ready")
        z_ready, zt_done, zt_out = m.sem("z_ready"), m.sem("zt_done"), m.sem("zt_out")
        block = m.stack.enter_context(nc.Block())

        @block.sync
        def _(sp):
            sp.dma_start(w[:], d["tok_W"]).then_inc(w_in, 16)
            for s in range(2):
                sp.dma_start(xt[:, s], d["xT"][s]).then_inc(x_in[s], 16)
            for t, src in ((pos, "t_pos"), (bias, "t_bias"), (gamma, "t_gamma"), (beta, "t_beta")):
                sp.dma_start(t[:], d[src]).then_inc(tab_in, 16)
            sp.dma_start(ident[:], d["ident"]).then_inc(tab_in, 16)
            with sp.Fori(0, PAIRS // 2 - 1) as i:
                for s in range(2):
                    sp.wait_ge(proj_done, 2 * i + s + 1)
                    sp.dma_start(xt[:, s], d["xT"][ds(2 * i + s + 2, 1)].rearrange("a p c n -> (a p) c n")
                                 ).then_inc(x_in[s], 16)

        @block.tensor
        def _(pe):
            def project(i, s, first):
                pe.wait_ge(x_in[s], 16 * i + 16)
                if not first:
                    pe.wait_ge(h_ready, 2 * i + s - 1)
                for c in range(DC):
                    mm = pe.matmul(ps[:, s, 0:E], xt[:, s, c, :], w[:, c, :], start=(c == 0), stop=(c == DC - 1))
                mm.then_inc(proj_done, 1)

            pe.wait_ge(w_in, 16)
            for s in range(2):
                project(0, s, True)
            with pe.Fori(1, PAIRS // 2) as i:
                for s in range(2):
                    project(i, s, False)
            pe.wait_ge(tab_in, 80)

            def turn(i, s, first):
                pe.wait_ge(z_ready, 2 * i + s + 1)
                if not first:
                    pe.wait_ge(zt_out, 2 * i + s - 1)
                for c in range(EC):
                    mm = pe.transpose(ps[:, 2 + s, c * P:(c + 1) * P], z[:, s, c * P:(c + 1) * P], ident[:])
                mm.then_inc(zt_done, 1)

            for s in range(2):
                turn(0, s, True)
            with pe.Fori(1, PAIRS // 2) as i:
                for s in range(2):
                    turn(i, s, False)

        @block.vector
        def _(dve):
            dve.wait_ge(tab_in, 80)
            dve.tensor_tensor(add[:], pos[:], bias[:], ALU.add).then_inc(add_ready, 1)
            dve.wait_ge(add_ready, 1)
            with dve.Fori(0, PAIRS // 2) as i:
                for s in range(2):
                    p = 2 * i + s
                    dve.wait_ge(proj_done, p + 1)
                    h = h_all[:, ds(p, 1), :].rearrange("q a e -> q (a e)")
                    dve.tensor_tensor(h, ps[:, s, 0:E], add[:], ALU.add).then_inc(h_ready, 1)
                    dve.wait_ge(h_ready, p + 1)
                    st = stats[:, ds(p, 1), :].rearrange("q a e -> q (a e)")
                    dve.bn_stats(st, h).then_inc(stats_ready, 1)

            def inverse_deviation(k, st_ready, ready):
                dve.wait_ge(st_ready, PAIRS)
                for p in range(PAIRS):
                    dve.bn_aggr(mv[:, k, p], stats[:, p]).then_inc(ready, 1)
                dve.wait_ge(ready, PAIRS)
                dve.tensor_scalar(ve[:, k], mv[:, k, :, 1], EPS_LN, None, ALU.add).then_inc(ve_ready, 1)
                dve.wait_ge(sd_ready, k + 1)
                dve.reciprocal(rs[:, k], sd[:, k]).then_inc(rs_ready, 1)
                dve.wait_ge(rs_ready, k + 1)

            inverse_deviation(0, stats_ready, mv_ready)
            with dve.Fori(0, PAIRS) as p:
                h = h_all[:, ds(p, 1), :].rearrange("q a e -> q (a e)")
                dve.tensor_scalar(h, h, mv[:, 0, ds(p, 1), 0], rs[:, 0, ds(p, 1)],
                                  ALU.subtract, ALU.mult).then_inc(n_ready, 1)
                dve.wait_ge(n_ready, p + 1)
                dve.tensor_tensor(h, h, gamma[:], ALU.mult).then_inc(g_ready, 1)
                dve.wait_ge(g_ready, p + 1)
                dve.tensor_tensor(h, h, beta[:], ALU.add).then_inc(h0_ready, 1)
                dve.wait_ge(h0_ready, p + 1)
                st = stats[:, ds(p, 1), :].rearrange("q a e -> q (a e)")
                dve.bn_stats(st, h).then_inc(stats2_ready, 1)
            inverse_deviation(1, stats2_ready, mv2_ready)

            def normalised(i, s, first):
                p = 2 * i + s
                if not first:
                    dve.wait_ge(zt_done, 2 * i + s - 1)
                h = h_all[:, ds(p, 1), :].rearrange("q a e -> q (a e)")
                dve.tensor_scalar(z[:, s], h, mv[:, 1, ds(p, 1), 0], rs[:, 1, ds(p, 1)],
                                  ALU.subtract, ALU.mult).then_inc(z_ready, 1)

            for s in range(2):
                normalised(0, s, True)
            with dve.Fori(1, PAIRS // 2) as i:
                for s in range(2):
                    normalised(i, s, False)

        @block.scalar
        def _(act):
            for k in range(2):
                act.wait_ge(ve_ready, k + 1)
                act.activation(sd[:, k], ve[:, k], ACT.Sqrt).then_inc(sd_ready, 1)
            with act.Fori(0, PAIRS // 2) as i:
                for s in range(2):
                    p = 2 * i + s
                    act.wait_ge(zt_done, p + 1)
                    src = ps[:, 2 + s, 0:E].rearrange("q (c i t) -> q c i t", c=EC, i=2)
                    for c in range(EC):
                        cp = act.activation(pair_columns(zT, p)[:, c], src[:, c, :, 0:T], ACT.Copy)
                    cp.then_inc(zt_out, 1)


def projections_stage(nc, d, ps, zT, kn, qn, v_rows):
    TILES = -(-TOKENS // P)
    NV = 2 * E
    with Mem(nc, "projections") as m:
        wi, wk, wq = (m.sb(n, [P, EC, E]) for n in ("w_in_t", "w_k_t", "w_q_t"))
        wvb = m.sb("w_vb_t", [P, EC, NV])
        bb = m.sb("b_beta_rows", [P, E])
        ones = m.sb("block_ones", [P, P])
        half = m.sb("tanh_half", [P, 2, CHUNK])
        xpT = m.sb("xpT", [P, EC, TOKENS])
        kT, qT = m.sb("kT", [P, EC, TOKENS]), m.sb("qT", [P, EC, TOKENS])
        sq = m.sb("k_squares", [P, 2, CHUNK])
        nrm = m.sb("k_norm", [P, EC, TOKENS])
        vb = m.sb("vb", [P, 2, NV])
        rest = m.sb("vb_rest", [P, 2, NV])
        parts = m.sb("vb_parts", [P, 2, PARTS, NV], BF16)
        (wts_in, mm_done, th_ready, xp2_ready, xp_ready, k_done, q_done, sq_ready, n2_done, n_ready, e_ready, r_ready,
         k_ready, kc_ready, qc_ready, turned, vb_done, bx_ready, bt_ready, b_ready, v_ready, p0_ready, r1_ready,
         p1_ready, p2_ready) = (m.sem(n) for n in (
            "wts_in", "mm_done", "th_ready", "xp2_ready", "xp_ready", "k_done", "q_done", "sq_ready", "n2_done",
            "n_ready", "e_ready", "r_ready", "k_ready", "kc_ready", "qc_ready", "turned", "vb_done", "bx_ready",
            "bt_ready", "b_ready", "v_ready", "p0_ready", "r1_ready", "p1_ready", "p2_ready"))
        rows_out = [m.sem("rows_out0"), m.sem("rows_out1")]
        block = m.stack.enter_context(nc.Block())
        cells = [(n, c) for n in range(B4) for c in range(EC)]

        def cols(n):
            return slice(n * CHUNK, (n + 1) * CHUNK)

        @block.sync
        def _(sp):
            for t, src in ((wi, "W_in"), (wk, "W_k"), (wq, "W_q"), (wvb, "W_vb"), (bb, "b_beta"), (ones, "block_ones")):
                sp.dma_start(t[:], d[src]).then_inc(wts_in, 16)
            for h4 in range(B4):
                for b4 in range(B4):
                    if h4 == 0 and b4 == 0:
                        sp.wait_ge(qc_ready, len(cells))
                    sp.dma_start(qn[32 * b4:32 * b4 + 32, h4::B4, :], qT[32 * h4:32 * h4 + 32, :, cols(b4)]
                                 ).then_inc(turned, 16)
            sp.wait_ge(k_ready, 1)
            for h4 in range(B4):
                for b4 in range(B4):
                    sp.dma_start(kn[32 * b4:32 * b4 + 32, h4::B4, :], kT[32 * h4:32 * h4 + 32, :, cols(b4)]
                                 ).then_inc(turned, 16)
            for i in range(TILES):
                rows = min(P, TOKENS - i * P)
                sp.wait_ge(p2_ready, i + 1)
                sp.dma_start(v_rows[i * P:i * P + rows, :], parts[0:rows, i % 2].rearrange("p a n -> p (a n)")
                             ).then_inc(rows_out[i % 2], 16)
            sp.wait_ge(turned, 16 * 2 * B4 * B4)
            sp.wait_ge(rows_out[0], 16 * ((TILES + 1) // 2))
            sp.wait_ge(rows_out[1], 16 * (TILES // 2))

        @block.tensor
        def _(pe):
            pe.wait_ge(wts_in, 96)

            def product(w, src, bank, n, c):
                for k in range(EC):
                    mm = pe.matmul(ps[:, bank, 0:CHUNK], w[:, k, c * P:(c + 1) * P], src[:, k, cols(n)],
                                   start=(k == 0), stop=(k == EC - 1))
                return mm

            for j, (n, c) in enumerate(cells):
                if j >= 2:
                    pe.wait_ge(xp2_ready, j - 1)
                product(wi, zT, j % 2, n, c).then_inc(mm_done, 1)
            for j, (n, c) in enumerate(cells):
                pe.wait_ge(xp_ready, 1)
                if j >= 2:
                    pe.wait_ge(qc_ready, j - 1)
                product(wq, xpT, 2 + j % 2, n, c).then_inc(q_done, 1)
            for j, (n, c) in enumerate(cells):
                if j >= 2:
                    pe.wait_ge(kc_ready, j - 1)
                product(wk, xpT, 4 + j % 2, n, c).then_inc(k_done, 1)
                pe.wait_ge(sq_ready, j + 1)
                if j >= 2:
                    pe.wait_ge(n_ready, j - 1)
                pe.matmul(ps[:, 6 + j % 2, 0:CHUNK], ones[:], sq[:, j % 2, :], start=True, stop=True
                          ).then_inc(n2_done, 1)
            for i in range(TILES):
                rows = min(P, TOKENS - i * P)
                if i < 2:
                    pe.wait_ge(xp2_ready, len(cells))
                else:
                    pe.wait_ge(bx_ready, i - 1)
                    pe.wait_ge(v_ready, i - 1)
                for k in range(EC):
                    mm = pe.matmul(ps[0:rows, i % 2, :], xpT[:, k, i * P:i * P + rows], wvb[:, k, :],
                                   start=(k == 0), stop=(k == EC - 1))
                mm.then_inc(vb_done, 1)

        @block.scalar
        def _(act):
            def root(j):
                n, c = cells[j]
                act.wait_ge(n2_done, j + 1)
                act.activation(nrm[:, c, cols(n)], ps[:, 6 + j % 2, 0:CHUNK], ACT.Sqrt).then_inc(n_ready, 1)

            for j, (n, c) in enumerate(cells):
                act.wait_ge(mm_done, j + 1)
                if j >= 2:
                    act.wait_ge(xp2_ready, j - 1)
                act.activation(half[:, j % 2], ps[:, j % 2, 0:CHUNK], ACT.Tanh, scale=0.5).then_inc(th_ready, 1)
            for j, (n, c) in enumerate(cells):
                act.wait_ge(q_done, j + 1)
                act.activation(qT[:, c, cols(n)], ps[:, 2 + j % 2, 0:CHUNK], ACT.Copy).then_inc(qc_ready, 1)
            for j, (n, c) in enumerate(cells):
                act.wait_ge(k_done, j + 1)
                if j >= 2:
                    act.wait_ge(n2_done, j - 1)
                act.activation(sq[:, j % 2], ps[:, 4 + j % 2, 0:CHUNK], ACT.Square).then_inc(sq_ready, 1)
                act.activation(kT[:, c, cols(n)], ps[:, 4 + j % 2, 0:CHUNK], ACT.Copy).then_inc(kc_ready, 1)
                if j >= 1:
                    root(j - 1)
            root(len(cells) - 1)
            for i in range(TILES):
                rows = min(P, TOKENS - i * P)
                s = i % 2
                act.wait_ge(bx_ready, i + 1)
                act.activation(vb[0:rows, s, E:], vb[0:rows, s, E:], ACT.Tanh, scale=0.5).then_inc(bt_ready, 1)
                act.wait_ge(b_ready, i + 1)
                act.wait_ge(v_ready, i + 1)
                if i >= 2:
                    act.wait_ge(rows_out[s], 16 * (i // 2))
                act.activation(parts[0:rows, s, 0], vb[0:rows, s], ACT.Copy).then_inc(p0_ready, 1)
                act.wait_ge(r1_ready, i + 1)
                act.activation(parts[0:rows, s, 1], rest[0:rows, s], ACT.Copy).then_inc(p1_ready, 1)

        @block.vector
        def _(dve):
            for j, (n, c) in enumerate(cells):
                dve.wait_ge(th_ready, j + 1)
                dve.scalar_tensor_tensor(out=xpT[:, c, cols(n)], in0=half[:, j % 2], scalar=1.0,
                                         in1=ps[:, j % 2, 0:CHUNK], op0=ALU.add, op1=ALU.mult).then_inc(xp2_ready, 1)
            dve.wait_ge(xp2_ready, len(cells))
            dve.tensor_scalar(xpT[:], xpT[:], 0.5, None, ALU.mult).then_inc(xp_ready, 1)
            dve.wait_ge(n_ready, len(cells))
            dve.tensor_scalar(nrm[:], nrm[:], 1e-6, None, ALU.add).then_inc(e_ready, 1)
            dve.wait_ge(e_ready, 1)
            dve.reciprocal(nrm[:], nrm[:]).then_inc(r_ready, 1)
            dve.wait_ge(r_ready, 1)
            dve.wait_ge(kc_ready, len(cells))
            dve.tensor_tensor(kT[:], kT[:], nrm[:], ALU.mult).then_inc(k_ready, 1)
            for i in range(TILES):
                rows = min(P, TOKENS - i * P)
                s = i % 2
                dve.wait_ge(vb_done, i + 1)
                if i >= 2:
                    dve.wait_ge(p0_ready, i - 1)
                dve.tensor_tensor(vb[0:rows, s, E:], ps[0:rows, s, E:], bb[0:rows], ALU.add).then_inc(bx_ready, 1)
                dve.tensor_copy(vb[0:rows, s, 0:E], ps[0:rows, s, 0:E]).then_inc(v_ready, 1)
                dve.wait_ge(bt_ready, i + 1)
                dve.tensor_scalar(vb[0:rows, s, E:], vb[0:rows, s, E:], 0.5, 0.5, ALU.mult, ALU.add).then_inc(b_ready, 1)
                dve.wait_ge(p0_ready, i + 1)
                dve.tensor_tensor(rest[0:rows, s], vb[0:rows, s], parts[0:rows, s, 0], ALU.subtract).then_inc(r1_ready, 1)
                dve.wait_ge(p1_ready, i + 1)
                dve.tensor_tensor(parts[0:rows, s, 2], rest[0:rows, s], parts[0:rows, s, 1], ALU.subtract
                                  ).then_inc(p2_ready, 1)


def scan_stage(nc, d, ps, kn, qn, v_rows, o_rows):
    HALF = B8 // 2
    N = HALF * E
    LAST = T - 1
    with Mem(nc, "scan") as m:
        S = [m.sb(f"state{a}", [P, N]) for a in range(2)]
        Pb = [m.sb(f"s_times_kn{a}", [P, N]) for a in range(2)]
        Qb = [m.sb(f"s_times_q{a}", [P, N]) for a in range(2)]
        Tb = [m.sb(f"beta_s{a}", [P, N]) for a in range(2)]
        bsb = [m.sb(f"beta_sb{a}", [P, N]) for a in range(2)]
        vrow = m.sb("v_row", [P, 2, B8, 2, E], BF16)
        obuf = m.sb("o_buf", [16, 2, 2, E])
        sel = m.sb("part_rows_to_block", [P, P], BF16)
        neg = m.sb("minus_block_ones", [P, P])
        osel = m.sb("block_sum_to_row", [P, 4, P])
        p_ready, r_done, u_ready, a_ready, s_ready, q_ready, o_done, t_ready = (
            [m.sem(f"{n}{a}") for a in range(2)] for n in (
                "p_ready", "r_done", "u_ready", "a_ready", "s_ready", "q_ready", "o_done", "t_ready"))
        beta_done, beta_ready, v1_done, o_out = (m.sem(n) for n in ("beta_done", "beta_ready", "v1_done", "o_out"))
        row_in, stored = ([m.sem(f"{n}{s}") for s in range(2)] for n in ("row_in", "stored"))
        zeroed, row_zeroed, const_in = m.sem("zeroed"), m.sem("row_zeroed"), m.sem("const_in")
        block = m.stack.enter_context(nc.Block())

        def st(ap):
            return ap.rearrange("q (b h i) -> q b h i", b=HALF, h=NH_CELL)

        def vec(ap, t, a):
            v = ap[:].rearrange("q h (b t) -> q b h t", t=T)[:, HALF * a:HALF * a + HALF, :, ds(t, 1)]
            return v.broadcast_to([P, HALF, NH_CELL, NCELL])

        def D(a):
            return ps[:, 2 * a:2 * a + 2, :].rearrange("q n (b h i) -> q (n b) h i", h=NH_CELL, i=NCELL)

        def cycles(eng, cycle, first=4, last=LAST + 1):
            for c in range(first):
                cycle(c, c % 2)
            with eng.Fori(first // 2, LAST // 2) as i:
                for s in range(2):
                    cycle(2 * i + s, s, i)
            for c in range(2 * (LAST // 2), last + 1):
                cycle(c, c % 2)

        @block.sync
        def _(sp):
            for t, src in ((sel, "part_rows_to_block"), (neg, "minus_block_ones"), (osel, "block_sum_to_row")):
                sp.dma_start(t[:], d[src]).then_inc(const_in, 16)
            rows = v_rows.rearrange("(g b t) (a n) -> a g b t n", g=B4, t=T, a=PARTS)

            def load(t, s):
                for a in range(PARTS):
                    sp.dma_start(vrow[B4 * a:B4 * a + B4, s].rearrange("q b k m -> q b (k m)"),
                                 rows[a][:, :, ds(t, 1), :].rearrange("g b t n -> g b (t n)")).then_inc(row_in[s], 16)

            def store(t, s):
                for k in range(4):
                    sp.dma_start(o_rows.rearrange("(g k b) t n -> k g b t n", g=B4, k=4)[k][:, :, ds(t, 1), :]
                                 .rearrange("g b t n -> g b (t n)"), obuf[4 * k:4 * k + 4, s]).then_inc(stored[s], 16)

            sp.wait_ge(row_zeroed, 1)
            load(0, 0)
            load(1, 1)

            def cycle(c, s, i=None):
                if i is not None or c >= 2:
                    sp.wait_ge(o_out, c - 1)
                    store(c - 2, s)
                if i is not None or c + 2 <= LAST:
                    sp.wait_ge(v1_done, c + 1)
                    load(c + 2, s)

            cycles(sp, cycle, last=LAST + 2)
            for s in range(2):
                sp.wait_ge(stored[s], 16 * 4 * (T // 2))

        @block.gpsimd
        def _(pool):
            def cycle(c, s, i=None):
                for a in range(2):
                    pool.wait_ge(beta_ready, 2 * c + 1 + a)
                    if i is None and c == 0:
                        pool.wait_ge(zeroed, 2)
                    else:
                        pool.wait_ge(s_ready[a], c)
                    pool.tensor_tensor(Tb[a][:], bsb[a][:], S[a][:], ALU.mult).then_inc(t_ready[a], 1)

            cycles(pool, cycle, last=LAST)

        @block.scalar
        def _(act):
            def beta_copy(a, c, first):
                act.wait_ge(beta_done, 2 * c + 1 + a)
                if not first:
                    act.wait_ge(t_ready[a], c)
                act.activation(bsb[a][:], ps[:, 4:6, :].rearrange("q n x -> q (n x)"), ACT.Copy).then_inc(beta_ready, 1)

            def tanh(a, n):
                act.wait_ge(a_ready[a], n)
                act.activation(S[a][:], Tb[a][:], ACT.Tanh).then_inc(s_ready[a], 1)

            def cycle(c, s, i=None):
                if i is not None or c >= 2:
                    act.wait_ge(o_done[1], c - 1)
                    if i is not None or c >= 4:
                        stores = (c // 2 if i is None else i) - 1
                        act.wait_ge(stored[s], 64 * stores)
                    act.activation(obuf[:, s].rearrange("q b m -> q (b m)"), ps[0:16, 6 + s, :], ACT.Copy
                                   ).then_inc(o_out, 1)
                if i is not None or 1 <= c <= LAST + 1:
                    tanh(1, c)
                if i is not None or c <= LAST:
                    beta_copy(1, c, i is None and c == 0)
                    tanh(0, c + 1)
                if i is not None or c < LAST:
                    beta_copy(0, c + 1, False)

            beta_copy(0, 0, True)
            cycles(act, cycle, last=LAST + 2)

        @block.vector
        def _(dve):
            for s in range(2):
                ms = dve.memset(vrow[:, s].rearrange("q b k m -> q (b k m)"), 0.0)
            ms.then_inc(row_zeroed, 1)
            for a in range(2):
                dve.memset(S[a][:], 0.0).then_inc(zeroed, 1)
            dve.wait_ge(zeroed, 2)

            def s_kn(a, c, first):
                if not first:
                    dve.wait_ge(s_ready[a], c)
                dve.tensor_tensor(st(Pb[a][:]), st(S[a][:]), vec(kn, c, a), ALU.mult).then_inc(p_ready[a], 1)

            def s_q(a, t, first):
                dve.wait_ge(s_ready[a], t + 1)
                if not first:
                    dve.wait_ge(o_done[a], t)
                dve.tensor_tensor(st(Qb[a][:]), st(S[a][:]), vec(qn, t, a), ALU.mult).then_inc(q_ready[a], 1)

            def update(a, t):
                dve.wait_ge(r_done[a], t + 1)
                dve.tensor_tensor(D(a), D(a), vec(kn, t, a), ALU.mult).then_inc(u_ready[a], 1)
                dve.wait_ge(u_ready[a], t + 1)
                dve.wait_ge(t_ready[a], t + 1)
                dve.tensor_tensor(Tb[a][:], ps[:, 2 * a:2 * a + 2, :].rearrange("q n x -> q (n x)"), Tb[a][:],
                                  ALU.add).then_inc(a_ready[a], 1)

            def cycle(c, s, i=None):
                front, back = i is not None or c <= LAST, i is not None or c >= 1
                if front:
                    s_kn(0, c, i is None and c == 0)
                if back:
                    s_q(0, c - 1, i is None and c == 1)
                    update(1, c - 1)
                if front:
                    update(0, c)
                    s_kn(1, c, i is None and c == 0)
                if back:
                    s_q(1, c - 1, i is None and c == 1)

            cycles(dve, cycle)

        @block.tensor
        def _(pe):
            pe.wait_ge(const_in, 48)

            def rows(kind, a, s, bank, more):
                for n in range(2):
                    b = HALF * a + 2 * n
                    mm = pe.matmul(ps[:, bank + n, :].rearrange("q (b m) -> q b m", b=2), sel[:],
                                   vrow[:, s, b:b + 2, kind, :], start=True, stop=not more)
                return mm

            def sums(a):
                for n in range(2):
                    mm = pe.matmul(ps[:, 2 * a + n, :], neg[:], Pb[a][:, 512 * n:512 * n + 512], start=False, stop=True)
                mm.then_inc(r_done[a], 1)

            def outs(a, s):
                for n in range(2):
                    k = 2 * a + n
                    mm = pe.matmul(ps[:, 6 + s, :], osel[:, k, :], Qb[a][:, 512 * n:512 * n + 512],
                                   start=(k == 0), stop=(k == 3))
                mm.then_inc(o_done[a], 1)

            def cycle(c, s, i=None):
                front, back = i is not None or c <= LAST, i is not None or c >= 1
                if front:
                    pe.wait_ge(p_ready[0], c + 1)
                    sums(0)
                    pe.wait_ge(beta_ready, 2 * c + 1)
                    rows(1, 1, s, 4, False).then_inc(beta_done, 1)
                if back:
                    pe.wait_ge(q_ready[0], c)
                    if i is not None or c >= 3:
                        pe.wait_ge(o_out, c - 2)
                    outs(0, 1 - s)
                if front:
                    if back:
                        pe.wait_ge(a_ready[1], c)
                    rows(0, 1, s, 2, True).then_inc(v1_done, 1)
                if i is not None or c < LAST:
                    passes = (c + 1) // 2 if i is None else i + s
                    pe.wait_ge(row_in[1 - s], 48 * passes + 48)
                    pe.wait_ge(a_ready[0], c + 1)
                    rows(0, 0, 1 - s, 0, True)
                    pe.wait_ge(beta_ready, 2 * c + 2)
                    rows(1, 0, 1 - s, 4, False).then_inc(beta_done, 1)
                if front:
                    pe.wait_ge(p_ready[1], c + 1)
                    sums(1)
                if back:
                    pe.wait_ge(q_ready[1], c)
                    outs(1, 1 - s)

            pe.wait_ge(row_in[0], 48)
            rows(1, 0, 0, 4, False).then_inc(beta_done, 1)
            rows(0, 0, 0, 0, True)
            cycles(pe, cycle)


def row(ap, p):
    return ap[:, ds(p, 1), :].rearrange("q a e -> q (a e)")


def ring(eng, step, count=PAIRS):
    for s in range(2):
        step(s, s, True)
    with eng.Fori(1, count // 2) as i:
        for s in range(2):
            step(2 * i + s, s, False)


def cell_output_stage(nc, d, ps, o_pad, h_all, xh_all, xnT, ident, wd, w_late, x_slots):
    with Mem(nc, "cell_output") as m:
        wo = m.sb("w_out_t", [P, EC, E])
        g1 = m.sb("g1_cols", [P, EC])
        o = m.sb("o_tile", [P, 2, E])
        th, a = m.sb("o_tanh", [P, 2, E]), m.sb("o_gate", [P, 2, E])
        cell = m.sb("cell", [P, 2, E])
        cellT = m.sb("cellT", [P, 2, E])
        stats = m.sb("h1_stats", [P, PAIRS, 6])
        mv = m.sb("h1_mv", [P, PAIRS, 2])
        ve, sd, rs = m.sb("h1_ve", [P, PAIRS]), m.sb("h1_sd", [P, PAIRS]), m.sb("h1_rs", [P, PAIRS])
        ss, ms, rm, rr = (m.sb(n, [P, PAIRS]) for n in ("xh_ss", "xh_ms", "xh_rms", "xh_rrms"))
        junk = m.sb("xh_squares", [P, E])
        zero = m.sb("empty_slot", [P, E])
        zero_ready, emptied = m.sem("zero_ready"), m.sem("emptied")
        xn = m.sb("xn", [P, 2, E])
        (w_in, zeroed, th_ready, a_ready, c_ready, ct_done, ct_out, y_done, h_ready, st_ready, mv_ready, ve_ready,
         sd_ready, rs_ready, xh_ready, ss_ready, ms_ready, rm_ready, rr_ready, xn_ready, xt_done, xt_out) = (
            m.sem(n) for n in ("w_in", "zeroed", "th_ready", "a_ready", "c_ready", "ct_done", "ct_out", "y_done",
                               "h_ready", "st_ready", "mv_ready", "ve_ready", "sd_ready", "rs_ready", "xh_ready",
                               "ss_ready", "ms_ready", "rm_ready", "rr_ready", "xn_ready", "xt_done", "xt_out"))
        o_in = [m.sem("o_in0"), m.sem("o_in1")]
        block = m.stack.enter_context(nc.Block())

        @block.sync
        def _(sp):
            sp.dma_start(wo[:], d["W_out"]).then_inc(w_in, 16)
            sp.dma_start(g1[:], d["g1"]).then_inc(w_in, 16)
            sp.wait_ge(zeroed, 1)

            def load(p, s, first):
                if not first:
                    sp.wait_ge(c_ready, p - 1)
                for k in range(2):
                    sp.dma_start(o[SLOT * k:SLOT * k + T, s], o_pad[ds(2 * p + k, 1)].rearrange("a t m -> (a t) m")
                                 ).then_inc(o_in[s], 16)

            ring(sp, load)
            sp.dma_start(wd[:], d["wd"]).then_inc(w_late, 16)
            sp.wait_ge(zero_ready, 1)
            sp.dma_start(x_slots.rearrange("(n q) e -> q n e", q=P),
                         zero[:].rearrange("q (a e) -> q a e", a=1).broadcast_to([P, TILES, E])).then_inc(emptied, 16)
            sp.wait_ge(emptied, 16)

        @block.scalar
        def _(act):
            def gate(p, s, first):
                act.wait_ge(o_in[s], 32 * (p // 2) + 32 if first else 16 * (p - s) + 32)
                if not first:
                    act.wait_ge(a_ready, p - 1)
                act.activation(th[:, s], o[:, s], ACT.Tanh, scale=0.5).then_inc(th_ready, 1)
                act.wait_ge(ct_done, p + 1)
                if not first:
                    act.wait_ge(y_done, p - 1)
                act.activation(cellT[:, s], ps[:, s, 0:E], ACT.Copy).then_inc(ct_out, 1)

            ring(act, gate)
            act.wait_ge(ve_ready, 1)
            act.activation(sd[:], ve[:], ACT.Sqrt).then_inc(sd_ready, 1)

            def squares(p):
                act.wait_ge(xh_ready, p + 1)
                act.activation(junk[:], row(xh_all, p), ACT.Square, accum_out=ss[:, ds(p, 1)]).then_inc(ss_ready, 1)

            squares(0)
            with act.Fori(1, PAIRS) as p:
                act.wait_ge(ss_ready, p)
                squares(p)
            act.wait_ge(ms_ready, 1)
            act.activation(rm[:], ms[:], ACT.Sqrt).then_inc(rm_ready, 1)
            with act.Fori(0, PAIRS // 2) as i:
                for s in range(2):
                    act.wait_ge(xt_done, 2 * i + s + 1)
                    for c in range(EC):
                        cp = act.activation(xnT[:, c, ds((2 * i + s) * P, P)], ps[:, 4 + s, c * P:(c + 1) * P],
                                            ACT.Copy, scale=g1[:, c:c + 1])
                    cp.then_inc(xt_out, 1)

        @block.tensor
        def _(pe):
            pe.wait_ge(w_in, 32)

            def turn(p, s, first):
                pe.wait_ge(c_ready, p + 1)
                if not first:
                    pe.wait_ge(ct_out, p - 1)
                for c in range(EC):
                    mm = pe.transpose(ps[:, s, c * P:(c + 1) * P], cell[:, s, c * P:(c + 1) * P], ident[:])
                mm.then_inc(ct_done, 1)
                pe.wait_ge(ct_out, p + 1)
                if not first:
                    pe.wait_ge(h_ready, p - 1)
                for c in range(EC):
                    mm = pe.matmul(ps[:, 2 + s, 0:E], cellT[:, s, c * P:(c + 1) * P], wo[:, c, :],
                                   start=(c == 0), stop=(c == EC - 1))
                mm.then_inc(y_done, 1)

            ring(pe, turn)

            def turn_xn(p, s, first):
                pe.wait_ge(xn_ready, p + 1)
                if not first:
                    pe.wait_ge(xt_out, p - 1)
                for c in range(EC):
                    mm = pe.transpose(ps[:, 4 + s, c * P:(c + 1) * P], xn[:, s, c * P:(c + 1) * P], ident[:])
                mm.then_inc(xt_done, 1)

            ring(pe, turn_xn)

        @block.vector
        def _(dve):
            dve.memset(o[:].rearrange("q a e -> q (a e)"), 0.0).then_inc(zeroed, 1)
            dve.memset(zero[:], 0.0).then_inc(zero_ready, 1)

            def front(p, s, first):
                dve.wait_ge(th_ready, p + 1)
                dve.scalar_tensor_tensor(out=a[:, s], in0=th[:, s], scalar=1.0, in1=o[:, s], op0=ALU.add, op1=ALU.mult
                                         ).then_inc(a_ready, 1)
                dve.wait_ge(a_ready, p + 1)
                if not first:
                    dve.wait_ge(ct_done, p - 1)
                dve.scalar_tensor_tensor(out=cell[:, s], in0=a[:, s], scalar=0.5, in1=o[:, s], op0=ALU.mult,
                                         op1=ALU.mult).then_inc(c_ready, 1)

            def back(p, s):
                dve.wait_ge(y_done, p + 1)
                dve.tensor_tensor(row(h_all, p), ps[:, 2 + s, 0:E], row(h_all, p), ALU.add).then_inc(h_ready, 1)
                dve.wait_ge(h_ready, p + 1)
                dve.bn_stats(row(stats, p), row(h_all, p)).then_inc(st_ready, 1)

            front(0, 0, True)
            front(1, 1, True)
            back(0, 0)
            with dve.Fori(1, PAIRS // 2) as i:
                front(2 * i, 0, False)
                back(2 * i - 1, 1)
                front(2 * i + 1, 1, False)
                back(2 * i, 0)
            back(PAIRS - 1, 1)
            dve.wait_ge(st_ready, PAIRS)
            for p in range(PAIRS):
                dve.bn_aggr(mv[:, p], stats[:, p]).then_inc(mv_ready, 1)
            dve.wait_ge(mv_ready, PAIRS)
            dve.tensor_scalar(ve[:], mv[:, :, 1], EPS_LN, None, ALU.add).then_inc(ve_ready, 1)
            dve.wait_ge(sd_ready, 1)
            dve.reciprocal(rs[:], sd[:]).then_inc(rs_ready, 1)
            dve.wait_ge(rs_ready, 1)
            with dve.Fori(0, PAIRS) as p:
                dve.tensor_scalar(row(xh_all, p), row(h_all, p), mv[:, ds(p, 1), 0], rs[:, ds(p, 1)],
                                  ALU.subtract, ALU.mult).then_inc(xh_ready, 1)
            dve.wait_ge(ss_ready, PAIRS)
            dve.tensor_scalar(ms[:], ss[:], 1.0 / E, EPS_RMS, ALU.mult, ALU.add).then_inc(ms_ready, 1)
            dve.wait_ge(rm_ready, 1)
            dve.reciprocal(rr[:], rm[:]).then_inc(rr_ready, 1)
            dve.wait_ge(rr_ready, 1)
            dve.wait_ge(xh_ready, PAIRS)

            def scaled(p, s, first):
                if not first:
                    dve.wait_ge(xt_done, p - 1)
                dve.tensor_scalar(xn[:, s], row(xh_all, p), rr[:, ds(p, 1)], None, ALU.mult).then_inc(xn_ready, 1)

            ring(dve, scaled)


def rotary_stage(nc, d, ps, xnT, qr, kr):
    NW = 512
    SLOTS = PAIRS * P // NW
    cells = [(n, c) for n in range(SLOTS) for c in range(EC)]
    with Mem(nc, "rotary") as m:
        w = m.sb("w_rope", [P, 4, EC, E])
        cos, sin = m.sb("cos", [P, SLOT]), m.sb("sin", [P, SLOT])
        t1, t2 = m.sb("rope_cos", [P, 2, 2, NW]), m.sb("rope_sin", [P, 2, 2, NW])
        w_in, mm_done, t1_ready, t2_ready, r_ready = (m.sem(n) for n in (
            "w_in", "mm_done", "t1_ready", "t2_ready", "r_ready"))
        block = m.stack.enter_context(nc.Block())

        @block.sync
        def _(sp):
            for k, src in enumerate(("wq", "wk", "wq_perm", "wk_perm")):
                sp.dma_start(w[:, k], d[src]).then_inc(w_in, 16)
            sp.dma_start(cos[:], d["cos"]).then_inc(w_in, 16)
            sp.dma_start(sin[:], d["sin"]).then_inc(w_in, 16)

        @block.tensor
        def _(pe):
            pe.wait_ge(w_in, 96)
            for j, (n, c) in enumerate(cells):
                if j >= 2:
                    pe.wait_ge(t2_ready, 2 * j - 2)
                for k in range(4):
                    for e in range(EC):
                        mm = pe.matmul(ps[:, 4 * (j % 2) + k, :], w[:, k, e, c * P:(c + 1) * P],
                                       xnT[:, e, n * NW:(n + 1) * NW], start=(e == 0), stop=(e == EC - 1))
                mm.then_inc(mm_done, 1)

        @block.vector
        def _(dve):
            dve.wait_ge(w_in, 96)

            def tab(t):
                return t[:].rearrange("q (a t) -> q a t", a=1).broadcast_to([P, NW // SLOT, SLOT])

            for j, (n, c) in enumerate(cells):
                dve.wait_ge(mm_done, j + 1)
                if j >= 2:
                    dve.wait_ge(r_ready, 2 * j - 2)
                for k in range(2):
                    for t, table, bank, ready in ((t1, cos, k, t1_ready), (t2, sin, 2 + k, t2_ready)):
                        dve.tensor_tensor(t[:, j % 2, k].rearrange("q (a t) -> q a t", t=SLOT),
                                          ps[:, 4 * (j % 2) + bank, :].rearrange("q (a t) -> q a t", t=SLOT),
                                          tab(table), ALU.mult).then_inc(ready, 1)

        @block.gpsimd
        def _(pool):
            for j, (n, c) in enumerate(cells):
                for k, dst in enumerate((qr, kr)):
                    pool.wait_ge(t1_ready, 2 * j + k + 1)
                    pool.wait_ge(t2_ready, 2 * j + k + 1)
                    pool.tensor_tensor(dst[:, c, n * NW:(n + 1) * NW], t1[:, j % 2, k], t2[:, j % 2, k], ALU.add
                                       ).then_inc(r_ready, 1)
            pool.wait_ge(r_ready, 2 * len(cells))


def attention_stage(nc, d, ps, xnT, qr, kr, h_all, xh_all, ss, ident):
    W = HG * T
    with Mem(nc, "attention") as m:
        wv, wo = m.sb("wv", [P, EC, E]), m.sb("wo", [P, EC, E])
        causal = m.sb("causal", [P, T])
        hmask = m.sb("head_mask", [P, HG])
        q = m.sb("q_pair", [P, 2, EC, P])
        x = m.sb("xn_pair", [P, 2, EC, 2, 2, SLOT])
        km = m.sb("k_masked", [P, 2, EC, 2, HG, T])
        v2 = m.sb("v_blocks", [P, 2, 2, HEADS // 2, 2, DH])
        sc = m.sb("scores", [P, 2, HEADS, T])
        pr = m.sb("probs", [P, 2, HEADS, SLOT])
        pt = m.sb("probs_t", [P, 2, HEADS // 2, P])
        mx, sm, ri = m.sb("max", [P, 2, HEADS]), m.sb("sum", [P, 2, HEADS]), m.sb("inv_sum", [P, 2, HEADS])
        at = m.sb("attn", [P, 2, E])
        atT = m.sb("attnT", [P, 2, E])
        junk = m.sb("hh_squares", [P, E])
        (c_in, zeroed, x_ready, q_ready, k_ready, v_done, v_out, s_done, sc_ready, mx_ready, sub_ready, p_ready,
         sum_ready, ri_ready, pt_done, pt_out, pv_done, at_ready, at_done, at_out, wo_done, hh_ready, r_ready,
         ss_ready) = (m.sem(n) for n in (
            "c_in", "zeroed", "x_ready", "q_ready", "k_ready", "v_done", "v_out", "s_done", "sc_ready", "mx_ready",
            "sub_ready", "p_ready", "sum_ready", "ri_ready", "pt_done", "pt_out", "pv_done", "at_ready", "at_done",
            "at_out", "wo_done", "hh_ready", "r_ready", "ss_ready"))
        block = m.stack.enter_context(nc.Block())
        PT, SC, VB, PV, AT, WO = 0, 2, 4, 5, 6, 7

        def cycles(eng, cycle):
            for c in range(4):
                cycle(c, c % 2, False)
            with eng.Fori(2, PAIRS // 2) as i:
                for s in range(2):
                    cycle(2 * i + s, s, True)
            cycle(PAIRS, 0, False)
            cycle(PAIRS + 1, 1, False)

        def has(c, loop, lag):
            return loop or 0 <= c - lag < PAIRS

        @block.sync
        def _(sp):
            for t, src in ((wv, "wv"), (wo, "wo"), (causal, "causal"), (hmask, "head_mask")):
                sp.dma_start(t[:], d[src]).then_inc(c_in, 16)

        @block.gpsimd
        def _(pool):
            pool.wait_ge(c_in, 64)

            def prepare(p, s, first):
                cols = ds(p * P, P)
                if not first:
                    pool.wait_ge(v_done, p - 1)
                for k in range(2):
                    cp = pool.tensor_copy(x[:, s, :, :, k, :], xnT[:, :, cols].rearrange("q c (i t) -> q c i t", i=2))
                cp.then_inc(x_ready, 1)
                if not first:
                    pool.wait_ge(s_done, p - 1)
                pool.tensor_copy(q[:, s], qr[:, :, cols]).then_inc(q_ready, 1)
                for c in range(EC):
                    for k in range(2):
                        keys = kr[:, c, ds(p * P + SLOT * k, T)].rearrange("q (a t) -> q a t", a=1)
                        mask = hmask[:].rearrange("q (h a) -> q h a", a=1)
                        mul = pool.tensor_tensor(km[:, s, c, k], keys.broadcast_to([P, HG, T]),
                                                 mask.broadcast_to([P, HG, T]), ALU.mult)
                mul.then_inc(k_ready, 1)

            ring(pool, prepare)

        @block.tensor
        def _(pe):
            pe.wait_ge(c_in, 64)

            def cycle(c, s, loop):
                if has(c, loop, 2):
                    pe.wait_ge(at_ready, c - 1)
                    if loop or c > 2:
                        pe.wait_ge(at_out, c - 2)
                    for e in range(EC):
                        mm = pe.transpose(ps[:, AT, e * P:(e + 1) * P], at[:, s, e * P:(e + 1) * P], ident[:])
                    mm.then_inc(at_done, 1)
                if has(c, loop, 1):
                    pe.wait_ge(p_ready, c)
                    if loop or c > 1:
                        pe.wait_ge(pt_out, c - 1)
                    for h in range(HEADS // 2):
                        mm = pe.transpose(ps[:, PT + h // 4, (h % 4) * P:(h % 4 + 1) * P],
                                          pr[:, 1 - s, 2 * h:2 * h + 2, :].rearrange("q h k -> q (h k)"), ident[:])
                    mm.then_inc(pt_done, 1)
                if has(c, loop, 0):
                    pe.wait_ge(x_ready, c + 1)
                    if loop or c > 0:
                        pe.wait_ge(v_out, c)
                    for k in range(2):
                        for e in range(EC):
                            mm = pe.matmul(ps[:, VB, k * E:(k + 1) * E], x[:, s, e, k].rearrange("q a t -> q (a t)"),
                                           wv[:, e, :], start=(e == 0), stop=(e == EC - 1))
                    mm.then_inc(v_done, 1)
                    pe.wait_ge(q_ready, c + 1)
                    pe.wait_ge(k_ready, c + 1)
                    if loop or c > 0:
                        pe.wait_ge(sc_ready, c)
                    for e in range(EC):
                        for k in range(2):
                            mm = pe.matmul(ps[SLOT * k:SLOT * k + SLOT, SC + e, 0:W], q[:, s, e, SLOT * k:SLOT * k + SLOT],
                                           km[:, s, e, k].rearrange("q h t -> q (h t)"), start=True, stop=True)
                    mm.then_inc(s_done, 1)
                if has(c, loop, 1):
                    pe.wait_ge(pt_out, c)
                    if loop or c > 1:
                        pe.wait_ge(at_ready, c - 1)
                    for k in range(2):
                        for h in range(HEADS // 2):
                            mm = pe.matmul(ps[SLOT * k:SLOT * k + SLOT, PV, 32 * h:32 * h + 32],
                                           pt[:, 1 - s, h, SLOT * k:SLOT * k + SLOT],
                                           v2[:, 1 - s, k, h].rearrange("q a e -> q (a e)"), start=True, stop=True)
                    mm.then_inc(pv_done, 1)
                if has(c, loop, 2):
                    pe.wait_ge(at_out, c - 1)
                    if loop or c > 2:
                        pe.wait_ge(hh_ready, c - 2)
                    for e in range(EC):
                        mm = pe.matmul(ps[:, WO, 0:E], atT[:, s, e * P:(e + 1) * P], wo[:, e, :],
                                       start=(e == 0), stop=(e == EC - 1))
                    mm.then_inc(wo_done, 1)

            cycles(pe, cycle)

        @block.scalar
        def _(act):
            def cycle(c, s, loop):
                if has(c, loop, 2):
                    act.wait_ge(at_done, c - 1)
                    if loop or c > 3:
                        act.wait_ge(wo_done, c - 2)
                    act.activation(atT[:, s], ps[:, AT, 0:E], ACT.Copy).then_inc(at_out, 1)
                if has(c, loop, 1):
                    act.wait_ge(pt_done, c)
                    act.activation(pt[:, 1 - s].rearrange("q h k -> q (h k)"),
                                   ps[:, PT:PT + 2, :].rearrange("q n x -> q (n x)"), ACT.Copy).then_inc(pt_out, 1)
                if has(c, loop, 0):
                    act.wait_ge(v_done, c + 1)
                    if loop or c > 1:
                        act.wait_ge(pv_done, c - 1)
                    else:
                        act.wait_ge(zeroed, 2)
                    for k in range(2):
                        rows = slice(SLOT * k, SLOT * k + SLOT)
                        src = ps[rows, VB, :].rearrange("q (i h a e) -> q i h a e", i=2, a=2, e=DH)
                        cp = act.activation(v2[rows, s, :, :, k, :], src[:, :, :, k, :], ACT.Copy)
                    cp.then_inc(v_out, 1)
                    act.wait_ge(sub_ready, c + 1)
                    if loop or c > 1:
                        act.wait_ge(pt_done, c - 1)
                        act.wait_ge(sum_ready, c - 1)
                    act.activation(pr[:, s, :, 0:T], sc[:, s], ACT.Exp, scale=float(DH) ** -0.5).then_inc(p_ready, 1)
                if has(c, loop, 2):
                    act.wait_ge(hh_ready, c - 1)
                    if loop or c > 2:
                        act.wait_ge(ss_ready, c - 2)
                    act.activation(junk[:], row(xh_all, c - 2), ACT.Square, accum_out=ss[:, ds(c - 2, 1)]
                                   ).then_inc(ss_ready, 1)

            cycles(act, cycle)
            act.wait_ge(ss_ready, PAIRS)

        @block.vector
        def _(dve):
            dve.memset(v2[:].rearrange("q s i h a e -> q (s i h a e)"), 0.0).then_inc(zeroed, 1)
            dve.memset(pr[:].rearrange("q s h k -> q (s h k)"), 0.0).then_inc(zeroed, 1)
            dve.wait_ge(c_in, 64)

            def per_head(t, s, n):
                return t[:, s].rearrange("q (h a) -> q h a", a=1).broadcast_to([P, HEADS, n])

            def cycle(c, s, loop):
                if has(c, loop, 1):
                    dve.wait_ge(p_ready, c)
                    if loop or c > 2:
                        dve.wait_ge(ri_ready, c - 2)
                    dve.tensor_reduce(sm[:, 1 - s], pr[:, 1 - s, :, 0:T], AX.X, ALU.add).then_inc(sum_ready, 1)
                    dve.wait_ge(sum_ready, c)
                    dve.reciprocal(ri[:, 1 - s], sm[:, 1 - s]).then_inc(ri_ready, 1)
                if has(c, loop, 0):
                    dve.wait_ge(s_done, c + 1)
                    if loop or c > 1:
                        dve.wait_ge(p_ready, c - 1)
                    mask = causal[:].rearrange("q (a t) -> q a t", a=1).broadcast_to([P, HG, T])
                    for e in range(EC):
                        add = dve.tensor_tensor(sc[:, s, HG * e:HG * e + HG],
                                                ps[:, SC + e, 0:W].rearrange("q (h t) -> q h t", t=T), mask, ALU.add)
                    add.then_inc(sc_ready, 1)
                    dve.wait_ge(sc_ready, c + 1)
                    dve.tensor_reduce(mx[:, s], sc[:, s], AX.X, ALU.max).then_inc(mx_ready, 1)
                    dve.wait_ge(mx_ready, c + 1)
                    dve.tensor_tensor(sc[:, s], sc[:, s], per_head(mx, s, T), ALU.subtract).then_inc(sub_ready, 1)
                if has(c, loop, 1):
                    dve.wait_ge(pv_done, c)
                    dve.wait_ge(ri_ready, c)
                    if loop or c > 2:
                        dve.wait_ge(at_done, c - 2)
                    dve.tensor_tensor(at[:, 1 - s].rearrange("q (h e) -> q h e", e=DH),
                                      ps[:, PV, 0:E].rearrange("q (h e) -> q h e", e=DH),
                                      per_head(ri, 1 - s, DH), ALU.mult).then_inc(at_ready, 1)
                if has(c, loop, 2):
                    p = c - 2
                    dve.wait_ge(wo_done, c - 1)
                    dve.tensor_tensor(row(xh_all, p), ps[:, WO, 0:E], row(xh_all, p), ALU.add).then_inc(hh_ready, 1)
                    dve.wait_ge(hh_ready, c - 1)
                    dve.tensor_tensor(row(h_all, p), row(xh_all, p), row(h_all, p), ALU.add).then_inc(r_ready, 1)

            cycles(dve, cycle)
            dve.wait_ge(r_ready, PAIRS)


def router_stage(nc, d, ps, h_all, xh_all, ss, wg, wu, w_in, slot_hi, slot_lo, w_hi, w_lo, tile_expert, x_slots, ident):
    with Mem(nc, "router") as m:
        wr = m.sb("w_router", [P, EC, EXPERTS])
        g2 = m.sb("g2_rows", [P, E])
        ms, rm, rr = (m.sb(n, [P, PAIRS]) for n in ("hh_ms", "hh_rms", "hh_rrms"))
        xf = m.sb("xf", [P, 2, E])
        xp = m.sb("xfT_pair", [P, 2, EC, P])
        (lg, pb, top, best, left, chosen, comb, inc, base, pos, t0, t1, totals) = (
            m.sb(n, [P, PAIRS, EXPERTS]) for n in (
                "logits", "router_probs", "top8", "top2", "others", "chosen", "combine", "until_pair", "before",
                "slot", "tmp0", "tmp1", "pair_totals"))
        red = m.sb("router_red", [P, 4, PAIRS])
        ones_row = m.sb("ones_row", [P, PAIRS])
        before, allones = m.sb("rows_before", [P, P]), m.sb("all_ones", [P, P])
        valid, off = m.sb("valid_rows", [P, 1]), m.sb("off_slots", [P, 1])
        starts, index = m.sb("tile_starts", [P, TOKENS // P + 1]), m.sb("tile_index", [P, TILES])
        cnt, end, first = (m.sb(n, [P, EXPERTS]) for n in ("tiles_of", "tile_end", "first_slot"))
        cmp = m.sb("more_than", [P, EXPERTS, TOKENS // P + 1])
        cmp2 = m.sb("at_or_after", [P, TILES, EXPERTS])
        te = m.sb("tile_expert_f", [P, TILES])
        hi, lo = m.sb("slot_hi_f", [P, 2, PAIRS]), m.sb("slot_lo_f", [P, 2, PAIRS])
        (c_in, ms_ready, rm_ready, rr_ready, xs_ready, xf_ready, xt_done, xt_out, l_done, l_ready, chain, e_ready,
         top_ready, left_ready, chosen_ready, rank_done, slots_ready, scattered) = (m.sem(n) for n in (
            "c_in", "ms_ready", "rm_ready", "rr_ready", "xs_ready", "xf_ready", "xt_done", "xt_out", "l_done",
            "l_ready", "chain", "e_ready", "top_ready", "left_ready", "chosen_ready", "rank_done", "slots_ready",
            "scattered"))
        block = m.stack.enter_context(nc.Block())

        @block.sync
        def _(sp):
            for t, src in ((wr, "w_router"), (g2, "g2_rows"), (before, "rows_before"), (allones, "all_ones"),
                           (valid, "valid_rows"), (off, "off_slots"), (starts, "tile_starts"), (index, "tile_index")):
                sp.dma_start(t[:], d[src]).then_inc(c_in, 16)
            for e in range(EXPERTS):
                for t, src in ((wg, "wg"), (wu, "wu")):
                    sp.dma_start(t[:, e], d[src][e]).then_inc(w_in, 16)

        @block.gpsimd
        def _(pool):
            pool.wait_ge(slots_ready, 2)
            for p in range(PAIRS):
                for slot in (slot_hi, slot_lo):
                    pool.indirect_dma_start(x_slots, bass.IndirectOffsetOnAxis(ap=slot[:, p:p + 1], axis=0),
                                            xh_all[:, p, :], None, bounds_check=TILES * P - 1, oob_is_err=False
                                            ).then_inc(scattered, 16)
            pool.wait_ge(scattered, 16 * 2 * PAIRS)

        @block.tensor
        def _(pe):
            pe.wait_ge(c_in, 128)

            def turn(p, s, first):
                pe.wait_ge(xf_ready, p + 1)
                if not first:
                    pe.wait_ge(xt_out, p - 1)
                for c in range(EC):
                    mm = pe.transpose(ps[:, s, c * P:(c + 1) * P], xf[:, s, c * P:(c + 1) * P], ident[:])
                mm.then_inc(xt_done, 1)
                pe.wait_ge(xt_out, p + 1)
                if not first:
                    pe.wait_ge(l_ready, p - 1)
                for c in range(EC):
                    mm = pe.matmul(ps[:, 2 + s, 0:EXPERTS], xp[:, s, c, :], wr[:, c, :], start=(c == 0), stop=(c == EC - 1))
                mm.then_inc(l_done, 1)

            ring(pe, turn)
            pe.wait_ge(chosen_ready, 1)
            moving = chosen[:].rearrange("q p e -> q (p e)")
            pe.matmul(ps[:, 4, 0:P], before[:], moving, start=True, stop=True).then_inc(rank_done, 1)
            pe.matmul(ps[:, 5, 0:P], allones[:], moving, start=True, stop=True).then_inc(rank_done, 1)

        @block.scalar
        def _(act):
            act.wait_ge(ms_ready, 1)
            act.activation(rm[:], ms[:], ACT.Sqrt).then_inc(rm_ready, 1)

            def out(p, s, first):
                act.wait_ge(xt_done, p + 1)
                if not first:
                    act.wait_ge(l_done, p - 1)
                act.activation(xp[:, s].rearrange("q c n -> q (c n)"), ps[:, s, 0:E], ACT.Copy).then_inc(xt_out, 1)

            ring(act, out)
            act.wait_ge(chain, 2)
            act.activation(pb[:], lg[:], ACT.Exp).then_inc(e_ready, 1)

        @block.vector
        def _(dve):
            steps = 0

            def then(ins):
                nonlocal steps
                steps += 1
                ins.then_inc(chain, 1)
                dve.wait_ge(chain, steps)

            dve.tensor_scalar(ms[:], ss[:], 1.0 / E, EPS_RMS, ALU.mult, ALU.add).then_inc(ms_ready, 1)
            dve.wait_ge(rm_ready, 1)
            dve.reciprocal(rr[:], rm[:]).then_inc(rr_ready, 1)
            dve.wait_ge(rr_ready, 1)
            dve.wait_ge(c_in, 128)

            def scaled(p, s, first):
                if not first:
                    dve.wait_ge(xt_done, p - 1)
                dve.scalar_tensor_tensor(out=xf[:, s], in0=row(xh_all, p), scalar=rr[:, ds(p, 1)], in1=g2[:],
                                         op0=ALU.mult, op1=ALU.mult).then_inc(xf_ready, 1)

            def logits(p, s):
                dve.tensor_scalar(row(xh_all, p), xf[:, s], 1.0, None, ALU.mult).then_inc(xs_ready, 1)
                dve.wait_ge(l_done, p + 1)
                dve.tensor_scalar(row(lg, p), ps[:, 2 + s, 0:EXPERTS], 1.0, None, ALU.mult).then_inc(l_ready, 1)

            scaled(0, 0, True)
            scaled(1, 1, True)
            dve.wait_ge(xf_ready, 1)
            logits(0, 0)
            with dve.Fori(1, PAIRS // 2) as i:
                dve.wait_ge(xs_ready, 2 * i - 1)
                scaled(2 * i, 0, False)
                dve.wait_ge(xf_ready, 2 * i)
                logits(2 * i - 1, 1)
                dve.wait_ge(xs_ready, 2 * i)
                scaled(2 * i + 1, 1, False)
                dve.wait_ge(xf_ready, 2 * i + 1)
                logits(2 * i, 0)
            dve.wait_ge(xf_ready, PAIRS)
            logits(PAIRS - 1, 1)

            def each(t):
                return t.rearrange("q (p a) -> q p a", a=1).broadcast_to([P, PAIRS, EXPERTS])

            dve.wait_ge(l_ready, PAIRS)
            then(dve.tensor_reduce(red[:, 0], lg[:], AX.X, ALU.max))
            then(dve.tensor_tensor(lg[:], lg[:], each(red[:, 0]), ALU.subtract))
            dve.wait_ge(e_ready, 1)
            then(dve.tensor_reduce(red[:, 1], pb[:], AX.X, ALU.add))
            then(dve.reciprocal(red[:, 2], red[:, 1]))
            then(dve.tensor_tensor(pb[:], pb[:], each(red[:, 2]), ALU.mult))
            then(dve.memset(best[:].rearrange("q p k -> q (p k)"), -1.0))
            for p in range(PAIRS):
                dve.max(top[:, p], pb[:, p]).then_inc(top_ready, 1)
            dve.wait_ge(top_ready, PAIRS)
            then(dve.tensor_copy(best[:, :, 0:2], top[:, :, 0:2]))
            for p in range(PAIRS):
                dve.match_replace(left[:, p], best[:, p], pb[:, p], -1.0).then_inc(left_ready, 1)
            dve.wait_ge(left_ready, PAIRS)
            then(dve.tensor_tensor(chosen[:], left[:], pb[:], ALU.not_equal))
            then(dve.tensor_scalar(chosen[:], chosen[:], valid[:, 0:1], None, ALU.mult))
            dve.sem_inc(chosen_ready, 1)
            then(dve.tensor_tensor(red[:, 3], top[:, :, 0], top[:, :, 1], ALU.add))
            then(dve.reciprocal(red[:, 0], red[:, 3]))
            then(dve.tensor_tensor(comb[:], pb[:], chosen[:], ALU.mult))
            then(dve.tensor_tensor(comb[:], comb[:], each(red[:, 0]), ALU.mult))
            then(dve.memset(ones_row[:], 1.0))

            dve.wait_ge(rank_done, 2)
            then(dve.tensor_copy(totals[:], ps[:, 5, 0:P].rearrange("q (p e) -> q p e", e=EXPERTS)))
            for e in range(EXPERTS):
                then(dve.tensor_tensor_scan(inc[:, :, e], ones_row[:], totals[:, :, e], 0.0, ALU.mult, ALU.add))
            n_starts = TOKENS // P + 1
            then(dve.tensor_tensor(cmp[:], inc[:, PAIRS - 1, :].rearrange("q (e a) -> q e a", a=1).broadcast_to(
                [P, EXPERTS, n_starts]), starts[:].rearrange("q (a n) -> q a n", a=1).broadcast_to(
                [P, EXPERTS, n_starts]), ALU.is_gt))
            then(dve.tensor_reduce(cnt[:], cmp[:], AX.X, ALU.add))
            then(dve.tensor_tensor_scan(end[:], ones_row[:, 0:EXPERTS], cnt[:], 0.0, ALU.mult, ALU.add))
            then(dve.tensor_tensor(first[:], end[:], cnt[:], ALU.subtract))
            then(dve.tensor_scalar(first[:], first[:], float(P), None, ALU.mult))
            then(dve.tensor_tensor(base[:], inc[:], totals[:], ALU.subtract))
            then(dve.tensor_tensor(base[:], base[:], first[:].rearrange("q (a e) -> q a e", a=1).broadcast_to(
                [P, PAIRS, EXPERTS]), ALU.add))
            then(dve.tensor_tensor(pos[:], ps[:, 4, 0:P].rearrange("q (p e) -> q p e", e=EXPERTS), base[:], ALU.add))

            then(dve.scalar_tensor_tensor(out=t0[:], in0=pos[:], scalar=1.0, in1=chosen[:], op0=ALU.add, op1=ALU.mult))
            then(dve.tensor_reduce(hi[:, 0], t0[:], AX.X, ALU.max))
            then(dve.tensor_scalar(hi[:, 0], hi[:, 0], 1.0, None, ALU.subtract))
            then(dve.tensor_scalar(t1[:], pos[:], -1.0, float(TILES * P), ALU.mult, ALU.add))
            then(dve.tensor_tensor(t1[:], t1[:], chosen[:], ALU.mult))
            then(dve.tensor_reduce(lo[:, 0], t1[:], AX.X, ALU.max))
            then(dve.tensor_scalar(lo[:, 0], lo[:, 0], -1.0, float(TILES * P), ALU.mult, ALU.add))
            for f, i32, w in ((hi, slot_hi, w_hi), (lo, slot_lo, w_lo)):
                then(dve.tensor_scalar(f[:, 1], f[:, 0], off[:, 0:1], None, ALU.add))
                dve.tensor_copy(i32[:], f[:, 1]).then_inc(slots_ready, 1)
            for f, i32, w in ((hi, slot_hi, w_hi), (lo, slot_lo, w_lo)):
                then(dve.tensor_tensor(t0[:], pos[:], each(f[:, 0]), ALU.is_equal))
                then(dve.tensor_tensor(t0[:], t0[:], comb[:], ALU.mult))
                then(dve.tensor_reduce(w[:], t0[:], AX.X, ALU.add))
            then(dve.tensor_tensor(cmp2[:], index[:].rearrange("q (n a) -> q n a", a=1).broadcast_to(
                [P, TILES, EXPERTS]), end[:].rearrange("q (a e) -> q a e", a=1).broadcast_to(
                [P, TILES, EXPERTS]), ALU.is_ge))
            then(dve.tensor_reduce(te[:], cmp2[:], AX.X, ALU.add))
            then(dve.tensor_scalar(te[:], te[:], float(EXPERTS - 1), None, ALU.min))
            then(dve.tensor_copy(tile_expert[:], te[:]))
            dve.wait_ge(xs_ready, PAIRS)


def experts_stage(nc, d, ps, wg, wu, wd, w_in, tile_expert, x_slots, y_slots, ident):
    HALF = HID // 2
    FULL = HID // P
    TAIL = HID - FULL * P
    G, U, HT, XT, Y = 0, 2, 4, 6, 7
    with Mem(nc, "experts") as m:
        x = m.sb("x_tile", [P, 2, E])
        xT = m.sb("xT_tile", [P, 2, E])
        g, h = m.sb("gate", [P, 2, HID]), m.sb("hidden", [P, 2, HID])
        hT = m.sb("hiddenT", [P, 2, FULL + 1, P])
        y = m.sb("y_tile", [P, 2, E])
        (xt_done, xt_out, gu_done, g_ready, h_ready, ht_done, ht_out, y_done, y_ready) = (m.sem(n) for n in (
            "xt_done", "xt_out", "gu_done", "g_ready", "h_ready", "ht_done", "ht_out", "y_done", "y_ready"))
        x_in, y_out = ([m.sem(f"{n}{s}") for s in range(2)] for n in ("x_in", "y_out"))
        block = m.stack.enter_context(nc.Block())

        def cycles(eng, cycle):
            for c in range(4):
                cycle(c, c % 2, False)
            with eng.Fori(2, TILES // 2 - 1) as i:
                for s in range(2):
                    cycle(2 * i + s, s, True)
            for c in range(TILES - 2, TILES + 1):
                cycle(c, c % 2, False)

        def tile(ap, t):
            return ap.rearrange("(n q) e -> n q e", q=P)[ds(t, 1)].rearrange("a q e -> (a q) e")

        @block.sync
        def _(sp):
            for s in range(2):
                sp.dma_start(x[:, s], tile(x_slots, s)).then_inc(x_in[s], 16)

            def cycle(c, s, loop):
                if loop or c + 2 < TILES:
                    sp.wait_ge(xt_done, c + 1)
                    sp.dma_start(x[:, s], tile(x_slots, c + 2)).then_inc(x_in[s], 16)
                if loop or c >= 1:
                    sp.wait_ge(y_ready, c)
                    sp.dma_start(tile(y_slots, c - 1), y[:, 1 - s]).then_inc(y_out[1 - s], 16)

            cycles(sp, cycle)
            for s in range(2):
                sp.wait_ge(y_out[s], 16 * (TILES // 2))

        @block.tensor
        def _(pe):
            def turn_x(t, s, n):
                pe.wait_ge(x_in[s], 16 * n)
                for c in range(EC):
                    mm = pe.transpose(ps[:, XT, c * P:(c + 1) * P], x[:, s, c * P:(c + 1) * P], ident[:])
                mm.then_inc(xt_done, 1)

            def expert(t):
                return pe.value_load(tile_expert[0:1, ds(t, 1)], min_val=0, max_val=EXPERTS - 1)

            def cycle(c, s, loop):
                if loop or 1 <= c:
                    pe.wait_ge(h_ready, 2 * c)
                    if loop or c >= 2:
                        pe.wait_ge(ht_out, c - 1)
                    for j in range(FULL + 1):
                        w = P if j < FULL else TAIL
                        mm = pe.transpose(ps[0:w, HT + j // 4, (j % 4) * P:(j % 4 + 1) * P],
                                          h[:, 1 - s, j * P:j * P + w], ident[:])
                    mm.then_inc(ht_done, 1)
                if loop or c < TILES:
                    e = expert(c)
                    pe.wait_ge(xt_out, c + 1)
                    for k in range(2):
                        for bank, w in ((G, wg), (U, wu)):
                            for i in range(EC):
                                mm = pe.matmul(ps[:, bank + k, 0:HALF], xT[:, s, i * P:(i + 1) * P],
                                               w[:, ds(e, 1), i, k * HALF:(k + 1) * HALF].rearrange("q a n -> q (a n)"),
                                               start=(i == 0), stop=(i == EC - 1))
                        mm.then_inc(gu_done, 1)
                if loop or c + 1 < TILES:
                    turn_x(c + 1, 1 - s, (c + 1) // 2 + 1 if not loop else c_half[0] + s + 1)
                if loop or 1 <= c:
                    e = expert(c - 1)
                    pe.wait_ge(ht_out, c)
                    if loop or c >= 2:
                        pe.wait_ge(y_ready, c - 1)
                    for j in range(FULL + 1):
                        w = P if j < FULL else TAIL
                        mm = pe.matmul(ps[:, Y, 0:E], hT[0:w, 1 - s, j, :],
                                       wd[0:w, ds(e, 1), j, :].rearrange("q a n -> q (a n)"),
                                       start=(j == 0), stop=(j == FULL))
                    mm.then_inc(y_done, 1)

            pe.wait_ge(w_in, 16 * (2 * EXPERTS + 1))
            turn_x(0, 0, 1)
            c_half = [None]
            cycle(0, 0, False)
            cycle(1, 1, False)
            with pe.Fori(1, TILES // 2 - 1) as i:
                c_half[0] = i
                for s in range(2):
                    cycle(2 * i + s, s, True)
            for c in range(TILES - 2, TILES + 1):
                cycle(c, c % 2, False)

        @block.scalar
        def _(act):
            def x_copy(t, s, first):
                act.wait_ge(xt_done, t + 1)
                if not first:
                    act.wait_ge(gu_done, 2 * t - 2)
                act.activation(xT[:, s], ps[:, XT, 0:E], ACT.Copy).then_inc(xt_out, 1)

            def cycle(c, s, loop):
                if loop or 1 <= c:
                    act.wait_ge(ht_done, c)
                    if loop or c >= 3:
                        act.wait_ge(y_done, c - 2)
                    act.activation(hT[:, 1 - s, 0:FULL].rearrange("q j n -> q (j n)"),
                                   ps[:, HT:HT + 2, :].rearrange("q n x -> q (n x)")[:, 0:FULL * P], ACT.Copy)
                    act.activation(hT[0:TAIL, 1 - s, FULL], ps[0:TAIL, HT + FULL // 4, (FULL % 4) * P:(FULL % 4 + 1) * P],
                                   ACT.Copy).then_inc(ht_out, 1)
                if loop or c < TILES:
                    for k in range(2):
                        act.wait_ge(gu_done, 2 * c + k + 1)
                        if loop or c >= 2:
                            act.wait_ge(h_ready, 2 * c + k - 3)
                        act.activation(g[:, s, k * HALF:(k + 1) * HALF], ps[:, G + k, 0:HALF], ACT.Silu
                                       ).then_inc(g_ready, 1)
                if loop or c + 1 < TILES:
                    x_copy(c + 1, 1 - s, not loop and c == 0)

            x_copy(0, 0, True)
            cycles(act, cycle)

        @block.vector
        def _(dve):
            def cycle(c, s, loop):
                if loop or c < TILES:
                    for k in range(2):
                        dve.wait_ge(g_ready, 2 * c + k + 1)
                        if loop or c >= 2:
                            dve.wait_ge(ht_done, c - 1)
                        dve.tensor_tensor(h[:, s, k * HALF:(k + 1) * HALF], ps[:, U + k, 0:HALF],
                                          g[:, s, k * HALF:(k + 1) * HALF], ALU.mult).then_inc(h_ready, 1)
                if loop or 1 <= c:
                    dve.wait_ge(y_done, c)
                    if loop or c >= 3:
                        y_stored(c, s, loop)
                    dve.tensor_copy(y[:, 1 - s], ps[:, Y, 0:E]).then_inc(y_ready, 1)

            def y_stored(c, s, loop):
                if loop:
                    if s == 0:
                        dve.wait_ge(y_out[1], 16 * half[0] - 16)
                    else:
                        dve.wait_ge(y_out[0], 16 * half[0])
                else:
                    dve.wait_ge(y_out[1 - s], 16 * ((c - 1) // 2))

            half = [None]
            for c in range(4):
                cycle(c, c % 2, False)
            with dve.Fori(2, TILES // 2 - 1) as i:
                half[0] = i
                for s in range(2):
                    cycle(2 * i + s, s, True)
            for c in range(TILES - 2, TILES + 1):
                cycle(c, c % 2, False)


def combine_stage(nc, h_all, slot_hi, slot_lo, w_hi, w_lo, y_slots, out):
    RING = 4
    GROUP = 4
    with Mem(nc, "combine") as m:
        y = m.sb("y_rows", [P, 2, RING, E])
        zeroed, added = m.sem("zeroed"), [m.sem("added_hi"), m.sem("added_lo")]
        y_in = [m.sem(f"y_in{s}") for s in range(RING)]
        stored = m.sem("out_stored")
        block = m.stack.enter_context(nc.Block())

        @block.gpsimd
        def _(pool):
            pool.wait_ge(zeroed, 1)
            for p in range(PAIRS):
                if p >= RING:
                    pool.wait_ge(added[1], p - RING + 1)
                for k, slot in enumerate((slot_hi, slot_lo)):
                    pool.indirect_dma_start(y[:, k, p % RING], None, y_slots,
                                            bass.IndirectOffsetOnAxis(ap=slot[:, p:p + 1], axis=0),
                                            bounds_check=TILES * P - 1, oob_is_err=False).then_inc(y_in[p % RING], 16)

        @block.vector
        def _(dve):
            dve.memset(y[:].rearrange("q k s e -> q (k s e)"), 0.0).then_inc(zeroed, 1)
            for p in range(PAIRS):
                dve.wait_ge(y_in[p % RING], 32 * (p // RING) + 32)
                for k, w in enumerate((w_hi, w_lo)):
                    if k:
                        dve.wait_ge(added[0], p + 1)
                    dve.scalar_tensor_tensor(out=h_all[:, p], in0=y[:, k, p % RING], scalar=w[:, p:p + 1],
                                             in1=h_all[:, p], op0=ALU.mult, op1=ALU.add).then_inc(added[k], 1)

        @block.sync
        def _(sp):
            rows = out.rearrange("(p i t) e -> i t p e", i=2, t=T)
            for p in range(0, PAIRS, GROUP):
                sp.wait_ge(added[1], p + GROUP)
                for k in range(2):
                    sp.dma_start(rows[k][:, p:p + GROUP], h_all[SLOT * k:SLOT * k + T, p:p + GROUP]
                                 ).then_inc(stored, 16)
            sp.wait_ge(stored, 16 * 2 * PAIRS // GROUP)


def build(nc, d, out):
    v_rows = nc.dram_tensor("v_rows", (TOKENS, PARTS * 2 * E), BF16).ap()
    o_rows = nc.dram_tensor("o_rows", (IMAGES, T, E), F32).ap()
    x_slots = nc.dram_tensor("x_slots", (TILES * P, E), F32).ap()
    y_slots = nc.dram_tensor("y_slots", (TILES * P, E), F32).ap()
    with nc.psum_tensor("ps", [P, 8, 512], F32) as ps, Mem(nc) as m:
        ident = m.sb("ident", [P, P])
        h_all = m.sb("h_all", [P, PAIRS, E])
        w_in = m.sem("expert_w_in")
        with nc.cleanup_on_exit(), Mem(nc) as cell:
            kn = cell.sb("kn", [P, NH_CELL, CHUNK])
            qn = cell.sb("qn", [P, NH_CELL, CHUNK])
            with Mem(nc) as early:
                zT = early.sb("zT", [P, EC, TOKENS])
                tokens_stage(nc, d, ps, h_all, zT, ident)
                projections_stage(nc, d, ps, zT, kn, qn, v_rows)
            scan_stage(nc, d, ps, kn, qn, v_rows, o_rows)
        xh_all = m.sb("xh_all", [P, PAIRS, E])
        ss = m.sb("hh_ss", [P, PAIRS])
        wd = m.sb("expert_wd", [P, EXPERTS, HID // P + 1, E])
        with Mem(nc) as att:
            xnT, qr, kr = (att.sb(n, [P, EC, PAIRS * P]) for n in ("xnT", "q_rot", "k_rot"))
            cell_output_stage(nc, d, ps, o_rows, h_all, xh_all, xnT, ident, wd, w_in, x_slots)
            rotary_stage(nc, d, ps, xnT, qr, kr)
            attention_stage(nc, d, ps, xnT, qr, kr, h_all, xh_all, ss, ident)
        wg, wu = (m.sb(n, [P, EXPERTS, EC, HID]) for n in ("expert_wg", "expert_wu"))
        slot_hi, slot_lo = (m.sb(n, [P, PAIRS], mybir.dt.int32) for n in ("slot_hi", "slot_lo"))
        w_hi, w_lo = m.sb("w_hi", [P, PAIRS]), m.sb("w_lo", [P, PAIRS])
        tile_expert = m.sb("tile_expert", [P, TILES], mybir.dt.int32)
        router_stage(nc, d, ps, h_all, xh_all, ss, wg, wu, w_in, slot_hi, slot_lo, w_hi, w_lo, tile_expert, x_slots,
                     ident)
        experts_stage(nc, d, ps, wg, wu, wd, w_in, tile_expert, x_slots, y_slots, ident)
        combine_stage(nc, h_all, slot_hi, slot_lo, w_hi, w_lo, y_slots, out)


def host_layout(np, bf16, inp):
    f = {k: np.ascontiguousarray(v) for k, v in inp.items()}
    a = {}

    def chunked(w):
        k = w.shape[0] // P
        return np.ascontiguousarray(w.reshape(k, P, w.shape[1]).transpose(1, 0, 2))

    x = f["x"].reshape(IMAGES, 3, 6, 16, 6, 16).transpose(0, 1, 3, 5, 2, 4).reshape(IMAGES, DC, P, PATCHES)
    xT = np.zeros((PAIRS, P, DC, 2, SLOT), np.float32)
    xT[..., 2:T] = x.reshape(PAIRS, 2, DC, P, PATCHES).transpose(0, 3, 2, 1, 4)
    a["xT"] = xT.reshape(PAIRS, P, DC, P)
    a["tok_W"] = chunked(f["L0_tok_W"])

    def padded(rows):
        t = np.zeros((2, SLOT, E), np.float32)
        t[:, :T] = rows
        return t.reshape(P, E)

    z = np.zeros((T, E), np.float32)
    pos, bias, gamma, beta = z.copy(), z.copy(), z.copy(), z.copy()
    pos[1:] = f["L0_tok_pos_embedding"][0]
    bias[1], bias[2:] = f["L0_tok_cls_token"][0, 0], f["L0_tok_b"]
    gamma[1:] = f["L0_tok_gamma"]
    beta[0], beta[1:] = f["cls_tok"][0, 0], f["L0_tok_beta"]
    a["t_pos"], a["t_bias"], a["t_gamma"], a["t_beta"] = (padded(t) for t in (pos, bias, gamma, beta))
    a["W_in"], a["W_k"], a["W_q"] = (chunked(f[f"L0_attn_{n}"].T) for n in ("W_in", "W_k", "W_q"))
    a["W_vb"] = chunked(np.concatenate([f["L0_attn_W_v"].T, f["L0_attn_W_beta"].T], 1))
    a["W_out"] = chunked(f["L0_attn_W_out"].T)
    a["b_beta"] = np.ascontiguousarray(np.broadcast_to(f["L0_attn_b_beta"].reshape(1, E), (P, E)))
    perm = np.arange(E).reshape(HEADS, 2, DH // 2)[:, ::-1].reshape(E)
    for n in ("wq", "wk"):
        a[n], a[n + "_perm"] = chunked(f[f"L0_ffn_{n}"]), chunked(f[f"L0_ffn_{n}"][:, perm])
    a["wv"], a["wo"] = chunked(f["L0_ffn_wv"]), chunked(f["L0_ffn_wo"])
    a["g1"] = np.ascontiguousarray(f["L0_ffn_g1"].reshape(EC, P).T)
    a["w_router"] = chunked(f["L0_ffn_w_router"])
    a["g2_rows"] = np.ascontiguousarray(np.broadcast_to(f["L0_ffn_g2"].reshape(1, E), (P, E)))
    a["wg"], a["wu"] = (np.stack([chunked(w) for w in f[f"L0_ffn_{n}"]]) for n in ("wg", "wu"))
    wd = np.zeros((EXPERTS, -(-HID // P) * P, E), np.float32)
    wd[:, :HID] = f["L0_ffn_wd"]
    a["wd"] = np.ascontiguousarray(np.stack([chunked(w) for w in wd]).transpose(1, 0, 2, 3))

    p = np.arange(P)
    a["ident"] = np.eye(P, dtype=np.float32)
    block = p // NCELL
    a["block_ones"] = (block[:, None] == block[None]).astype(np.float32)
    a["minus_block_ones"] = -a["block_ones"]
    osel = np.zeros((P, 4, P), np.float32)
    for k in range(4):
        osel[p, k, B4 * k + block] = 1.0
    a["block_sum_to_row"] = osel
    rows = (p[:, None] < PARTS * B4) & (p[:, None] % B4 == block[None])
    a["part_rows_to_block"] = rows.astype(bf16)
    freq = 1.0 / 10000.0 ** (np.arange(0, DH, 2, dtype=np.float32) / DH)
    ang = np.einsum("i,j->ij", np.arange(T, dtype=np.float32), freq)
    ang = np.concatenate([ang, ang], -1)[:, p % DH].T
    cos, sin = np.zeros((P, SLOT), np.float32), np.zeros((P, SLOT), np.float32)
    cos[:, :T] = np.cos(ang)
    sin[:, :T] = np.sin(ang) * np.where(p % DH < DH // 2, -1.0, 1.0)[:, None]
    a["cos"], a["sin"] = cos.astype(np.float32), sin.astype(np.float32)
    t = p % SLOT
    a["causal"] = np.where(np.arange(T)[None] > t[:, None], -1e30, 0.0).astype(np.float32)
    valid = p % SLOT < T
    a["valid_rows"] = valid.astype(np.float32)[:, None]
    a["off_slots"] = np.where(valid, 0.0, TILES * P + 1.0 + p).astype(np.float32)[:, None]
    a["rows_before"] = (p[:, None] < p[None]).astype(np.float32)
    a["all_ones"] = np.ones((P, P), np.float32)
    a["tile_starts"] = np.ascontiguousarray(np.broadcast_to(P * np.arange(TOKENS // P + 1, dtype=np.float32),
                                                            (P, TOKENS // P + 1)))
    a["tile_index"] = np.ascontiguousarray(np.broadcast_to(np.arange(TILES, dtype=np.float32), (P, TILES)))
    a["head_mask"] = (p[:, None] // DH == np.arange(HG)[None]).astype(np.float32)
    return a


def kernel(**inputs):
    import ml_dtypes
    import numpy as np
    import concourse.bacc as bacc
    from concourse.bass_utils import run_bass_kernel_spmd

    nc = bacc.Bacc("TRN2", target_bir_lowering=False, num_devices=1)
    arrays = host_layout(np, ml_dtypes.bfloat16, inputs)
    d = {k: nc.dram_tensor(f"in_{k}", v.shape, mybir.dt.from_np(v.dtype), kind="ExternalInput").ap()
         for k, v in arrays.items()}
    out = nc.dram_tensor("out_0", (TOKENS, E), F32, kind="ExternalOutput").ap()
    build(nc, d, out)
    r = run_bass_kernel_spmd(nc, [{f"in_{k}": v for k, v in arrays.items()}], core_ids=[0])
    return r.results[0]["out_0"].reshape(IMAGES, T, E)
```

```python
from contextlib import ExitStack

import concourse.bass as bass
from concourse import mybir
from concourse.alu_op_type import AluOpType as ALU

ACT = mybir.ActivationFunctionType
AX = mybir.AxisListType
F32 = mybir.dt.float32
BF16 = mybir.dt.bfloat16
ds = bass.ds

P = 128
IMAGES = 32
PATCHES = 36
T = PATCHES + 2
E = 256
EC = E // P
DPATCH = 768
DC = DPATCH // P
PAIRS = IMAGES // 2
SLOT = 64
TOKENS = IMAGES * T
NH_CELL, NCELL = 8, 32
B4 = P // NCELL
B8 = IMAGES // B4
CHUNK = B8 * T
HEADS, DH = 16, 16
HG = HEADS // EC
EXPERTS = 8
HID = 704
TOPK = 2
TILES = (TOKENS * TOPK + EXPERTS * (P - 1)) // P
NT = -(-TOKENS // P)
LAST_ROWS = TOKENS - (NT - 1) * P
PAIRS_FIRST = 13
NT_FIRST = PAIRS_FIRST * 2 * T // P
PARTS = 3
EPS_LN = 1e-5
EPS_RMS = 1e-6


class Mem:

    def __init__(self, nc, stage="core"):
        self.stage = stage
        self.nc, self.stack = nc, ExitStack()

    def __enter__(self):
        self.stack.__enter__()
        return self

    def __exit__(self, *a):
        return self.stack.__exit__(*a)

    def sb(self, name, shape, dt=F32):
        return self.stack.enter_context(self.nc.sbuf_tensor(name, shape, dt))

    def sem(self, name):
        return self.nc.alloc_semaphore(f"{self.stage}_{name}")


def pair_columns(ap, p, n=1):
    return ap[:, :, ds(p * 2 * T, 2 * T * n)].rearrange("q c (i t) -> q c i t", t=T)


def tokens_stage(nc, d, ps, h_all, zT, xpT, ident, wi, wts_in, later):
    GROUP = 4
    GROUPS = PAIRS // GROUP
    with Mem(nc, "tokens") as m:
        w = m.sb("tok_w", [P, DC, E])
        xt = m.sb("tok_x", [P, GROUP, DC, P])
        pos, bias = m.sb("tok_pos", [P, E]), m.sb("tok_bias", [P, E])
        gamma, beta = m.sb("tok_gamma", [P, E]), m.sb("tok_beta", [P, E])
        add = m.sb("tok_add", [P, E])
        n1, n2 = m.sb("tok_normed", [P, GROUP, E]), m.sb("tok_scaled", [P, GROUP, E])
        stats, stats2 = m.sb("tok_stats", [P, GROUP, 6]), m.sb("tok_stats2", [P, GROUP, 6])
        mv = m.sb("tok_mv", [P, 2, GROUP, 2])
        ve, sd, rs = m.sb("tok_ve", [P, 2, GROUP]), m.sb("tok_sd", [P, 2, GROUP]), m.sb("tok_rs", [P, 2, GROUP])
        z = m.sb("tok_z", [P, GROUP, E])
        half = m.sb("tanh_half", [P, 4, CHUNK])
        in_done, th_ready, xp_ready = m.sem("in_done"), m.sem("th_ready"), m.sem("xp_ready")
        cells = [(n, c) for n in range(B4) for c in range(EC)]
        w_in, tab_in = m.sem("w_in"), m.sem("tab_in")
        x_in = [m.sem(f"x_in{s}") for s in range(GROUP)]
        add_ready, proj_done, h_ready, stats_ready, mv_ready = (m.sem(n) for n in (
            "add_ready", "proj_done", "h_ready", "stats_ready", "mv_ready"))
        ve_ready, sd_ready, rs_ready = m.sem("ve_ready"), m.sem("sd_ready"), m.sem("rs_ready")
        n_ready, g_ready, h0_ready = m.sem("n_ready"), m.sem("g_ready"), m.sem("h0_ready")
        stats2_ready, mv2_ready = m.sem("stats2_ready"), m.sem("mv2_ready")
        z_ready, zt_done, zt_out = m.sem("z_ready"), m.sem("zt_done"), m.sem("zt_out")
        block = m.stack.enter_context(nc.Block())

        @block.sync
        def _(sp):
            sp.dma_start(w[:], d["tok_W"]).then_inc(w_in, 16)
            for s in range(GROUP):
                sp.dma_start(xt[:, s], d["xT"][s]).then_inc(x_in[s], 16)
            for t, src in ((pos, "t_pos"), (bias, "t_bias"), (gamma, "t_gamma"), (beta, "t_beta")):
                sp.dma_start(t[:], d[src]).then_inc(tab_in, 16)
            sp.dma_start(ident[:], d["ident"]).then_inc(tab_in, 16)
            for t, src, arrived in later:
                sp.dma_start(t[:], d[src]).then_inc(arrived, 16)
            with sp.Fori(1, GROUPS) as g:
                for s in range(GROUP):
                    sp.wait_ge(proj_done, GROUP * g + (s + 1 - GROUP))
                    sp.dma_start(xt[:, s], d["xT"][ds(GROUP * g + s, 1)].rearrange("a p c n -> (a p) c n")
                                 ).then_inc(x_in[s], 16)

        @block.tensor
        def _(pe):
            def project(g, first):
                for s in range(GROUP):
                    pe.wait_ge(x_in[s], 16 * g + 16)
                    if not first:
                        pe.wait_ge(h_ready, GROUP * g + (s + 1 - GROUP))
                    for c in range(DC):
                        mm = pe.matmul(ps[:, s, 0:E], xt[:, s, c, :], w[:, c, :], start=(c == 0), stop=(c == DC - 1))
                    mm.then_inc(proj_done, 1)

            def turn(g, first):
                for s in range(GROUP):
                    pe.wait_ge(z_ready, GROUP * g + s + 1)
                    if not first:
                        pe.wait_ge(zt_out, GROUP * g + (s + 1 - GROUP))
                    for c in range(EC):
                        mm = pe.transpose(ps[:, GROUP + s, c * P:(c + 1) * P], z[:, s, c * P:(c + 1) * P], ident[:])
                    mm.then_inc(zt_done, 1)

            pe.wait_ge(w_in, 16)
            project(0, True)
            pe.wait_ge(tab_in, 80)
            project(1, False)
            turn(0, True)
            with pe.Fori(2, GROUPS) as g:
                project(g, False)
                turn(g - 1, False)

            def input_product(j):
                n, c = cells[j]
                if j < 4:
                    pe.wait_ge(h_ready, PAIRS)
                else:
                    pe.wait_ge(xp_ready, j - 3)
                for k in range(EC):
                    mm = pe.matmul(ps[:, j % 4, 0:CHUNK], wi[:, k, c * P:(c + 1) * P],
                                   zT[:, k, n * CHUNK:(n + 1) * CHUNK], start=(k == 0), stop=(k == EC - 1))
                mm.then_inc(in_done, 1)

            pe.wait_ge(wts_in, 96)
            pe.wait_ge(zt_out, 2 * GROUP)
            for j in range(4):
                input_product(j)
            turn(GROUPS - 1, False)
            pe.wait_ge(zt_out, PAIRS)
            for j in range(4, len(cells)):
                input_product(j)

        @block.vector
        def _(dve):
            dve.wait_ge(tab_in, 80)
            dve.tensor_tensor(add[:], pos[:], bias[:], ALU.add).then_inc(add_ready, 1)
            dve.wait_ge(add_ready, 1)

            def alone(sem, value):
                dve.wait_ge(add_ready, 1)
                dve.wait_ge(sem, value)

            def inverse_deviation(k, g, source, st_ready, ready):
                alone(st_ready, GROUP * g + GROUP)
                for s in range(GROUP):
                    dve.bn_aggr(mv[:, k, s], source[:, s]).then_inc(ready, 1)
                dve.wait_ge(ready, GROUP * g + GROUP)
                dve.tensor_scalar(ve[:, k], mv[:, k, :, 1], EPS_LN, None, ALU.add).then_inc(ve_ready, 1)
                dve.wait_ge(sd_ready, 2 * g + k + 1)
                dve.reciprocal(rs[:, k], sd[:, k]).then_inc(rs_ready, 1)
                dve.wait_ge(rs_ready, 2 * g + k + 1)

            def group(g, first):
                for s in range(GROUP):
                    dve.wait_ge(proj_done, GROUP * g + s + 1)
                    dve.tensor_tensor(row(h_all, GROUP * g + s), ps[:, s, 0:E], add[:], ALU.add).then_inc(h_ready, 1)
                alone(h_ready, GROUP * g + GROUP)
                for s in range(GROUP):
                    dve.bn_stats(stats[:, s], row(h_all, GROUP * g + s)).then_inc(stats_ready, 1)
                inverse_deviation(0, g, stats, stats_ready, mv_ready)
                for s in range(GROUP):
                    dve.tensor_scalar(n1[:, s], row(h_all, GROUP * g + s), mv[:, 0, s, 0:1], rs[:, 0, s:s + 1],
                                      ALU.subtract, ALU.mult).then_inc(n_ready, 1)
                for s in range(GROUP):
                    dve.wait_ge(n_ready, GROUP * g + s + 1)
                    dve.tensor_tensor(n2[:, s], n1[:, s], gamma[:], ALU.mult).then_inc(g_ready, 1)
                for s in range(GROUP):
                    dve.wait_ge(g_ready, GROUP * g + s + 1)
                    dve.tensor_tensor(row(h_all, GROUP * g + s), n2[:, s], beta[:], ALU.add).then_inc(h0_ready, 1)
                alone(h0_ready, GROUP * g + GROUP)
                for s in range(GROUP):
                    dve.bn_stats(stats2[:, s], row(h_all, GROUP * g + s)).then_inc(stats2_ready, 1)
                inverse_deviation(1, g, stats2, stats2_ready, mv2_ready)
                for s in range(GROUP):
                    if not first:
                        dve.wait_ge(zt_done, GROUP * g + (s + 1 - GROUP))
                    dve.tensor_scalar(z[:, s], row(h_all, GROUP * g + s), mv[:, 1, s, 0:1], rs[:, 1, s:s + 1],
                                      ALU.subtract, ALU.mult).then_inc(z_ready, 1)

            group(0, True)
            with dve.Fori(1, GROUPS) as g:
                group(g, False)
            for j, (n, c) in enumerate(cells):
                dve.wait_ge(th_ready, j + 1)
                dve.scalar_tensor_tensor(out=xpT[:, c, n * CHUNK:(n + 1) * CHUNK], in0=half[:, j % 4], scalar=1.0,
                                         in1=ps[:, j % 4, 0:CHUNK], op0=ALU.add, op1=ALU.mult).then_inc(xp_ready, 1)

        @block.scalar
        def _(act):
            def deviations(g):
                for k in range(2):
                    act.wait_ge(ve_ready, 2 * g + k + 1)
                    act.activation(sd[:, k], ve[:, k], ACT.Sqrt).then_inc(sd_ready, 1)

            def copy_out(g):
                for s in range(GROUP):
                    act.wait_ge(zt_done, GROUP * g + s + 1)
                    src = ps[:, GROUP + s, 0:E].rearrange("q (c i t) -> q c i t", c=EC, i=2)
                    for c in range(EC):
                        cp = act.activation(pair_columns(zT, GROUP * g + s)[:, c], src[:, c, :, 0:T], ACT.Copy)
                    cp.then_inc(zt_out, 1)

            deviations(0)
            with act.Fori(1, GROUPS) as g:
                deviations(g)
                copy_out(g - 1)

            def tanh(j):
                act.wait_ge(in_done, j + 1)
                if j >= 4:
                    act.wait_ge(xp_ready, j - 3)
                act.activation(half[:, j % 4], ps[:, j % 4, 0:CHUNK], ACT.Tanh, scale=0.5).then_inc(th_ready, 1)

            for j in range(4):
                tanh(j)
            copy_out(GROUPS - 1)
            for j in range(4, len(cells)):
                tanh(j)


def load_row(sp, v_rows, vrow, t, s, row_in):
    rows = v_rows.rearrange("(g b t) (a n) -> a g b t n", g=B4, t=T, a=PARTS)
    for a in range(PARTS):
        sp.dma_start(vrow[B4 * a:B4 * a + B4, s].rearrange("q b k m -> q b (k m)"),
                     rows[a][:, :, ds(t, 1), :].rearrange("g b t n -> g b (t n)")).then_inc(row_in[s], 16)


def projections_stage(nc, ps, xpT, wt, wts_in, kn, qn, v_rows, vrow, states, row_in):
    TILES = -(-TOKENS // P)
    NV = 2 * E
    RING = 4
    LAG = 3
    PLAN = [("v", i) for i in range(TILES + LAG)]
    for n, at in enumerate((0, 3, 6)):
        PLAN.insert(at + n, ("k", n))
    PLAN.append(("k", B4 - 1))
    wk, wq, wvb, bb, ones = wt
    with Mem(nc, "projections") as m:
        kT, qT = m.sb("kT", [P, EC, TOKENS]), m.sb("qT", [P, EC, TOKENS])
        sq = m.sb("k_squares", [P, 2, CHUNK])
        nrm = m.sb("k_norm", [P, EC, TOKENS])
        vb = m.sb("vb", [P, RING, NV])
        rest = m.sb("vb_rest", [P, RING, NV])
        parts = m.sb("vb_parts", [P, RING, PARTS, NV], BF16)
        (k_done, q_done, sq_ready, n2_done, n_ready, e_ready, r_ready,
         k_ready, kc_ready, qc_ready, turned, vb_done, bx_ready, bt_ready, b_ready, v_ready, p0_ready, r1_ready,
         p1_ready, p2_ready) = (m.sem(n) for n in (
            "k_done", "q_done", "sq_ready", "n2_done",
            "n_ready", "e_ready", "r_ready", "k_ready", "kc_ready", "qc_ready", "turned", "vb_done", "bx_ready",
            "bt_ready", "b_ready", "v_ready", "p0_ready", "r1_ready", "p1_ready", "p2_ready"))
        rows_out = [m.sem(f"rows_out{s}") for s in range(RING)]
        zeroed = m.sem("zeroed")
        block = m.stack.enter_context(nc.Block())
        cells = [(n, c) for n in range(B4) for c in range(EC)]

        def cols(n):
            return slice(n * CHUNK, (n + 1) * CHUNK)

        def size(i):
            return min(P, TOKENS - i * P)

        @block.sync
        def _(sp):
            def turn(dst, src, n, ready, count):
                sp.wait_ge(ready, count)
                for h4 in range(B4):
                    sp.dma_start(dst[32 * n:32 * n + 32, h4::B4, :], src[32 * h4:32 * h4 + 32, :, cols(n)]
                                 ).then_inc(turned, 16)

            def store(i):
                sp.wait_ge(p2_ready, i + 1)
                sp.dma_start(v_rows[i * P:i * P + size(i), :], parts[0:size(i), i % RING].rearrange("p a n -> p (a n)")
                             ).then_inc(rows_out[i % RING], 16)

            for kind, i in PLAN:
                if kind == "k":
                    turn(qn, qT, i, qc_ready, EC * (i + 1))
                    if i == B4 - 1:
                        for s in range(RING):
                            sp.wait_ge(rows_out[s], 16 * len(range(s, TILES, RING)))
                        sp.wait_ge(zeroed, 3)
                        for t in range(2):
                            load_row(sp, v_rows, vrow, t, t, row_in)
                    if i >= 1:
                        turn(kn, kT, i - 1, k_ready, i)
                elif i >= LAG:
                    store(i - LAG)
            turn(kn, kT, B4 - 1, k_ready, B4)
            sp.wait_ge(turned, 16 * 2 * B4 * B4)

        @block.tensor
        def _(pe):
            pe.wait_ge(wts_in, 96)

            def product(w, src, bank, n, c):
                for k in range(EC):
                    mm = pe.matmul(ps[:, bank, 0:CHUNK], w[:, k, c * P:(c + 1) * P], src[:, k, cols(n)],
                                   start=(k == 0), stop=(k == EC - 1))
                return mm

            def values(i):
                if i >= 2:
                    pe.wait_ge(bx_ready, i - 1)
                    pe.wait_ge(v_ready, i - 1)
                for k in range(EC):
                    mm = pe.matmul(ps[0:size(i), i % 2, :], xpT[:, k, i * P:i * P + size(i)], wvb[:, k, :],
                                   start=(k == 0), stop=(k == EC - 1))
                mm.then_inc(vb_done, 1)

            def keys_queries(n):
                for c in range(EC):
                    j = EC * n + c
                    if j >= 2:
                        pe.wait_ge(qc_ready, j - 1)
                    product(wq, xpT, 2 + j % 2, n, c).then_inc(q_done, 1)
                for c in range(EC):
                    j = EC * n + c
                    if j >= 2:
                        pe.wait_ge(kc_ready, j - 1)
                    product(wk, xpT, 4 + j % 2, n, c).then_inc(k_done, 1)
                for c in range(EC):
                    j = EC * n + c
                    pe.wait_ge(sq_ready, j + 1)
                    if j >= 2:
                        pe.wait_ge(n_ready, j - 1)
                    pe.matmul(ps[:, 6 + j % 2, 0:CHUNK], ones[:], sq[:, j % 2, :], start=True, stop=True
                              ).then_inc(n2_done, 1)

            for kind, i in PLAN:
                if kind == "k":
                    keys_queries(i)
                elif i < TILES:
                    values(i)

        @block.scalar
        def _(act):
            def squash(i):
                s, rows = i % RING, size(i)
                act.wait_ge(vb_done, i + 1)
                if i >= RING:
                    act.wait_ge(r1_ready, i - RING + 1)
                    act.wait_ge(p0_ready, i - RING + 1)
                act.wait_ge(bx_ready, i + 1)
                act.activation(vb[0:rows, s, 0:E], ps[0:rows, i % 2, 0:E], ACT.Copy, scale=0.5).then_inc(v_ready, 1)
                act.activation(vb[0:rows, s, E:], vb[0:rows, s, E:], ACT.Tanh, scale=0.5).then_inc(bt_ready, 1)

            def part0(i):
                s, rows = i % RING, size(i)
                act.wait_ge(b_ready, i + 1)
                act.wait_ge(v_ready, i + 1)
                if i >= RING:
                    act.wait_ge(rows_out[s], 16 * (i // RING))
                act.activation(parts[0:rows, s, 0], vb[0:rows, s], ACT.Copy).then_inc(p0_ready, 1)

            def part1(i):
                s, rows = i % RING, size(i)
                act.wait_ge(r1_ready, i + 1)
                act.activation(parts[0:rows, s, 1], rest[0:rows, s], ACT.Copy).then_inc(p1_ready, 1)

            def keys_queries(n):
                for c in range(EC):
                    j = EC * n + c
                    act.wait_ge(q_done, j + 1)
                    act.activation(qT[:, c, cols(n)], ps[:, 2 + j % 2, 0:CHUNK], ACT.Copy, scale=0.5
                                   ).then_inc(qc_ready, 1)
                for c in range(EC):
                    j = EC * n + c
                    act.wait_ge(k_done, j + 1)
                    if j >= 2:
                        act.wait_ge(n2_done, j - 1)
                    act.activation(sq[:, j % 2], ps[:, 4 + j % 2, 0:CHUNK], ACT.Square, scale=0.5).then_inc(sq_ready, 1)
                    act.activation(kT[:, c, cols(n)], ps[:, 4 + j % 2, 0:CHUNK], ACT.Copy, scale=0.5
                                   ).then_inc(kc_ready, 1)
                for c in range(EC):
                    j = EC * n + c
                    act.wait_ge(n2_done, j + 1)
                    act.activation(nrm[:, c, cols(n)], ps[:, 6 + j % 2, 0:CHUNK], ACT.Sqrt).then_inc(n_ready, 1)

            for kind, i in PLAN:
                if kind == "k":
                    keys_queries(i)
                    continue
                for step, tile in ((squash, i), (part0, i - 1), (part1, i - 2)):
                    if 0 <= tile < TILES:
                        step(tile)

        @block.vector
        def _(dve):
            def biased(i):
                s, rows = i % RING, size(i)
                dve.wait_ge(vb_done, i + 1)
                if i >= RING:
                    dve.wait_ge(r1_ready, i - RING + 1)
                    dve.wait_ge(p0_ready, i - RING + 1)
                dve.scalar_tensor_tensor(out=vb[0:rows, s, E:], in0=ps[0:rows, i % 2, E:], scalar=0.5, in1=bb[0:rows],
                                         op0=ALU.mult, op1=ALU.add).then_inc(bx_ready, 1)

            def sigmoid(i):
                s, rows = i % RING, size(i)
                dve.wait_ge(bt_ready, i + 1)
                dve.tensor_scalar(vb[0:rows, s, E:], vb[0:rows, s, E:], 0.5, 0.5, ALU.mult, ALU.add).then_inc(b_ready, 1)

            def rest0(i):
                s, rows = i % RING, size(i)
                dve.wait_ge(p0_ready, i + 1)
                if i >= RING:
                    dve.wait_ge(p2_ready, i - RING + 1)
                dve.tensor_tensor(rest[0:rows, s], vb[0:rows, s], parts[0:rows, s, 0], ALU.subtract).then_inc(r1_ready, 1)

            def normalised(n):
                dve.wait_ge(n_ready, EC * (n + 1))
                dve.tensor_scalar(nrm[:, :, cols(n)], nrm[:, :, cols(n)], 1e-6, None, ALU.add).then_inc(e_ready, 1)
                dve.wait_ge(e_ready, n + 1)
                dve.reciprocal(nrm[:, :, cols(n)], nrm[:, :, cols(n)]).then_inc(r_ready, 1)
                dve.wait_ge(r_ready, n + 1)
                dve.wait_ge(kc_ready, EC * (n + 1))
                dve.tensor_tensor(kT[:, :, cols(n)], kT[:, :, cols(n)], nrm[:, :, cols(n)], ALU.mult
                                  ).then_inc(k_ready, 1)

            for kind, i in PLAN:
                if kind == "k":
                    if i >= 1:
                        normalised(i - 1)
                    continue
                for step, tile in ((biased, i), (sigmoid, i - 1), (rest0, i - 2)):
                    if 0 <= tile < TILES:
                        step(tile)
            normalised(B4 - 1)

        @block.gpsimd
        def _(pool):
            pool.memset(vrow[:].rearrange("q s b k m -> q (s b k m)"), 0.0).then_inc(zeroed, 1)
            for S in states:
                pool.memset(S[:], 0.0).then_inc(zeroed, 1)
            pool.wait_ge(zeroed, 3)
            for i in range(TILES):
                s, rows = i % RING, size(i)
                pool.wait_ge(p1_ready, i + 1)
                pool.tensor_tensor(parts[0:rows, s, 2], rest[0:rows, s], parts[0:rows, s, 1], ALU.subtract
                                   ).then_inc(p2_ready, 1)


def scan_stage(nc, d, ps, kn, qn, v_rows, o_rows, vrow, S, const, const_in, row_in, later):
    HALF = B8 // 2
    N = HALF * E
    LAST = T - 1
    OWN = HALF - 2
    with Mem(nc, "scan") as m:
        sel, neg, osel = const
        Pb = [m.sb(f"s_times_kn{a}", [P, N]) for a in range(2)]
        Qb = [m.sb(f"s_times_q{a}", [P, N]) for a in range(2)]
        Tb = [m.sb(f"beta_s{a}", [P, N]) for a in range(2)]
        bsb = [m.sb(f"beta_sb{a}", [P, N]) for a in range(2)]
        obuf = m.sb("o_buf", [P, 2, 2, E])
        p_ready, r_done, u_ready, a_ready, s_ready, q_ready, q_last_ready, o_done, t_ready = (
            [m.sem(f"{n}{a}") for a in range(2)] for n in (
                "p_ready", "r_done", "u_ready", "a_ready", "s_ready", "q_ready", "q_last_ready", "o_done",
                "t_ready"))
        beta_done, beta_ready, v1_done, o_out = (m.sem(n) for n in ("beta_done", "beta_ready", "v1_done", "o_out"))
        stored = [m.sem("stored0"), m.sem("stored1")]
        block = m.stack.enter_context(nc.Block())

        def st(ap):
            return ap.rearrange("q (b h i) -> q b h i", b=HALF, h=NH_CELL)

        def vec(ap, t, a):
            v = ap[:].rearrange("q h (b t) -> q b h t", t=T)[:, HALF * a:HALF * a + HALF, :, ds(t, 1)]
            return v.broadcast_to([P, HALF, NH_CELL, NCELL])

        def D(a):
            return ps[:, 2 * a:2 * a + 2, :].rearrange("q n (b h i) -> q (n b) h i", h=NH_CELL, i=NCELL)

        def cycles(eng, cycle, first=4, last=LAST + 1):
            for c in range(first):
                cycle(c, c % 2)
            with eng.Fori(first // 2, LAST // 2) as i:
                for s in range(2):
                    cycle(2 * i + s, s, i)
            for c in range(2 * (LAST // 2), last + 1):
                cycle(c, c % 2)

        @block.sync
        def _(sp):
            for t, src, arrived in later:
                sp.dma_start(t[:], d[src]).then_inc(arrived, 16)

            def store(t, s):
                for k in range(4):
                    sp.dma_start(o_rows.rearrange("(g k b) t n -> k g b t n", g=B4, k=4)[k][:, :, ds(t, 1), :]
                                 .rearrange("g b t n -> g b (t n)"), obuf[32 * k:32 * k + 4, s]).then_inc(stored[s], 16)

            def cycle(c, s, i=None):
                if i is not None or c >= 2:
                    sp.wait_ge(o_out, c - 1)
                    store(c - 2, s)
                if i is not None or c + 2 <= LAST:
                    sp.wait_ge(v1_done, c + 1)
                    load_row(sp, v_rows, vrow, c + 2, s, row_in)

            cycles(sp, cycle, last=LAST + 2)
            for s in range(2):
                sp.wait_ge(stored[s], 16 * 4 * (T // 2))

        @block.gpsimd
        def _(pool):
            def cycle(c, s, i=None):
                for a in range(2):
                    if i is not None or c <= LAST:
                        pool.wait_ge(beta_ready, 2 * c + 1 + a)
                    if i is not None or c > 0:
                        pool.wait_ge(s_ready[a], c)
                    if i is not None or c <= LAST:
                        pool.tensor_tensor(Tb[a][:], bsb[a][:], S[a][:], ALU.mult).then_inc(t_ready[a], 1)
                    if i is not None or c >= 1:
                        if i is not None or c >= 2:
                            pool.wait_ge(o_done[a], c - 1)
                        pool.tensor_tensor(st(Qb[a][:])[:, OWN:], st(S[a][:])[:, OWN:], vec(qn, c - 1, a)[:, OWN:],
                                           ALU.mult).then_inc(q_last_ready[a], 1)

            cycles(pool, cycle)

        @block.scalar
        def _(act):
            def beta_copy(a, c, first):
                act.wait_ge(beta_done, 2 * c + 1 + a)
                if not first:
                    act.wait_ge(t_ready[a], c)
                act.activation(bsb[a][:], ps[:, 4:6, :].rearrange("q n x -> q (n x)"), ACT.Copy).then_inc(beta_ready, 1)

            def tanh(a, n, first):
                act.wait_ge(a_ready[a], n)
                if not first:
                    act.wait_ge(q_last_ready[a], n - 1)
                act.activation(S[a][:], Tb[a][:], ACT.Tanh).then_inc(s_ready[a], 1)

            def cycle(c, s, i=None):
                if i is not None or c >= 2:
                    act.wait_ge(o_done[1], c - 1)
                    if i is not None or c >= 4:
                        stores = (c // 2 if i is None else i) - 1
                        act.wait_ge(stored[s], 64 * stores)
                    act.activation(obuf[:, s].rearrange("q b m -> q (b m)"), ps[:, 6 + s, :], ACT.Copy
                                   ).then_inc(o_out, 1)
                if i is not None or 1 <= c <= LAST + 1:
                    tanh(1, c, i is None and c == 1)
                if i is not None or c <= LAST:
                    beta_copy(1, c, i is None and c == 0)
                    tanh(0, c + 1, i is None and c == 0)
                if i is not None or c < LAST:
                    beta_copy(0, c + 1, False)

            beta_copy(0, 0, True)
            cycles(act, cycle, last=LAST + 2)

        @block.vector
        def _(dve):
            def s_kn(a, c, first):
                if not first:
                    dve.wait_ge(s_ready[a], c)
                dve.tensor_tensor(st(Pb[a][:]), st(S[a][:]), vec(kn, c, a), ALU.mult).then_inc(p_ready[a], 1)

            def s_q(a, t, first):
                dve.wait_ge(s_ready[a], t + 1)
                if not first:
                    dve.wait_ge(o_done[a], t)
                dve.tensor_tensor(st(Qb[a][:])[:, 0:OWN], st(S[a][:])[:, 0:OWN], vec(qn, t, a)[:, 0:OWN], ALU.mult
                                  ).then_inc(q_ready[a], 1)

            def update(a, t):
                dve.wait_ge(r_done[a], t + 1)
                dve.tensor_tensor(D(a), D(a), vec(kn, t, a), ALU.mult).then_inc(u_ready[a], 1)
                dve.wait_ge(u_ready[a], t + 1)
                dve.wait_ge(t_ready[a], t + 1)
                dve.tensor_tensor(Tb[a][:], ps[:, 2 * a:2 * a + 2, :].rearrange("q n x -> q (n x)"), Tb[a][:],
                                  ALU.add).then_inc(a_ready[a], 1)

            def cycle(c, s, i=None):
                front, back = i is not None or c <= LAST, i is not None or c >= 1
                if front:
                    s_kn(0, c, i is None and c == 0)
                if back:
                    s_q(0, c - 1, i is None and c == 1)
                    update(1, c - 1)
                if front:
                    update(0, c)
                    s_kn(1, c, i is None and c == 0)
                if back:
                    s_q(1, c - 1, i is None and c == 1)

            cycles(dve, cycle)

        @block.tensor
        def _(pe):
            pe.wait_ge(const_in, 48)

            def rows(kind, a, s, bank, more):
                for n in range(2):
                    b = HALF * a + 2 * n
                    mm = pe.matmul(ps[:, bank + n, :].rearrange("q (b m) -> q b m", b=2), sel[:],
                                   vrow[:, s, b:b + 2, kind, :], start=True, stop=not more)
                return mm

            def sums(a):
                for n in range(2):
                    mm = pe.matmul(ps[:, 2 * a + n, :], neg[:], Pb[a][:, 512 * n:512 * n + 512], start=False, stop=True)
                mm.then_inc(r_done[a], 1)

            def outs(a, s):
                for n in range(2):
                    k = 2 * a + n
                    mm = pe.matmul(ps[32 * k:32 * k + 32, 6 + s, :], osel[:], Qb[a][:, 512 * n:512 * n + 512],
                                   start=True, stop=True)
                mm.then_inc(o_done[a], 1)

            def cycle(c, s, i=None):
                front, back = i is not None or c <= LAST, i is not None or c >= 1
                if front:
                    pe.wait_ge(p_ready[0], c + 1)
                    sums(0)
                    pe.wait_ge(beta_ready, 2 * c + 1)
                    rows(1, 1, s, 4, False).then_inc(beta_done, 1)
                if back:
                    pe.wait_ge(q_ready[0], c)
                    pe.wait_ge(q_last_ready[0], c)
                    if i is not None or c >= 3:
                        pe.wait_ge(o_out, c - 2)
                    outs(0, 1 - s)
                if front:
                    if back:
                        pe.wait_ge(a_ready[1], c)
                    rows(0, 1, s, 2, True).then_inc(v1_done, 1)
                if i is not None or c < LAST:
                    passes = (c + 1) // 2 if i is None else i + s
                    pe.wait_ge(row_in[1 - s], 48 * passes + 48)
                    pe.wait_ge(a_ready[0], c + 1)
                    rows(0, 0, 1 - s, 0, True)
                    pe.wait_ge(beta_ready, 2 * c + 2)
                    rows(1, 0, 1 - s, 4, False).then_inc(beta_done, 1)
                if front:
                    pe.wait_ge(p_ready[1], c + 1)
                    sums(1)
                if back:
                    pe.wait_ge(q_ready[1], c)
                    pe.wait_ge(q_last_ready[1], c)
                    outs(1, 1 - s)

            pe.wait_ge(row_in[0], 48)
            rows(1, 0, 0, 4, False).then_inc(beta_done, 1)
            rows(0, 0, 0, 0, True)
            cycles(pe, cycle)


def row(ap, p):
    return ap[:, ds(p, 1), :].rearrange("q a e -> q (a e)")


def ring(eng, step, count=PAIRS):
    for s in range(2):
        step(s, s, True)
    with eng.Fori(1, count // 2) as i:
        for s in range(2):
            step(2 * i + s, s, False)


def cell_output_stage(nc, ps, o_pad, h_all, xh_all, xnT, ident, wo, g1, w_in, x_slots):
    GROUP = 4
    GROUPS = PAIRS // GROUP
    CT, Y, XT = 0, 2, 6
    with Mem(nc, "cell_output") as m:
        o = m.sb("o_all", [P, PAIRS, E])
        th, sq = m.sb("o_tanh", [P, PAIRS, E]), m.sb("o_squares", [P, PAIRS, E])
        cell = m.sb("cell", [P, GROUP, E])
        cellT = m.sb("cellT", [P, GROUP, E])
        stats, mv = m.sb("h1_stats", [P, GROUP, 6]), m.sb("h1_mv", [P, GROUP, 2])
        ve, sd, rs, shift, vr, ms, rm, rr = (m.sb(n, [P, GROUP]) for n in (
            "h1_ve", "h1_sd", "h1_rs", "h1_shift", "h1_vr", "xh_ms", "xh_rms", "xh_rrms"))
        xn = m.sb("xn", [P, GROUP, E])
        zero = m.sb("empty_slot", [P, E])
        (zeroed, zero_ready, emptied, th_ready, c_ready, ct_done, ct_out, y_done, h_ready, st_ready,
         mv_ready, ve_ready, sd_ready, rs_ready, shift_ready, xh_ready, vr_ready, ms_ready, rm_ready, rr_ready, xn_ready,
         xt_done,
         xt_out) = (
            m.sem(n) for n in (
                "zeroed", "zero_ready", "emptied", "th_ready", "c_ready", "ct_done", "ct_out",
                "y_done", "h_ready", "st_ready", "mv_ready", "ve_ready", "sd_ready", "rs_ready",
                "shift_ready", "xh_ready", "vr_ready", "ms_ready", "rm_ready", "rr_ready", "xn_ready", "xt_done",
                "xt_out"))
        o_in = [m.sem("o_in_first"), m.sem("o_in_rest")]
        block = m.stack.enter_context(nc.Block())

        def bank(first_bank, s):
            return ps[:, first_bank + s % 2, 0:E]

        @block.sync
        def _(sp):
            images = o_pad.rearrange("(p k) t m -> k t p m", k=2)
            for g in range(GROUPS):
                sp.wait_ge(zeroed, g + 1)
                for k in range(2):
                    sp.dma_start(o[SLOT * k:SLOT * k + T, g * GROUP:(g + 1) * GROUP],
                                 images[k][:, g * GROUP:(g + 1) * GROUP]).then_inc(o_in[min(g, 1)], 16)
            sp.wait_ge(zero_ready, 1)
            sp.dma_start(x_slots.rearrange("(n q) e -> q n e", q=P),
                         zero[:].rearrange("q (a e) -> q a e", a=1).broadcast_to([P, TILES, E])).then_inc(emptied, 16)
            sp.wait_ge(emptied, 16)

        @block.scalar
        def _(act):
            def tanh(g):
                act.wait_ge(o_in[min(g, 1)], 32 if g == 0 else 32 * (GROUPS - 1))
                for s in range(GROUP):
                    act.activation(row(sq, GROUP * g + s), row(o, GROUP * g + s), ACT.Square)
                    act.activation(row(th, GROUP * g + s), row(o, GROUP * g + s), ACT.Tanh, scale=0.5
                                   ).then_inc(th_ready, 1)

            def copy_cell(g, first):
                for s in range(GROUP):
                    act.wait_ge(ct_done, GROUP * g + s + 1)
                    if not first:
                        act.wait_ge(y_done, GROUP * g + (s + 1 - GROUP))
                    act.activation(cellT[:, s], bank(CT, s), ACT.Copy, scale=0.5).then_inc(ct_out, 1)

            def copy_xn(g):
                for s in range(GROUP):
                    act.wait_ge(xt_done, GROUP * g + s + 1)
                    src = bank(XT, s).rearrange("q (c i t) -> q c i t", c=EC, i=2)
                    for c in range(EC):
                        cp = act.activation(pair_columns(xnT, GROUP * g + s)[:, c], src[:, c, :, 0:T], ACT.Copy,
                                            scale=g1[:, c:c + 1])
                    cp.then_inc(xt_out, 1)

            def roots(g):
                act.wait_ge(ve_ready, g + 1)
                act.activation(sd[:], ve[:], ACT.Sqrt).then_inc(sd_ready, 1)
                act.wait_ge(ms_ready, g + 1)
                act.activation(rm[:], ms[:], ACT.Sqrt).then_inc(rm_ready, 1)

            def normalised(g):
                act.wait_ge(shift_ready, g + 1)
                for s in range(GROUP):
                    act.activation(row(xh_all, GROUP * g + s), row(h_all, GROUP * g + s), ACT.Identity,
                                   scale=rs[:, s:s + 1], bias=shift[:, s:s + 1]).then_inc(xh_ready, 1)

            tanh(0)
            copy_cell(0, True)
            tanh(1)
            tanh(2)
            copy_cell(1, False)
            tanh(3)
            roots(0)
            normalised(0)
            act.wait_ge(w_in, 32)
            with act.Fori(1, GROUPS - 1) as g:
                copy_xn(g - 1)
                copy_cell(g + 1, False)
                roots(g)
                normalised(g)
            copy_xn(GROUPS - 2)
            roots(GROUPS - 1)
            normalised(GROUPS - 1)
            copy_xn(GROUPS - 1)

        @block.tensor
        def _(pe):
            def turn(g, first):
                for s in range(GROUP):
                    pe.wait_ge(c_ready, GROUP * g + s + 1)
                    if not first or s >= 2:
                        pe.wait_ge(ct_out, GROUP * g + s - 1)
                    for c in range(EC):
                        mm = pe.transpose(bank(CT, s)[:, c * P:(c + 1) * P], cell[:, s, c * P:(c + 1) * P], ident[:])
                    mm.then_inc(ct_done, 1)

            def product(g, first):
                for s in range(GROUP):
                    pe.wait_ge(ct_out, GROUP * g + s + 1)
                    if not first:
                        pe.wait_ge(h_ready, GROUP * g + (s + 1 - GROUP))
                    for c in range(EC):
                        mm = pe.matmul(ps[:, Y + s, 0:E], cellT[:, s, c * P:(c + 1) * P], wo[:, c, :],
                                       start=(c == 0), stop=(c == EC - 1))
                    mm.then_inc(y_done, 1)

            def turn_xn(g, first):
                for s in range(GROUP):
                    pe.wait_ge(xn_ready, GROUP * g + s + 1)
                    if not first or s >= 2:
                        pe.wait_ge(xt_out, GROUP * g + s - 1)
                    for c in range(EC):
                        mm = pe.transpose(bank(XT, s)[:, c * P:(c + 1) * P], xn[:, s, c * P:(c + 1) * P], ident[:])
                    mm.then_inc(xt_done, 1)

            pe.wait_ge(w_in, 32)
            turn(0, True)
            product(0, True)
            turn(1, False)
            product(1, False)
            turn_xn(0, True)
            with pe.Fori(2, GROUPS) as g:
                turn(g, False)
                product(g, False)
                turn_xn(g - 1, False)
            turn_xn(GROUPS - 1, False)

        @block.gpsimd
        def _(pool):
            for g in range(GROUPS):
                pool.memset(o[:, g * GROUP:(g + 1) * GROUP].rearrange("q a e -> q (a e)"), 0.0).then_inc(zeroed, 1)

        @block.vector
        def _(dve):
            dve.memset(zero[:], 0.0).then_inc(zero_ready, 1)

            def alone(sem, value):
                dve.wait_ge(zero_ready, 1)
                dve.wait_ge(sem, value)

            def front(g, first):
                for s in range(GROUP):
                    dve.wait_ge(th_ready, GROUP * g + s + 1)
                    if not first:
                        dve.wait_ge(ct_done, GROUP * g + (s + 1 - GROUP))
                    dve.scalar_tensor_tensor(out=cell[:, s], in0=row(th, GROUP * g + s), scalar=1.0,
                                             in1=row(sq, GROUP * g + s), op0=ALU.add, op1=ALU.mult).then_inc(c_ready, 1)

            def back(g, first):
                for s in range(GROUP):
                    dve.wait_ge(y_done, GROUP * g + s + 1)
                    dve.tensor_tensor(row(h_all, GROUP * g + s), ps[:, Y + s, 0:E], row(h_all, GROUP * g + s), ALU.add
                                      ).then_inc(h_ready, 1)
                alone(h_ready, GROUP * g + GROUP)
                for s in range(GROUP):
                    dve.bn_stats(stats[:, s], row(h_all, GROUP * g + s)).then_inc(st_ready, 1)
                alone(st_ready, GROUP * g + GROUP)
                for s in range(GROUP):
                    dve.bn_aggr(mv[:, s], stats[:, s]).then_inc(mv_ready, 1)
                dve.wait_ge(mv_ready, GROUP * g + GROUP)
                dve.tensor_scalar(ve[:], mv[:, :, 1], EPS_LN, None, ALU.add).then_inc(ve_ready, 1)
                dve.wait_ge(sd_ready, g + 1)
                if not first:
                    dve.wait_ge(xh_ready, GROUP * g)
                dve.reciprocal(rs[:], sd[:]).then_inc(rs_ready, 1)
                dve.wait_ge(rs_ready, g + 1)
                dve.tensor_tensor(vr[:], mv[:, :, 1], rs[:], ALU.mult).then_inc(vr_ready, 1)
                dve.scalar_tensor_tensor(out=shift[:], in0=mv[:, :, 0], scalar=-1.0, in1=rs[:], op0=ALU.mult,
                                         op1=ALU.mult).then_inc(shift_ready, 1)
                dve.wait_ge(vr_ready, 2 * g + 1)
                dve.tensor_tensor(vr[:], vr[:], rs[:], ALU.mult).then_inc(vr_ready, 1)
                dve.wait_ge(vr_ready, 2 * g + 2)
                dve.tensor_scalar(ms[:], vr[:], EPS_RMS, None, ALU.add).then_inc(ms_ready, 1)
                dve.wait_ge(rm_ready, g + 1)
                dve.reciprocal(rr[:], rm[:]).then_inc(rr_ready, 1)
                dve.wait_ge(rr_ready, 2 * g + 1)
                dve.tensor_tensor(rr[:], rr[:], rs[:], ALU.mult).then_inc(rr_ready, 1)
                dve.wait_ge(rr_ready, 2 * g + 2)
                for s in range(GROUP):
                    if not first:
                        dve.wait_ge(xt_done, GROUP * g + (s + 1 - GROUP))
                    dve.tensor_scalar(xn[:, s], row(h_all, GROUP * g + s), mv[:, s, 0:1], rr[:, s:s + 1],
                                      ALU.subtract, ALU.mult).then_inc(xn_ready, 1)

            front(0, True)
            front(1, False)
            back(0, True)
            with dve.Fori(1, GROUPS - 1) as g:
                front(g + 1, False)
                back(g, False)
            back(GROUPS - 1, False)


def rotary_stage(nc, ps, xnT, qr, kr, w, cos, sin, w_in):
    NW = CHUNK
    cells = [(n, c) for n in range(TOKENS // NW) for c in range(EC)]
    with Mem(nc, "rotary") as m:
        t1, t2 = m.sb("rope_cos", [P, 2, 2, NW]), m.sb("rope_sin", [P, 2, 2, NW])
        mm_done, t1_ready, t2_ready, r_ready = (m.sem(n) for n in (
            "mm_done", "t1_ready", "t2_ready", "r_ready"))
        block = m.stack.enter_context(nc.Block())

        @block.tensor
        def _(pe):
            pe.wait_ge(w_in, 96)
            for j, (n, c) in enumerate(cells):
                if j >= 2:
                    pe.wait_ge(t2_ready, 2 * j - 2)
                for k in range(4):
                    for e in range(EC):
                        mm = pe.matmul(ps[:, 4 * (j % 2) + k, 0:NW], w[k][:, e, c * P:(c + 1) * P],
                                       xnT[:, e, n * NW:(n + 1) * NW], start=(e == 0), stop=(e == EC - 1))
                mm.then_inc(mm_done, 1)

        @block.vector
        def _(dve):
            dve.wait_ge(w_in, 96)

            def tab(t):
                return t[:].rearrange("q (a t) -> q a t", a=1).broadcast_to([P, NW // T, T])

            for j, (n, c) in enumerate(cells):
                dve.wait_ge(mm_done, j + 1)
                if j >= 2:
                    dve.wait_ge(r_ready, 2 * j - 2)
                for k in range(2):
                    for t, table, bank, ready in ((t1, cos, k, t1_ready), (t2, sin, 2 + k, t2_ready)):
                        dve.tensor_tensor(t[:, j % 2, k].rearrange("q (a t) -> q a t", t=T),
                                          ps[:, 4 * (j % 2) + bank, 0:NW].rearrange("q (a t) -> q a t", t=T),
                                          tab(table), ALU.mult).then_inc(ready, 1)

        @block.gpsimd
        def _(pool):
            for j, (n, c) in enumerate(cells):
                for k, dst in enumerate((qr, kr)):
                    pool.wait_ge(t1_ready, 2 * j + k + 1)
                    pool.wait_ge(t2_ready, 2 * j + k + 1)
                    pool.tensor_tensor(dst[:, c, n * NW:(n + 1) * NW], t1[:, j % 2, k], t2[:, j % 2, k], ALU.add
                                       ).then_inc(r_ready, 1)
            pool.wait_ge(r_ready, 2 * len(cells))


def attention_stage(nc, d, ps, xnT, qr, kr, wv, wo, causal, hmask, c_in, h_all, xh_all, ident, hh_rows, r_rows, hh,
                    r, hh_in, r_in, later):
    W = HG * T
    with Mem(nc, "attention") as m:
        q = m.sb("q_pair", [P, 2, EC, P])
        x = m.sb("xn_pair", [P, 2, EC, 2, SLOT])
        km = m.sb("k_masked", [P, 2, EC, 2, HG, T])
        v2 = m.sb("v_blocks", [P, 2, 2, HEADS // 2, 2, DH])
        sc = m.sb("scores", [P, 2, HEADS, T])
        pr = m.sb("probs", [P, 2, HEADS, SLOT])
        pt = m.sb("probs_t", [P, 2, HEADS // 2, P])
        mx, sm, ri = m.sb("max", [P, 2, HEADS]), m.sb("sum", [P, 2, HEADS]), m.sb("inv_sum", [P, 2, HEADS])
        at = m.sb("attn", [P, 2, E])
        atT = m.sb("attnT", [P, 2, E])
        stored = [m.sem("stored_first"), m.sem("stored_rest")]
        emptied = m.sem("emptied")
        (zeroed, x_ready, q_ready, k_ready, v_done, v_out, s_done, sc_ready, mx_ready, sub_ready, p_ready,
         sum_ready, ri_ready, pt_done, pt_out, pv_done, at_ready, at_done, at_out, wo_done, hh_ready,
         r_ready) = (m.sem(n) for n in (
            "zeroed", "x_ready", "q_ready", "k_ready", "v_done", "v_out", "s_done", "sc_ready", "mx_ready",
            "sub_ready", "p_ready", "sum_ready", "ri_ready", "pt_done", "pt_out", "pv_done", "at_ready", "at_done",
            "at_out", "wo_done", "hh_ready", "r_ready"))
        block = m.stack.enter_context(nc.Block())
        PT, SC, VB, PV, AT, WO = 0, 2, 4, 5, 6, 7

        def cycles(eng, cycle):
            for c in range(4):
                cycle(c, c % 2, False)
            with eng.Fori(2, PAIRS // 2) as i:
                for s in range(2):
                    cycle(2 * i + s, s, True)
            cycle(PAIRS, 0, False)
            cycle(PAIRS + 1, 1, False)

        def has(c, loop, lag):
            return loop or 0 <= c - lag < PAIRS

        @block.sync
        def _(sp):
            for t, src, arrived in later:
                sp.dma_start(t[:], d[src]).then_inc(arrived, 16)

            def store(p, done):
                sp.wait_ge(r_ready, p + 1)
                for src, rows in ((xh_all, hh_rows), (h_all, r_rows)):
                    for k in range(2):
                        image = rows.rearrange("(n t) e -> n t e", t=T)[ds(2 * p + k, 1)]
                        sp.dma_start(image.rearrange("a t e -> (a t) e"),
                                     row(src, p)[SLOT * k:SLOT * k + T]).then_inc(done, 16)

            def load(tile0, tile1, rows, hh_in):
                for dst, src, arrived in ((hh, hh_rows, hh_in), (r, r_rows, r_in)):
                    part = src[tile0 * P:tile0 * P + (tile1 - tile0 - 1) * P + rows]
                    sp.dma_start(dst[0:rows, tile0:tile1], part.rearrange("(n q) e -> q n e", q=rows)
                                 ).then_inc(arrived, 16)

            with sp.Fori(0, PAIRS_FIRST) as p:
                store(p, stored[0])
            sp.wait_ge(stored[0], 64 * PAIRS_FIRST)
            load(0, NT_FIRST, P, hh_in[0])
            with sp.Fori(PAIRS_FIRST, PAIRS) as p:
                store(p, stored[1])
            sp.wait_ge(stored[1], 64 * (PAIRS - PAIRS_FIRST))
            load(NT_FIRST, NT - 1, P, hh_in[1])
            load(NT - 1, NT, LAST_ROWS, hh_in[1])

        @block.gpsimd
        def _(pool):
            pool.memset(x[:].rearrange("q s c i t -> q (s c i t)"), 0.0).then_inc(emptied, 1)
            pool.memset(q[:].rearrange("q s c n -> q (s c n)"), 0.0).then_inc(emptied, 1)
            pool.wait_ge(c_in, 64)
            pool.wait_ge(emptied, 2)

            def prepare(p, s, first):
                if not first:
                    pool.wait_ge(s_done, p - 1)
                pool.tensor_copy(q[:, s].rearrange("q c (i t) -> q c i t", i=2)[:, :, :, 0:T], pair_columns(qr, p)
                                 ).then_inc(q_ready, 1)
                for c in range(EC):
                    for k in range(2):
                        keys = kr[:, c, ds(2 * T * p + T * k, T)].rearrange("q (a t) -> q a t", a=1)
                        mask = hmask[:].rearrange("q (h a) -> q h a", a=1)
                        mul = pool.tensor_tensor(km[:, s, c, k], keys.broadcast_to([P, HG, T]),
                                                 mask.broadcast_to([P, HG, T]), ALU.mult)
                mul.then_inc(k_ready, 1)
                if not first:
                    pool.wait_ge(v_done, p - 1)
                pool.tensor_copy(x[:, s, :, :, 0:T], pair_columns(xnT, p)).then_inc(x_ready, 1)

            ring(pool, prepare)

        @block.tensor
        def _(pe):
            pe.wait_ge(c_in, 64)

            def cycle(c, s, loop):
                if has(c, loop, 2):
                    pe.wait_ge(at_ready, c - 1)
                    if loop or c > 2:
                        pe.wait_ge(at_out, c - 2)
                    for e in range(EC):
                        mm = pe.transpose(ps[:, AT, e * P:(e + 1) * P], at[:, s, e * P:(e + 1) * P], ident[:])
                    mm.then_inc(at_done, 1)
                if has(c, loop, 1):
                    pe.wait_ge(p_ready, c)
                    if loop or c > 1:
                        pe.wait_ge(pt_out, c - 1)
                    for h in range(HEADS // 2):
                        mm = pe.transpose(ps[:, PT + h // 4, (h % 4) * P:(h % 4 + 1) * P],
                                          pr[:, 1 - s, 2 * h:2 * h + 2, :].rearrange("q h k -> q (h k)"), ident[:])
                    mm.then_inc(pt_done, 1)
                if has(c, loop, 0):
                    pe.wait_ge(q_ready, c + 1)
                    pe.wait_ge(k_ready, c + 1)
                    if loop or c > 0:
                        pe.wait_ge(sc_ready, c)
                    for e in range(EC):
                        for k in range(2):
                            mm = pe.matmul(ps[SLOT * k:SLOT * k + SLOT, SC + e, 0:W],
                                           q[:, s, e, SLOT * k:SLOT * k + SLOT],
                                           km[:, s, e, k].rearrange("q h t -> q (h t)"), start=True, stop=True)
                    mm.then_inc(s_done, 1)
                    pe.wait_ge(x_ready, c + 1)
                    if loop or c > 0:
                        pe.wait_ge(v_out, c)
                    for k in range(2):
                        for e in range(EC):
                            for a in range(2):
                                mm = pe.matmul(ps[SLOT * a:SLOT * a + SLOT, VB, k * P:(k + 1) * P], x[:, s, e, k, :],
                                               wv[:, e, a * P:(a + 1) * P], start=(e == 0), stop=(e == EC - 1))
                    mm.then_inc(v_done, 1)
                if has(c, loop, 1):
                    pe.wait_ge(pt_out, c)
                    if loop or c > 1:
                        pe.wait_ge(at_ready, c - 1)
                    for k in range(2):
                        for h in range(HEADS // 2):
                            mm = pe.matmul(ps[SLOT * k:SLOT * k + SLOT, PV, 32 * h:32 * h + 32],
                                           pt[:, 1 - s, h, SLOT * k:SLOT * k + SLOT],
                                           v2[:, 1 - s, k, h].rearrange("q a e -> q (a e)"), start=True, stop=True)
                    mm.then_inc(pv_done, 1)
                if has(c, loop, 2):
                    pe.wait_ge(at_out, c - 1)
                    if loop or c > 2:
                        pe.wait_ge(hh_ready, c - 2)
                    for e in range(EC):
                        mm = pe.matmul(ps[:, WO, 0:E], atT[:, s, e * P:(e + 1) * P], wo[:, e, :],
                                       start=(e == 0), stop=(e == EC - 1))
                    mm.then_inc(wo_done, 1)

            cycles(pe, cycle)

        @block.scalar
        def _(act):
            def cycle(c, s, loop):
                if has(c, loop, 2):
                    act.wait_ge(at_done, c - 1)
                    if loop or c > 3:
                        act.wait_ge(wo_done, c - 2)
                    act.activation(atT[:, s], ps[:, AT, 0:E], ACT.Copy).then_inc(at_out, 1)
                if has(c, loop, 1):
                    act.wait_ge(pt_done, c)
                    act.activation(pt[:, 1 - s].rearrange("q h k -> q (h k)"),
                                   ps[:, PT:PT + 2, :].rearrange("q n x -> q (n x)"), ACT.Copy).then_inc(pt_out, 1)
                if has(c, loop, 0):
                    act.wait_ge(v_done, c + 1)
                    if loop or c > 1:
                        act.wait_ge(pv_done, c - 1)
                    else:
                        act.wait_ge(zeroed, 2)
                    for k in range(2):
                        rows = slice(SLOT * k, SLOT * k + SLOT)
                        src = ps[rows, VB, 0:E].rearrange("q (i h e) -> q i h e", i=2, e=DH)
                        cp = act.activation(v2[rows, s, :, :, k, :], src, ACT.Copy)
                    cp.then_inc(v_out, 1)
                    act.wait_ge(sub_ready, c + 1)
                    if loop or c > 1:
                        act.wait_ge(pt_done, c - 1)
                        act.wait_ge(sum_ready, c - 1)
                    act.activation(pr[:, s, :, 0:T], sc[:, s], ACT.Exp, scale=float(DH) ** -0.5).then_inc(p_ready, 1)

            cycles(act, cycle)

        @block.vector
        def _(dve):
            dve.memset(v2[:].rearrange("q s i h a e -> q (s i h a e)"), 0.0).then_inc(zeroed, 1)
            dve.memset(pr[:].rearrange("q s h k -> q (s h k)"), 0.0).then_inc(zeroed, 1)
            dve.memset(hh[LAST_ROWS:P, NT - 1], 0.0)
            dve.wait_ge(c_in, 64)

            def per_head(t, s, n):
                return t[:, s].rearrange("q (h a) -> q h a", a=1).broadcast_to([P, HEADS, n])

            def cycle(c, s, loop):
                if has(c, loop, 1):
                    dve.wait_ge(p_ready, c)
                    if loop or c > 2:
                        dve.wait_ge(ri_ready, c - 2)
                    dve.tensor_reduce(sm[:, 1 - s], pr[:, 1 - s, :, 0:T], AX.X, ALU.add).then_inc(sum_ready, 1)
                    dve.wait_ge(sum_ready, c)
                    dve.reciprocal(ri[:, 1 - s], sm[:, 1 - s]).then_inc(ri_ready, 1)
                if has(c, loop, 0):
                    dve.wait_ge(s_done, c + 1)
                    if loop or c > 1:
                        dve.wait_ge(p_ready, c - 1)
                    mask = causal[:].rearrange("q (a t) -> q a t", a=1).broadcast_to([P, HG, T])
                    for e in range(EC):
                        add = dve.tensor_tensor(sc[:, s, HG * e:HG * e + HG],
                                                ps[:, SC + e, 0:W].rearrange("q (h t) -> q h t", t=T), mask, ALU.add)
                    add.then_inc(sc_ready, 1)
                    dve.wait_ge(sc_ready, c + 1)
                    dve.tensor_reduce(mx[:, s], sc[:, s], AX.X, ALU.max).then_inc(mx_ready, 1)
                    dve.wait_ge(mx_ready, c + 1)
                    dve.tensor_tensor(sc[:, s], sc[:, s], per_head(mx, s, T), ALU.subtract).then_inc(sub_ready, 1)
                if has(c, loop, 1):
                    dve.wait_ge(pv_done, c)
                    dve.wait_ge(ri_ready, c)
                    if loop or c > 2:
                        dve.wait_ge(at_done, c - 2)
                    dve.tensor_tensor(at[:, 1 - s].rearrange("q (h e) -> q h e", e=DH),
                                      ps[:, PV, 0:E].rearrange("q (h e) -> q h e", e=DH),
                                      per_head(ri, 1 - s, DH), ALU.mult).then_inc(at_ready, 1)
                if has(c, loop, 2):
                    p = c - 2
                    dve.wait_ge(wo_done, c - 1)
                    dve.tensor_tensor(row(xh_all, p), ps[:, WO, 0:E], row(xh_all, p), ALU.add).then_inc(hh_ready, 1)
                    dve.wait_ge(hh_ready, c - 1)
                    dve.tensor_tensor(row(h_all, p), row(xh_all, p), row(h_all, p), ALU.add).then_inc(r_ready, 1)

            cycles(dve, cycle)
            dve.wait_ge(r_ready, PAIRS)


def router_stage(nc, d, ps, hh, hh_in, const, c_in, wg, wu, wd, w_in, wd_in, slot_hi, slot_lo, w_hi, w_lo,
                 tile_expert, x_slots, ident):
    with Mem(nc, "router") as m:
        wr, g2, before, allones, valid, starts, index = const
        ss, ms, rm, rr = (m.sb(n, [P, NT]) for n in ("hh_ss", "hh_ms", "hh_rms", "hh_rrms"))
        junk = m.sb("hh_squares", [P, 2, E])
        xf = hh
        xp = m.sb("xfT_tile", [P, 2, EC, P])
        (lg, pb, top, best, left, chosen, comb, inc, base, pos, t0, t1, totals) = (
            m.sb(n, [P, NT, EXPERTS]) for n in (
                "logits", "router_probs", "top8", "top2", "others", "chosen", "combine", "until_tile", "before",
                "slot", "tmp0", "tmp1", "tile_totals"))
        red = m.sb("router_red", [P, 4, NT])
        ones_row = m.sb("ones_row", [P, NT])
        cnt, end, first = (m.sb(n, [P, EXPERTS]) for n in ("tiles_of", "tile_end", "first_slot"))
        cmp = m.sb("more_than", [P, EXPERTS, TOKENS // P + 1])
        cmp2 = m.sb("at_or_after", [P, TILES, EXPERTS])
        te = m.sb("tile_expert_f", [P, TILES])
        hi, lo = m.sb("slot_hi_f", [P, NT]), m.sb("slot_lo_f", [P, NT])
        (ss_ready, ms_ready, rm_ready, rr_ready, xf_ready, xt_done, xt_out, l_done, l_ready, chain, e_ready,
         top_ready, left_ready, chosen_ready, rank_done, slots_ready, scattered) = (m.sem(n) for n in (
            "ss_ready", "ms_ready", "rm_ready", "rr_ready", "xf_ready", "xt_done", "xt_out", "l_done",
            "l_ready", "chain", "e_ready", "top_ready", "left_ready", "chosen_ready", "rank_done", "slots_ready",
            "scattered"))
        block = m.stack.enter_context(nc.Block())

        @block.sync
        def _(sp):
            for e in range(EXPERTS):
                for t, src in ((wg, "wg"), (wu, "wu")):
                    sp.dma_start(t[:, e], d[src][e]).then_inc(w_in, 16)
            sp.dma_start(wd[:], d["wd"]).then_inc(wd_in, 16)

        @block.gpsimd
        def _(pool):
            pool.wait_ge(slots_ready, 2)
            for p in range(NT):
                rows = P if p < NT - 1 else LAST_ROWS
                for slot in (slot_hi, slot_lo):
                    pool.indirect_dma_start(x_slots, bass.IndirectOffsetOnAxis(ap=slot[0:rows, p:p + 1], axis=0),
                                            xf[0:rows, p, :], None, bounds_check=TILES * P - 1, oob_is_err=False
                                            ).then_inc(scattered, 16)
            pool.wait_ge(scattered, 16 * 2 * NT)

        @block.tensor
        def _(pe):
            pe.wait_ge(c_in, 16 * len(const))

            def turn(p, s, first):
                pe.wait_ge(xf_ready, p + 1)
                if not first:
                    pe.wait_ge(xt_out, p - 1)
                for c in range(EC):
                    mm = pe.transpose(ps[:, s, c * P:(c + 1) * P], xf[:, p, c * P:(c + 1) * P], ident[:])
                mm.then_inc(xt_done, 1)

            def logits(p, s, first):
                pe.wait_ge(xt_out, p + 1)
                if not first:
                    pe.wait_ge(l_ready, p - 1)
                for c in range(EC):
                    mm = pe.matmul(ps[:, 2 + s, 0:EXPERTS], xp[:, s, c, :], wr[:, c, :], start=(c == 0), stop=(c == EC - 1))
                mm.then_inc(l_done, 1)

            turn(0, 0, True)
            for p in range(NT):
                if p + 1 < NT:
                    turn(p + 1, (p + 1) % 2, p < 1)
                logits(p, p % 2, p < 2)
            pe.wait_ge(chosen_ready, 1)
            moving = chosen[:].rearrange("q p e -> q (p e)")
            pe.matmul(ps[:, 4, 0:NT * EXPERTS], before[:], moving, start=True, stop=True).then_inc(rank_done, 1)
            pe.matmul(ps[:, 5, 0:NT * EXPERTS], allones[:], moving, start=True, stop=True).then_inc(rank_done, 1)

        @block.scalar
        def _(act):
            act.wait_ge(hh_in[0], 16)
            for t in range(NT):
                if t == NT_FIRST:
                    act.wait_ge(hh_in[1], 32)
                if t >= 2:
                    act.wait_ge(ss_ready, t - 1)
                act.activation(junk[:, t % 2], hh[:, t], ACT.Square, accum_out=ss[:, t:t + 1]).then_inc(ss_ready, 1)
            act.wait_ge(ms_ready, 1)
            act.activation(rm[:], ms[:], ACT.Sqrt).then_inc(rm_ready, 1)

            def out(p, s, first):
                act.wait_ge(xt_done, p + 1)
                if not first:
                    act.wait_ge(l_done, p - 1)
                act.activation(xp[:, s].rearrange("q c n -> q (c n)"), ps[:, s, 0:E], ACT.Copy).then_inc(xt_out, 1)

            ring(act, out, NT)
            act.wait_ge(chain, 2)
            act.activation(pb[:], lg[:], ACT.Exp).then_inc(e_ready, 1)

        @block.vector
        def _(dve):
            steps = 0

            def then(ins):
                nonlocal steps
                steps += 1
                ins.then_inc(chain, 1)
                dve.wait_ge(chain, steps)

            dve.wait_ge(ss_ready, NT)
            dve.tensor_scalar(ms[:], ss[:], 1.0 / E, EPS_RMS, ALU.mult, ALU.add).then_inc(ms_ready, 1)
            dve.wait_ge(rm_ready, 1)
            dve.reciprocal(rr[:], rm[:]).then_inc(rr_ready, 1)
            dve.wait_ge(rr_ready, 1)
            dve.wait_ge(c_in, 16 * len(const))
            dve.wait_ge(hh_in[0], 16)
            dve.wait_ge(hh_in[1], 32)

            def scaled(p):
                dve.scalar_tensor_tensor(out=row(xf, p), in0=row(hh, p), scalar=rr[:, ds(p, 1)], in1=g2[:],
                                         op0=ALU.mult, op1=ALU.mult).then_inc(xf_ready, 1)

            def logits(p, s):
                dve.wait_ge(l_done, p + 1)
                dve.tensor_scalar(row(lg, p), ps[:, 2 + s, 0:EXPERTS], 1.0, None, ALU.mult).then_inc(l_ready, 1)

            with dve.Fori(0, NT) as p:
                scaled(p)
            with dve.Fori(0, NT // 2) as i:
                for s in range(2):
                    logits(2 * i + s, s)

            def each(t):
                return t.rearrange("q (p a) -> q p a", a=1).broadcast_to([P, NT, EXPERTS])

            dve.wait_ge(l_ready, NT)
            then(dve.tensor_reduce(red[:, 0], lg[:], AX.X, ALU.max))
            then(dve.tensor_tensor(lg[:], lg[:], each(red[:, 0]), ALU.subtract))
            dve.wait_ge(e_ready, 1)
            then(dve.tensor_reduce(red[:, 1], pb[:], AX.X, ALU.add))
            then(dve.reciprocal(red[:, 2], red[:, 1]))
            then(dve.tensor_tensor(pb[:], pb[:], each(red[:, 2]), ALU.mult))
            then(dve.memset(best[:].rearrange("q p k -> q (p k)"), -1.0))
            for p in range(NT):
                dve.max(top[:, p], pb[:, p]).then_inc(top_ready, 1)
            dve.wait_ge(top_ready, NT)
            then(dve.tensor_copy(best[:, :, 0:2], top[:, :, 0:2]))
            for p in range(NT):
                dve.match_replace(left[:, p], best[:, p], pb[:, p], -1.0).then_inc(left_ready, 1)
            dve.wait_ge(left_ready, NT)
            then(dve.tensor_tensor(chosen[:], left[:], pb[:], ALU.not_equal))
            then(dve.tensor_tensor(chosen[:], chosen[:], each(valid[:]), ALU.mult))
            dve.sem_inc(chosen_ready, 1)
            then(dve.tensor_tensor(red[:, 3], top[:, :, 0], top[:, :, 1], ALU.add))
            then(dve.reciprocal(red[:, 0], red[:, 3]))
            then(dve.tensor_tensor(comb[:], pb[:], chosen[:], ALU.mult))
            then(dve.tensor_tensor(comb[:], comb[:], each(red[:, 0]), ALU.mult))
            then(dve.memset(ones_row[:], 1.0))

            dve.wait_ge(rank_done, 2)
            then(dve.tensor_copy(totals[:], ps[:, 5, 0:NT * EXPERTS].rearrange("q (p e) -> q p e", e=EXPERTS)))
            for e in range(EXPERTS):
                then(dve.tensor_tensor_scan(inc[:, :, e], ones_row[:], totals[:, :, e], 0.0, ALU.mult, ALU.add))
            n_starts = TOKENS // P + 1
            then(dve.tensor_tensor(cmp[:], inc[:, NT - 1, :].rearrange("q (e a) -> q e a", a=1).broadcast_to(
                [P, EXPERTS, n_starts]), starts[:].rearrange("q (a n) -> q a n", a=1).broadcast_to(
                [P, EXPERTS, n_starts]), ALU.is_gt))
            then(dve.tensor_reduce(cnt[:], cmp[:], AX.X, ALU.add))
            then(dve.tensor_tensor_scan(end[:], ones_row[:, 0:EXPERTS], cnt[:], 0.0, ALU.mult, ALU.add))
            then(dve.tensor_tensor(first[:], end[:], cnt[:], ALU.subtract))
            then(dve.tensor_scalar(first[:], first[:], float(P), None, ALU.mult))
            then(dve.tensor_tensor(base[:], inc[:], totals[:], ALU.subtract))
            then(dve.tensor_tensor(base[:], base[:], first[:].rearrange("q (a e) -> q a e", a=1).broadcast_to(
                [P, NT, EXPERTS]), ALU.add))
            then(dve.tensor_tensor(pos[:], ps[:, 4, 0:NT * EXPERTS].rearrange("q (p e) -> q p e", e=EXPERTS), base[:], ALU.add))

            then(dve.scalar_tensor_tensor(out=t0[:], in0=pos[:], scalar=1.0, in1=chosen[:], op0=ALU.add, op1=ALU.mult))
            then(dve.tensor_reduce(hi[:], t0[:], AX.X, ALU.max))
            then(dve.tensor_scalar(hi[:], hi[:], 1.0, None, ALU.subtract))
            then(dve.tensor_scalar(t1[:], pos[:], -1.0, float(TILES * P), ALU.mult, ALU.add))
            then(dve.tensor_tensor(t1[:], t1[:], chosen[:], ALU.mult))
            then(dve.tensor_reduce(lo[:], t1[:], AX.X, ALU.max))
            then(dve.tensor_scalar(lo[:], lo[:], -1.0, float(TILES * P), ALU.mult, ALU.add))
            for f, i32, w in ((hi, slot_hi, w_hi), (lo, slot_lo, w_lo)):
                dve.tensor_copy(i32[:], f[:]).then_inc(slots_ready, 1)
            for f, i32, w in ((hi, slot_hi, w_hi), (lo, slot_lo, w_lo)):
                then(dve.tensor_tensor(t0[:], pos[:], each(f[:]), ALU.is_equal))
                then(dve.tensor_tensor(t0[:], t0[:], comb[:], ALU.mult))
                then(dve.tensor_reduce(w[:], t0[:], AX.X, ALU.add))
            then(dve.tensor_tensor(cmp2[:], index[:].rearrange("q (n a) -> q n a", a=1).broadcast_to(
                [P, TILES, EXPERTS]), end[:].rearrange("q (a e) -> q a e", a=1).broadcast_to(
                [P, TILES, EXPERTS]), ALU.is_ge))
            then(dve.tensor_reduce(te[:], cmp2[:], AX.X, ALU.add))
            then(dve.tensor_scalar(te[:], te[:], float(EXPERTS - 1), None, ALU.min))
            then(dve.tensor_copy(tile_expert[:], te[:]))


def experts_stage(nc, ps, wg, wu, wd, w_in, wd_in, tile_expert, x_slots, y_slots, ident):
    HALF = HID // 2
    FULL = HID // P
    TAIL = HID - FULL * P
    G, U, HT, XT, Y = 0, 2, 4, 6, 7
    with Mem(nc, "experts") as m:
        x = m.sb("x_tile", [P, 2, E])
        xT = m.sb("xT_tile", [P, 2, E])
        g, h = m.sb("gate", [P, 2, HID]), m.sb("hidden", [P, 2, HID])
        hT = m.sb("hiddenT", [P, 2, FULL + 1, P])
        y = m.sb("y_tile", [P, 2, E])
        (xt_done, xt_out, gu_done, g_ready, h_ready, ht_done, ht_out, y_done, y_ready) = (m.sem(n) for n in (
            "xt_done", "xt_out", "gu_done", "g_ready", "h_ready", "ht_done", "ht_out", "y_done", "y_ready"))
        x_in, y_out = ([m.sem(f"{n}{s}") for s in range(2)] for n in ("x_in", "y_out"))
        block = m.stack.enter_context(nc.Block())

        def cycles(eng, cycle):
            for c in range(4):
                cycle(c, c % 2, False)
            with eng.Fori(2, TILES // 2 - 1) as i:
                for s in range(2):
                    cycle(2 * i + s, s, True)
            for c in range(TILES - 2, TILES + 1):
                cycle(c, c % 2, False)

        def tile(ap, t):
            return ap.rearrange("(n q) e -> n q e", q=P)[ds(t, 1)].rearrange("a q e -> (a q) e")

        @block.sync
        def _(sp):
            for s in range(2):
                sp.dma_start(x[:, s], tile(x_slots, s)).then_inc(x_in[s], 16)

            def cycle(c, s, loop):
                if loop or c + 2 < TILES:
                    sp.wait_ge(xt_done, c + 1)
                    sp.dma_start(x[:, s], tile(x_slots, c + 2)).then_inc(x_in[s], 16)
                if loop or c >= 1:
                    sp.wait_ge(y_ready, c)
                    sp.dma_start(tile(y_slots, c - 1), y[:, 1 - s]).then_inc(y_out[1 - s], 16)

            cycles(sp, cycle)
            for s in range(2):
                sp.wait_ge(y_out[s], 16 * (TILES // 2))

        @block.tensor
        def _(pe):
            def turn_x(t, s, n):
                pe.wait_ge(x_in[s], 16 * n)
                for c in range(EC):
                    mm = pe.transpose(ps[:, XT, c * P:(c + 1) * P], x[:, s, c * P:(c + 1) * P], ident[:])
                mm.then_inc(xt_done, 1)

            def expert(t):
                return pe.value_load(tile_expert[0:1, ds(t, 1)], min_val=0, max_val=EXPERTS - 1)

            def cycle(c, s, loop):
                if loop or 1 <= c:
                    pe.wait_ge(h_ready, 2 * c)
                    if loop or c >= 2:
                        pe.wait_ge(ht_out, c - 1)
                    for j in range(FULL + 1):
                        w = P if j < FULL else TAIL
                        mm = pe.transpose(ps[0:w, HT + j // 4, (j % 4) * P:(j % 4 + 1) * P],
                                          h[:, 1 - s, j * P:j * P + w], ident[:])
                    mm.then_inc(ht_done, 1)
                if loop or c < TILES:
                    e = expert(c)
                    pe.wait_ge(xt_out, c + 1)
                    for k in range(2):
                        for bank, w in ((G, wg), (U, wu)):
                            for i in range(EC):
                                mm = pe.matmul(ps[:, bank + k, 0:HALF], xT[:, s, i * P:(i + 1) * P],
                                               w[:, ds(e, 1), i, k * HALF:(k + 1) * HALF].rearrange("q a n -> q (a n)"),
                                               start=(i == 0), stop=(i == EC - 1))
                        mm.then_inc(gu_done, 1)
                if loop or c + 1 < TILES:
                    turn_x(c + 1, 1 - s, (c + 1) // 2 + 1 if not loop else c_half[0] + s + 1)
                if loop or 1 <= c:
                    e = expert(c - 1)
                    pe.wait_ge(ht_out, c)
                    if loop or c >= 2:
                        pe.wait_ge(y_ready, c - 1)
                    for j in range(FULL + 1):
                        w = P if j < FULL else TAIL
                        mm = pe.matmul(ps[:, Y, 0:E], hT[0:w, 1 - s, j, :],
                                       wd[0:w, ds(e, 1), j, :].rearrange("q a n -> q (a n)"),
                                       start=(j == 0), stop=(j == FULL))
                    mm.then_inc(y_done, 1)

            pe.wait_ge(w_in, 16 * 2 * EXPERTS)
            turn_x(0, 0, 1)
            c_half = [None]
            cycle(0, 0, False)
            pe.wait_ge(wd_in, 16)
            cycle(1, 1, False)
            with pe.Fori(1, TILES // 2 - 1) as i:
                c_half[0] = i
                for s in range(2):
                    cycle(2 * i + s, s, True)
            for c in range(TILES - 2, TILES + 1):
                cycle(c, c % 2, False)

        @block.scalar
        def _(act):
            def x_copy(t, s, first):
                act.wait_ge(xt_done, t + 1)
                if not first:
                    act.wait_ge(gu_done, 2 * t - 2)
                act.activation(xT[:, s], ps[:, XT, 0:E], ACT.Copy).then_inc(xt_out, 1)

            def cycle(c, s, loop):
                if loop or 1 <= c:
                    act.wait_ge(ht_done, c)
                    if loop or c >= 3:
                        act.wait_ge(y_done, c - 2)
                    act.activation(hT[:, 1 - s, 0:FULL].rearrange("q j n -> q (j n)"),
                                   ps[:, HT:HT + 2, :].rearrange("q n x -> q (n x)")[:, 0:FULL * P], ACT.Copy)
                    act.activation(hT[0:TAIL, 1 - s, FULL], ps[0:TAIL, HT + FULL // 4, (FULL % 4) * P:(FULL % 4 + 1) * P],
                                   ACT.Copy).then_inc(ht_out, 1)
                if loop or c < TILES:
                    for k in range(2):
                        act.wait_ge(gu_done, 2 * c + k + 1)
                        if loop or c >= 2:
                            act.wait_ge(h_ready, 2 * c + k - 3)
                        act.activation(g[:, s, k * HALF:(k + 1) * HALF], ps[:, G + k, 0:HALF], ACT.Silu
                                       ).then_inc(g_ready, 1)
                if loop or c + 1 < TILES:
                    x_copy(c + 1, 1 - s, not loop and c == 0)

            x_copy(0, 0, True)
            cycles(act, cycle)

        @block.vector
        def _(dve):
            def cycle(c, s, loop):
                if loop or c < TILES:
                    for k in range(2):
                        dve.wait_ge(g_ready, 2 * c + k + 1)
                        if loop or c >= 2:
                            dve.wait_ge(ht_done, c - 1)
                        dve.tensor_tensor(h[:, s, k * HALF:(k + 1) * HALF], ps[:, U + k, 0:HALF],
                                          g[:, s, k * HALF:(k + 1) * HALF], ALU.mult).then_inc(h_ready, 1)
                if loop or 1 <= c:
                    dve.wait_ge(y_done, c)
                    if loop or c >= 3:
                        y_stored(c, s, loop)
                    dve.tensor_copy(y[:, 1 - s], ps[:, Y, 0:E]).then_inc(y_ready, 1)

            def y_stored(c, s, loop):
                if loop:
                    if s == 0:
                        dve.wait_ge(y_out[1], 16 * half[0] - 16)
                    else:
                        dve.wait_ge(y_out[0], 16 * half[0])
                else:
                    dve.wait_ge(y_out[1 - s], 16 * ((c - 1) // 2))

            half = [None]
            for c in range(4):
                cycle(c, c % 2, False)
            with dve.Fori(2, TILES // 2 - 1) as i:
                half[0] = i
                for s in range(2):
                    cycle(2 * i + s, s, True)
            for c in range(TILES - 2, TILES + 1):
                cycle(c, c % 2, False)


def combine_stage(nc, r, r_in, slot_hi, slot_lo, w_hi, w_lo, y_slots, out):
    GROUP = 2
    with Mem(nc, "combine") as m:
        y = m.sb("y_rows", [P, 2, NT, E])
        added = [m.sem("added_hi"), m.sem("added_lo")]
        y_in = [m.sem(f"y_in{t}") for t in range(NT)]
        stored = m.sem("out_stored")
        block = m.stack.enter_context(nc.Block())

        def size(t):
            return P if t < NT - 1 else LAST_ROWS

        @block.gpsimd
        def _(pool):
            for t in range(NT):
                for k, slot in enumerate((slot_hi, slot_lo)):
                    pool.indirect_dma_start(y[0:size(t), k, t], None, y_slots,
                                            bass.IndirectOffsetOnAxis(ap=slot[0:size(t), t:t + 1], axis=0),
                                            bounds_check=TILES * P - 1, oob_is_err=False).then_inc(y_in[t], 16)

        @block.vector
        def _(dve):
            dve.wait_ge(r_in, 48)
            for t in range(NT):
                dve.wait_ge(y_in[t], 32)
                for k, w in enumerate((w_hi, w_lo)):
                    if k:
                        dve.wait_ge(added[0], t + 1)
                    dve.scalar_tensor_tensor(out=r[0:size(t), t], in0=y[0:size(t), k, t], scalar=w[0:size(t), t:t + 1],
                                             in1=r[0:size(t), t], op0=ALU.mult, op1=ALU.add).then_inc(added[k], 1)

        @block.sync
        def _(sp):
            def store(tile0, tile1, rows):
                sp.wait_ge(added[1], tile1)
                part = out[tile0 * P:tile0 * P + (tile1 - tile0 - 1) * P + rows]
                sp.dma_start(part.rearrange("(n q) e -> q n e", q=rows), r[0:rows, tile0:tile1]).then_inc(stored, 16)

            for t in range(0, NT - GROUP, GROUP):
                store(t, t + GROUP, P)
            store(NT - GROUP, NT - 1, P)
            store(NT - 1, NT, LAST_ROWS)
            sp.wait_ge(stored, 16 * ((NT - GROUP) // GROUP + 2))


def build(nc, d, out):
    v_rows = nc.dram_tensor("v_rows", (TOKENS, PARTS * 2 * E), BF16).ap()
    o_rows = nc.dram_tensor("o_rows", (IMAGES, T, E), F32).ap()
    hh_rows, r_rows = (nc.dram_tensor(n, (TOKENS, E), F32).ap() for n in ("hh_rows", "r_rows"))
    x_slots = nc.dram_tensor("x_slots", (TILES * P, E), F32).ap()
    y_slots = nc.dram_tensor("y_slots", (TILES * P, E), F32).ap()
    with nc.psum_tensor("ps", [P, 8, 512], F32) as ps, Mem(nc) as m:
        ident = m.sb("ident", [P, P])
        hh, r = m.sb("hh_tiles", [P, NT, E]), m.sb("r_tiles", [P, NT, E])
        router_const = tuple((m.sb(name, shape), name) for name, shape in (
            ("w_router", [P, EC, EXPERTS]), ("g2_rows", [P, E]), ("rows_before", [P, P]), ("all_ones", [P, P]),
            ("valid_rows", [P, NT]), ("tile_starts", [P, TOKENS // P + 1]), ("tile_index", [P, TILES])))
        with Mem(nc) as rows:
            h_all = rows.sb("h_all", [P, PAIRS, E])
            out_weights, rotary_weights, attention_weights = (
                tuple((rows.sb(f"{name}_t", shape), name) for name, shape in group) for group in (
                    (("W_out", [P, EC, E]), ("g1", [P, EC])),
                    (("wq", [P, EC, E]), ("wk", [P, EC, E]), ("wq_perm", [P, EC, E]), ("wk_perm", [P, EC, E]),
                     ("cos", [P, T]), ("sin", [P, T])),
                    (("wv", [P, EC, E]), ("wo", [P, EC, E]), ("causal", [P, T]), ("head_mask", [P, HG]))))
            out_in, rotary_in, attention_in = (rows.sem(n) for n in ("out_w_in", "rotary_w_in", "attention_w_in"))
            with nc.cleanup_on_exit(), Mem(nc) as cell:
                kn = cell.sb("kn", [P, NH_CELL, CHUNK])
                qn = cell.sb("qn", [P, NH_CELL, CHUNK])
                vrow = cell.sb("v_row", [P, 2, B8, 2, E], BF16)
                states = [cell.sb(f"state{a}", [P, B8 // 2 * E]) for a in range(2)]
                scan_const = tuple((cell.sb(name, shape, dt), name) for name, shape, dt in (
                    ("part_rows_to_block", [P, P], BF16), ("minus_block_ones", [P, P], F32),
                    ("block_sum_to_row", [P, NCELL], F32)))
                row_in = [cell.sem("row_in0"), cell.sem("row_in1")]
                const_in, wts_in = cell.sem("scan_const_in"), cell.sem("projection_weights_in")
                with Mem(nc) as early:
                    zT = early.sb("zT", [P, EC, TOKENS])
                    weights = tuple((early.sb(f"{name}_t", shape), name) for name, shape in (
                        ("W_in", [P, EC, E]), ("W_k", [P, EC, E]), ("W_q", [P, EC, E]), ("W_vb", [P, EC, 2 * E]),
                        ("b_beta", [P, E]), ("block_ones", [P, P])))
                    xpT = early.sb("xp2T", [P, EC, TOKENS])
                    tokens_stage(nc, d, ps, h_all, zT, xpT, ident, weights[0][0], wts_in,
                                 [(t, name, wts_in) for t, name in weights] +
                                 [(t, name, const_in) for t, name in scan_const])
                    projections_stage(nc, ps, xpT, [t for t, _ in weights[1:]], wts_in, kn, qn, v_rows, vrow,
                                      states, row_in)
                scan_stage(nc, d, ps, kn, qn, v_rows, o_rows, vrow, states, [t for t, _ in scan_const], const_in, row_in,
                           [(t, name, arrived) for group, arrived in (
                               (out_weights, out_in), (rotary_weights, rotary_in), (attention_weights, attention_in))
                            for t, name in group])
            xh_all = rows.sb("xh_all", [P, PAIRS, E])
            hh_in = [m.sem("hh_in_first"), m.sem("hh_in_rest")]
            r_in, router_in, w_in, wd_in = (m.sem(n) for n in (
                "r_in", "router_const_in", "gate_up_weights_in", "down_weights_in"))
            xnT, qr, kr = (rows.sb(n, [P, EC, TOKENS]) for n in ("xnT", "q_rot", "k_rot"))
            cell_output_stage(nc, ps, o_rows, h_all, xh_all, xnT, ident, *(t for t, _ in out_weights), out_in, x_slots)
            wq, wk, wq_perm, wk_perm, cos, sin = (t for t, _ in rotary_weights)
            rotary_stage(nc, ps, xnT, qr, kr, (wq, wk, wq_perm, wk_perm), cos, sin, rotary_in)
            attention_stage(nc, d, ps, xnT, qr, kr, *(t for t, _ in attention_weights), attention_in, h_all,
                            xh_all, ident, hh_rows, r_rows, hh, r, hh_in, r_in,
                            [(t, name, router_in) for t, name in router_const])
        slot_hi, slot_lo = (m.sb(n, [P, NT], mybir.dt.int32) for n in ("slot_hi", "slot_lo"))
        w_hi, w_lo = m.sb("w_hi", [P, NT]), m.sb("w_lo", [P, NT])
        with Mem(nc) as experts:
            wg, wu = (experts.sb(n, [P, EXPERTS, EC, HID]) for n in ("expert_wg", "expert_wu"))
            wd = experts.sb("expert_wd", [P, EXPERTS, HID // P + 1, E])
            tile_expert = experts.sb("tile_expert", [P, TILES], mybir.dt.int32)
            router_stage(nc, d, ps, hh, hh_in, [t for t, _ in router_const], router_in, wg, wu, wd, w_in, wd_in,
                         slot_hi, slot_lo, w_hi, w_lo, tile_expert, x_slots, ident)
            experts_stage(nc, ps, wg, wu, wd, w_in, wd_in, tile_expert, x_slots, y_slots, ident)
        combine_stage(nc, r, r_in, slot_hi, slot_lo, w_hi, w_lo, y_slots, out)


def host_layout(np, bf16, inp):
    f = {k: np.ascontiguousarray(v) for k, v in inp.items()}
    a = {}

    def chunked(w):
        k = w.shape[0] // P
        return np.ascontiguousarray(w.reshape(k, P, w.shape[1]).transpose(1, 0, 2))

    x = f["x"].reshape(IMAGES, 3, 6, 16, 6, 16).transpose(0, 1, 3, 5, 2, 4).reshape(IMAGES, DC, P, PATCHES)
    xT = np.zeros((PAIRS, P, DC, 2, SLOT), np.float32)
    xT[..., 2:T] = x.reshape(PAIRS, 2, DC, P, PATCHES).transpose(0, 3, 2, 1, 4)
    a["xT"] = xT.reshape(PAIRS, P, DC, P)
    a["tok_W"] = chunked(f["L0_tok_W"])

    def padded(rows):
        t = np.zeros((2, SLOT, E), np.float32)
        t[:, :T] = rows
        return t.reshape(P, E)

    z = np.zeros((T, E), np.float32)
    pos, bias, gamma, beta = z.copy(), z.copy(), z.copy(), z.copy()
    pos[1:] = f["L0_tok_pos_embedding"][0]
    bias[1], bias[2:] = f["L0_tok_cls_token"][0, 0], f["L0_tok_b"]
    gamma[1:] = f["L0_tok_gamma"]
    beta[0], beta[1:] = f["cls_tok"][0, 0], f["L0_tok_beta"]
    a["t_pos"], a["t_bias"], a["t_gamma"], a["t_beta"] = (padded(t) for t in (pos, bias, gamma, beta))
    a["W_in"], a["W_k"], a["W_q"] = (chunked(f[f"L0_attn_{n}"].T) for n in ("W_in", "W_k", "W_q"))
    a["W_vb"] = chunked(np.concatenate([f["L0_attn_W_v"].T, f["L0_attn_W_beta"].T], 1))
    a["W_out"] = chunked(f["L0_attn_W_out"].T)
    a["b_beta"] = np.ascontiguousarray(np.broadcast_to(f["L0_attn_b_beta"].reshape(1, E), (P, E)))
    perm = np.arange(E).reshape(HEADS, 2, DH // 2)[:, ::-1].reshape(E)
    for n in ("wq", "wk"):
        a[n], a[n + "_perm"] = chunked(f[f"L0_ffn_{n}"]), chunked(f[f"L0_ffn_{n}"][:, perm])
    parity = np.arange(E).reshape(HEADS // 2, 2, DH).transpose(1, 0, 2).reshape(E)
    a["wv"], a["wo"] = chunked(f["L0_ffn_wv"][:, parity]), chunked(f["L0_ffn_wo"])
    a["g1"] = np.ascontiguousarray(f["L0_ffn_g1"].reshape(EC, P).T)
    a["w_router"] = chunked(f["L0_ffn_w_router"])
    a["g2_rows"] = np.ascontiguousarray(np.broadcast_to(f["L0_ffn_g2"].reshape(1, E), (P, E)))
    a["wg"], a["wu"] = (np.stack([chunked(w) for w in f[f"L0_ffn_{n}"]]) for n in ("wg", "wu"))
    wd = np.zeros((EXPERTS, -(-HID // P) * P, E), np.float32)
    wd[:, :HID] = f["L0_ffn_wd"]
    a["wd"] = np.ascontiguousarray(np.stack([chunked(w) for w in wd]).transpose(1, 0, 2, 3))

    p = np.arange(P)
    a["ident"] = np.eye(P, dtype=np.float32)
    block = p // NCELL
    a["block_ones"] = (block[:, None] == block[None]).astype(np.float32)
    a["minus_block_ones"] = -a["block_ones"]
    a["block_sum_to_row"] = (block[:, None] == np.arange(NCELL)[None]).astype(np.float32)
    rows = (p[:, None] < PARTS * B4) & (p[:, None] % B4 == block[None])
    a["part_rows_to_block"] = rows.astype(bf16)
    freq = 1.0 / 10000.0 ** (np.arange(0, DH, 2, dtype=np.float32) / DH)
    ang = np.einsum("i,j->ij", np.arange(T, dtype=np.float32), freq)
    ang = np.concatenate([ang, ang], -1)[:, p % DH].T
    sign = np.where(p % DH < DH // 2, -1.0, 1.0)[:, None]
    a["cos"], a["sin"] = np.cos(ang).astype(np.float32), (np.sin(ang) * sign).astype(np.float32)
    t = p % SLOT
    a["causal"] = np.where(np.arange(T)[None] > t[:, None], -1e30, 0.0).astype(np.float32)
    a["valid_rows"] = (P * np.arange(NT)[None] + p[:, None] < TOKENS).astype(np.float32)
    a["rows_before"] = (p[:, None] < p[None]).astype(np.float32)
    a["all_ones"] = np.ones((P, P), np.float32)
    a["tile_starts"] = np.ascontiguousarray(np.broadcast_to(P * np.arange(TOKENS // P + 1, dtype=np.float32),
                                                            (P, TOKENS // P + 1)))
    a["tile_index"] = np.ascontiguousarray(np.broadcast_to(np.arange(TILES, dtype=np.float32), (P, TILES)))
    a["head_mask"] = (p[:, None] // DH == np.arange(HG)[None]).astype(np.float32)
    return a


def kernel(**inputs):
    import ml_dtypes
    import numpy as np
    import concourse.bacc as bacc
    from concourse.bass_utils import run_bass_kernel_spmd

    nc = bacc.Bacc("TRN2", target_bir_lowering=False, num_devices=1)
    arrays = host_layout(np, ml_dtypes.bfloat16, inputs)
    d = {k: nc.dram_tensor(f"in_{k}", v.shape, mybir.dt.from_np(v.dtype), kind="ExternalInput").ap()
         for k, v in arrays.items()}
    out = nc.dram_tensor("out_0", (TOKENS, E), F32, kind="ExternalOutput").ap()
    build(nc, d, out)
    r = run_bass_kernel_spmd(nc, [{f"in_{k}": v for k, v in arrays.items()}], core_ids=[0])
    return r.results[0]["out_0"].reshape(IMAGES, T, E)
```
